# Optimizing a Trainium2 kernel written in Bass

```python
import numpy as np
import jax
import jax.numpy as jnp

def _softmax(x, axis=-1):
    return jax.nn.softmax(x, axis=axis)

def _gelu(x):
    return jax.nn.gelu(x, approximate=True)

def _silu(x):
    return jax.nn.silu(x)

def _sigmoid(x):
    return jax.nn.sigmoid(x)

def _layernorm(x, axis=-1, eps=1e-05):
    m = jnp.mean(x, axis=axis, keepdims=True)
    v = jnp.var(x, axis=axis, keepdims=True)
    return (x - m) / jnp.sqrt(v + eps)

def _scatter_add(tgt, idx, src, axis=0):
    return tgt.at[idx].add(src)

def _segment_sum(src, seg, n):
    return jax.ops.segment_sum(src, seg, n)
kernel_name = 'mk_cond_seq_d4_seqx_r4_4664d1'

def setup_inputs(seed: int=0):
    np.random.seed(seed)
    _w = jnp.asarray

    def _rec_inputs():
        import jax
        import jax.numpy as jnp
        _rk = jax.random.key(seed)
        x = 0.4999 + 0.2886 * jax.random.normal(jax.random.fold_in(_rk, 1), (16, 256, 256), jnp.float32)
        _lenS = 256 - jax.random.randint(jax.random.fold_in(_rk, 7), (16,), 0, max(1, 256 // 4) + 1, jnp.int32)
        _lenS2 = 256 - jax.random.randint(jax.random.fold_in(_rk, 8), (16,), 0, max(1, 256 // 4) + 1, jnp.int32)
        condB_dt = jax.random.uniform(jax.random.fold_in(_rk, 11), (16,), jnp.float32, 0.0, 0.981965)
        itok_B_0_15 = jax.random.randint(jax.random.fold_in(_rk, 12), (16,), 0, 16, jnp.int32)
        condB_t = jax.random.uniform(jax.random.fold_in(_rk, 13), (16,), jnp.float32, 0.0, 0.983423)
        itok_B_34_63 = jax.random.randint(jax.random.fold_in(_rk, 15), (16,), 34, 64, jnp.int32)
        fside_Bx16xSxS_0 = -1.47943e-05 + 1.00017 * jax.random.normal(jax.random.fold_in(_rk, 16), (16, 16, 256, 256), jnp.float32)
        _validS = jnp.arange(256)[None, :] < _lenS[:, None]
        _validS2 = jnp.arange(256)[None, :] < _lenS2[:, None]
        _causal = jnp.tril(jnp.ones((256, 256), dtype=bool))
        mask_Bx1xSxS_bk0 = jnp.logical_not(jnp.broadcast_to(_validS[:, None, None, :], (16, 1, 256, 256)))
        return (x, condB_dt, itok_B_0_15, condB_t, itok_B_34_63, fside_Bx16xSxS_0, mask_Bx1xSxS_bk0)
    x, condB_dt, itok_B_0_15, condB_t, itok_B_34_63, fside_Bx16xSxS_0, mask_Bx1xSxS_bk0 = _rec_inputs()

    def _L0_cond_setup():
        import jax, jax.numpy as jnp
        import numpy as np
        B, NX, NY = (16, 256, 256)

        def _grad(f, axis):
            fm = jnp.moveaxis(f, axis, -1)
            g = (jnp.roll(fm, -1, -1) - jnp.roll(fm, 1, -1)) * 0.5
            g0 = (-3.0 * fm[..., 0] + 4.0 * fm[..., 1] - fm[..., 2]) * 0.5
            gN = (3.0 * fm[..., -1] - 4.0 * fm[..., -2] + fm[..., -3]) * 0.5
            g = g.at[..., 0].set(g0).at[..., -1].set(gN)
            return jnp.moveaxis(g, -1, axis)

        def _grad2(f, axis):
            fm = jnp.moveaxis(f, axis, -1)
            g = jnp.roll(fm, -1, -1) - 2.0 * fm + jnp.roll(fm, 1, -1)
            g0 = 2.0 * fm[..., 0] - 5.0 * fm[..., 1] + 4.0 * fm[..., 2] - fm[..., 3]
            gN = 2.0 * fm[..., -1] - 5.0 * fm[..., -2] + 4.0 * fm[..., -3] - fm[..., -4]
            g = g.at[..., 0].set(g0).at[..., -1].set(gN)
            return jnp.moveaxis(g, -1, axis)
        key = jax.random.key(seed)
        k1, k2, k3, k4 = jax.random.split(key, 4)
        f = jax.random.uniform(k1, (B, NX, NY), dtype=jnp.float32)
        A_grid = jax.random.normal(k2, (2, NX, NY), dtype=jnp.float32)
        B_grid = jax.random.uniform(k3, (3, NX, NY), dtype=jnp.float32)
        dt = jax.random.uniform(k4, (B,), dtype=jnp.float32)
        return {'f': f, 'A_grid': A_grid, 'B_grid': B_grid, 'dt': dt}
    _L0_cond_all = _L0_cond_setup()
    _L0_cond_in = {k: v for k, v in _L0_cond_all.items() if k in ('A_grid', 'B_grid')}
    del _L0_cond_all

    def _L1_cond_setup():
        import jax, jax.numpy as jnp
        import numpy as np
        B, S, D = (32, 256, 256)
        A = 64
        E = 16
        LN_EPS = 1e-05
        key = jax.random.key(seed)
        ks = jax.random.split(key, 10)
        s = lambda fan_in: 1.0 / np.sqrt(fan_in)
        return {'hidden_states': jax.random.normal(ks[0], (B, S, D), dtype=jnp.float32), 'domain_id': jax.random.randint(ks[1], (B,), 0, E, dtype=jnp.int64), 'down_W': jax.random.uniform(ks[2], (A, D), jnp.float32, -s(D), s(D)), 'down_b': jax.random.uniform(ks[3], (A,), jnp.float32, -s(D), s(D)), 'up_W': jax.random.uniform(ks[4], (D, A), jnp.float32, -s(A), s(A)), 'up_b': jax.random.uniform(ks[5], (D,), jnp.float32, -s(A), s(A)), 'expert_W': jax.random.uniform(ks[6], (E, A, A), jnp.float32, -s(A), s(A)), 'expert_b': jax.random.uniform(ks[7], (E, A), jnp.float32, -s(A), s(A)), 'domain_emb': jax.random.normal(ks[8], (E, A), dtype=jnp.float32), 'ln_gamma': jnp.ones((D,), jnp.float32), 'ln_beta': jnp.zeros((D,), jnp.float32)}
    _L1_cond_all = _L1_cond_setup()
    _L1_cond_in = {k: v for k, v in _L1_cond_all.items() if k in ('down_W', 'down_b', 'up_W', 'up_b', 'expert_W', 'expert_b', 'domain_emb', 'ln_gamma', 'ln_beta')}
    del _L1_cond_all

    def _L2_cond_setup():
        import jax, jax.numpy as jnp
        import numpy as np
        import math
        B, S, D, E = (32, 256, 256, 128)

        def _layer_norm(x, gamma, beta, eps=1e-05):
            mean = jnp.mean(x, axis=(-2, -1), keepdims=True)
            var = jnp.mean(jnp.square(x - mean), axis=(-2, -1), keepdims=True)
            return (x - mean) * jax.lax.rsqrt(var + eps) * gamma + beta

        def _noise_encoding(t, channels):
            half = channels // 2
            freqs = jnp.exp(jnp.arange(half, dtype=jnp.float32) * (-math.log(10000.0) / (half - 1)))
            emb = 5000.0 * t[:, None] * freqs[None, :]
            return jnp.concatenate([jnp.sin(emb), jnp.cos(emb)], axis=1)
        key = jax.random.key(seed)
        ks = jax.random.split(key, 20)

        def lin(k, fan_in, shape):
            return jax.random.normal(k, shape, jnp.float32) / np.sqrt(fan_in)
        inp = {'x': jax.random.normal(ks[0], (B, S, D), jnp.float32), 't': jax.random.uniform(ks[1], (B,), jnp.float32), 'W1': lin(ks[2], E, (E, 4 * E)), 'b1': jnp.zeros((4 * E,), jnp.float32), 'W2': lin(ks[3], 4 * E, (4 * E, 4 * E)), 'b2': jnp.zeros((4 * E,), jnp.float32), 'Wsc': lin(ks[4], 4 * E, (4 * E, D)), 'bsc': jnp.zeros((D,), jnp.float32), 'Wsh': lin(ks[5], 4 * E, (4 * E, D)), 'bsh': jnp.zeros((D,), jnp.float32), 'gamma': jnp.ones((S, D), jnp.float32), 'beta': jnp.zeros((S, D), jnp.float32), 'W_in': lin(ks[6], D, (D, D)), 'b_in': jnp.zeros((D,), jnp.float32), 'W_out': lin(ks[7], D, (D, D)), 'b_out': jnp.zeros((D,), jnp.float32)}
        return inp
    _L2_cond_all = _L2_cond_setup()
    _L2_cond_in = {k: v for k, v in _L2_cond_all.items() if k in ('W1', 'b1', 'W2', 'b2', 'Wsc', 'bsc', 'Wsh', 'bsh', 'gamma', 'beta', 'W_in', 'b_in', 'W_out', 'b_out')}
    del _L2_cond_all

    def _L3_cond_setup():
        import jax, jax.numpy as jnp
        import numpy as np
        import math
        D_MODEL = 256
        N_HEAD = 16
        HEAD_DIM = D_MODEL // N_HEAD
        D_FF = 1024
        NUM_STEPS = 100.0
        RESCALE = 4000.0
        EPS = 1e-05

        def _sin_emb(t):
            half = D_MODEL // 2
            x = t.astype(jnp.float32) / NUM_STEPS * RESCALE
            freqs = jnp.exp(jnp.arange(half, dtype=jnp.float32) * (-math.log(10000.0) / (half - 1)))
            e = x[:, None] * freqs[None, :]
            return jnp.concatenate([jnp.sin(e), jnp.cos(e)], axis=-1)

        def _ln(x):
            m = jnp.mean(x, axis=-1, keepdims=True)
            v = jnp.var(x, axis=-1, keepdims=True)
            return (x - m) / jnp.sqrt(v + EPS)

        def _gelu2(x):
            return x * jax.nn.sigmoid(1.702 * x)
        key = jax.random.key(seed)
        ks = jax.random.split(key, 24)
        B, S, D, F = (4, 128, D_MODEL, D_FF)
        std = 0.02
        inp = {'src': jax.random.normal(ks[0], (B, S, D), dtype=jnp.float32), 'src_mask': jax.random.randint(ks[1], (B, 1, S, S), 0, 2).astype(bool), 'timestep': jax.random.randint(ks[2], (B,), 0, 100, dtype=jnp.int32), 'attention_bias': jax.random.normal(ks[3], (B, N_HEAD, S, S), dtype=jnp.float32), 'W_ada': jax.random.normal(ks[4], (D, 2 * D), dtype=jnp.float32) * std, 'b_ada': jnp.zeros((2 * D,), dtype=jnp.float32), 'Wq': jax.random.normal(ks[5], (D, D), dtype=jnp.float32) * std, 'bq': jnp.zeros((D,), dtype=jnp.float32), 'Wk': jax.random.normal(ks[6], (D, D), dtype=jnp.float32) * std, 'bk': jnp.zeros((D,), dtype=jnp.float32), 'Wv': jax.random.normal(ks[7], (D, D), dtype=jnp.float32) * std, 'bv': jnp.zeros((D,), dtype=jnp.float32), 'Wo': jax.random.normal(ks[8], (D, D), dtype=jnp.float32) * std, 'bo': jnp.zeros((D,), dtype=jnp.float32), 'W1': jax.random.normal(ks[9], (D, F), dtype=jnp.float32) * std, 'b1': jnp.zeros((F,), dtype=jnp.float32), 'W2': jax.random.normal(ks[10], (F, D), dtype=jnp.float32) * std, 'b2': jnp.zeros((D,), dtype=jnp.float32), 'g2': jnp.ones((D,), dtype=jnp.float32), 'beta2': jnp.zeros((D,), dtype=jnp.float32)}
        return inp
    _L3_cond_all = _L3_cond_setup()
    _L3_cond_in = {k: v for k, v in _L3_cond_all.items() if k in ('W_ada', 'b_ada', 'Wq', 'bq', 'Wk', 'bk', 'Wv', 'bv', 'Wo', 'bo', 'W1', 'b1', 'W2', 'b2', 'g2', 'beta2')}
    del _L3_cond_all
    return {'x': x, 'condB_dt': condB_dt, 'itok_B_0_15': itok_B_0_15, 'condB_t': condB_t, 'itok_B_34_63': itok_B_34_63, 'fside_Bx16xSxS_0': fside_Bx16xSxS_0, 'mask_Bx1xSxS_bk0': mask_Bx1xSxS_bk0, 'L0_cond_A_grid': _L0_cond_in['A_grid'], 'L0_cond_B_grid': _L0_cond_in['B_grid'], 'L1_cond_down_W': _L1_cond_in['down_W'], 'L1_cond_down_b': _L1_cond_in['down_b'], 'L1_cond_up_W': _L1_cond_in['up_W'], 'L1_cond_up_b': _L1_cond_in['up_b'], 'L1_cond_expert_W': _L1_cond_in['expert_W'], 'L1_cond_expert_b': _L1_cond_in['expert_b'], 'L1_cond_domain_emb': _L1_cond_in['domain_emb'], 'L1_cond_ln_gamma': _L1_cond_in['ln_gamma'], 'L1_cond_ln_beta': _L1_cond_in['ln_beta'], 'L2_cond_W1': _L2_cond_in['W1'], 'L2_cond_b1': _L2_cond_in['b1'], 'L2_cond_W2': _L2_cond_in['W2'], 'L2_cond_b2': _L2_cond_in['b2'], 'L2_cond_Wsc': _L2_cond_in['Wsc'], 'L2_cond_bsc': _L2_cond_in['bsc'], 'L2_cond_Wsh': _L2_cond_in['Wsh'], 'L2_cond_bsh': _L2_cond_in['bsh'], 'L2_cond_gamma': _L2_cond_in['gamma'], 'L2_cond_beta': _L2_cond_in['beta'], 'L2_cond_W_in': _L2_cond_in['W_in'], 'L2_cond_b_in': _L2_cond_in['b_in'], 'L2_cond_W_out': _L2_cond_in['W_out'], 'L2_cond_b_out': _L2_cond_in['b_out'], 'L3_cond_W_ada': _L3_cond_in['W_ada'], 'L3_cond_b_ada': _L3_cond_in['b_ada'], 'L3_cond_Wq': _L3_cond_in['Wq'], 'L3_cond_bq': _L3_cond_in['bq'], 'L3_cond_Wk': _L3_cond_in['Wk'], 'L3_cond_bk': _L3_cond_in['bk'], 'L3_cond_Wv': _L3_cond_in['Wv'], 'L3_cond_bv': _L3_cond_in['bv'], 'L3_cond_Wo': _L3_cond_in['Wo'], 'L3_cond_bo': _L3_cond_in['bo'], 'L3_cond_W1': _L3_cond_in['W1'], 'L3_cond_b1': _L3_cond_in['b1'], 'L3_cond_W2': _L3_cond_in['W2'], 'L3_cond_b2': _L3_cond_in['b2'], 'L3_cond_g2': _L3_cond_in['g2'], 'L3_cond_beta2': _L3_cond_in['beta2']}

def reference(x, condB_dt, itok_B_0_15, condB_t, itok_B_34_63, fside_Bx16xSxS_0, mask_Bx1xSxS_bk0, L0_cond_A_grid, L0_cond_B_grid, L1_cond_down_W, L1_cond_down_b, L1_cond_up_W, L1_cond_up_b, L1_cond_expert_W, L1_cond_expert_b, L1_cond_domain_emb, L1_cond_ln_gamma, L1_cond_ln_beta, L2_cond_W1, L2_cond_b1, L2_cond_W2, L2_cond_b2, L2_cond_Wsc, L2_cond_bsc, L2_cond_Wsh, L2_cond_bsh, L2_cond_gamma, L2_cond_beta, L2_cond_W_in, L2_cond_b_in, L2_cond_W_out, L2_cond_b_out, L3_cond_W_ada, L3_cond_b_ada, L3_cond_Wq, L3_cond_bq, L3_cond_Wk, L3_cond_bk, L3_cond_Wv, L3_cond_bv, L3_cond_Wo, L3_cond_bo, L3_cond_W1, L3_cond_b1, L3_cond_W2, L3_cond_b2, L3_cond_g2, L3_cond_beta2):
    import jax
    import jax.numpy as jnp

    def _L0_cond_ref(f, A_grid, B_grid, dt):
        import jax, jax.numpy as jnp
        import numpy as np
        B, NX, NY = (16, 256, 256)

        def _grad(f, axis):
            fm = jnp.moveaxis(f, axis, -1)
            g = (jnp.roll(fm, -1, -1) - jnp.roll(fm, 1, -1)) * 0.5
            g0 = (-3.0 * fm[..., 0] + 4.0 * fm[..., 1] - fm[..., 2]) * 0.5
            gN = (3.0 * fm[..., -1] - 4.0 * fm[..., -2] + fm[..., -3]) * 0.5
            g = g.at[..., 0].set(g0).at[..., -1].set(gN)
            return jnp.moveaxis(g, -1, axis)

        def _grad2(f, axis):
            fm = jnp.moveaxis(f, axis, -1)
            g = jnp.roll(fm, -1, -1) - 2.0 * fm + jnp.roll(fm, 1, -1)
            g0 = 2.0 * fm[..., 0] - 5.0 * fm[..., 1] + 4.0 * fm[..., 2] - fm[..., 3]
            gN = 2.0 * fm[..., -1] - 5.0 * fm[..., -2] + 4.0 * fm[..., -3] - fm[..., -4]
            g = g.at[..., 0].set(g0).at[..., -1].set(gN)
            return jnp.moveaxis(g, -1, axis)
        Af = A_grid[None] * f[:, None]
        Bf = B_grid[None] * f[:, None]
        gradv_Af = _grad(Af[:, 0], 1) + _grad(Af[:, 1], 2)
        gradvv_Bf = _grad2(Bf[:, 0], 1) + _grad2(Bf[:, 1], 2) + _grad(_grad(Bf[:, 2], 2), 1) + _grad(_grad(Bf[:, 2], 1), 2)
        df = -gradv_Af + gradvv_Bf * 0.5
        f_new = f + df * dt[:, None, None]
        return jnp.maximum(f_new, 0.0)

    def _L1_cond_ref(hidden_states, domain_id, down_W, down_b, up_W, up_b, expert_W, expert_b, domain_emb, ln_gamma, ln_beta):
        import jax, jax.numpy as jnp
        import numpy as np
        B, S, D = (32, 256, 256)
        A = 64
        E = 16
        LN_EPS = 1e-05
        residual = hidden_states
        hidden = jnp.einsum('bsd,ad->bsa', hidden_states, down_W) + down_b
        hidden = jax.nn.gelu(hidden, approximate=False)
        valid = (domain_id >= 0) & (domain_id < E)
        idx = jnp.clip(domain_id, 0, E - 1)
        Wsel = expert_W[idx]
        bsel = expert_b[idx]
        expert_out = jnp.einsum('bsa,boa->bso', hidden, Wsel) + bsel[:, None, :]
        domain_output = jnp.where(valid[:, None, None], expert_out, hidden)
        hidden = domain_output + domain_emb[idx][:, None, :]
        hidden = jnp.einsum('bsa,da->bsd', hidden, up_W) + up_b
        x = hidden + residual
        mu = jnp.mean(x, axis=-1, keepdims=True)
        var = jnp.mean(jnp.square(x - mu), axis=-1, keepdims=True)
        return (x - mu) * jax.lax.rsqrt(var + LN_EPS) * ln_gamma + ln_beta

    def _L2_cond_ref(x, t, W1, b1, W2, b2, Wsc, bsc, Wsh, bsh, gamma, beta, W_in, b_in, W_out, b_out):
        import jax, jax.numpy as jnp
        import numpy as np
        import math
        B, S, D, E = (32, 256, 256, 128)

        def _layer_norm(x, gamma, beta, eps=1e-05):
            mean = jnp.mean(x, axis=(-2, -1), keepdims=True)
            var = jnp.mean(jnp.square(x - mean), axis=(-2, -1), keepdims=True)
            return (x - mean) * jax.lax.rsqrt(var + eps) * gamma + beta

        def _noise_encoding(t, channels):
            half = channels // 2
            freqs = jnp.exp(jnp.arange(half, dtype=jnp.float32) * (-math.log(10000.0) / (half - 1)))
            emb = 5000.0 * t[:, None] * freqs[None, :]
            return jnp.concatenate([jnp.sin(emb), jnp.cos(emb)], axis=1)
        h = _noise_encoding(t, E)
        h = jax.nn.silu(h @ W1 + b1)
        h = h @ W2 + b2
        scale = (h @ Wsc + bsc)[:, None, :]
        shift = (h @ Wsh + bsh)[:, None, :]
        out = jax.nn.silu(scale * _layer_norm(x, gamma, beta) + shift)
        out = out @ W_in + b_in
        out = jax.nn.silu(scale * _layer_norm(out, gamma, beta) + shift)
        out = out @ W_out + b_out
        return out + x

    def _L3_cond_ref(src, src_mask, timestep, attention_bias, W_ada, b_ada, Wq, bq, Wk, bk, Wv, bv, Wo, bo, W1, b1, W2, b2, g2, beta2):
        import jax, jax.numpy as jnp
        import numpy as np
        import math
        D_MODEL = 256
        N_HEAD = 16
        HEAD_DIM = D_MODEL // N_HEAD
        D_FF = 1024
        NUM_STEPS = 100.0
        RESCALE = 4000.0
        EPS = 1e-05

        def _sin_emb(t):
            half = D_MODEL // 2
            x = t.astype(jnp.float32) / NUM_STEPS * RESCALE
            freqs = jnp.exp(jnp.arange(half, dtype=jnp.float32) * (-math.log(10000.0) / (half - 1)))
            e = x[:, None] * freqs[None, :]
            return jnp.concatenate([jnp.sin(e), jnp.cos(e)], axis=-1)

        def _ln(x):
            m = jnp.mean(x, axis=-1, keepdims=True)
            v = jnp.var(x, axis=-1, keepdims=True)
            return (x - m) / jnp.sqrt(v + EPS)

        def _gelu2(x):
            return x * jax.nn.sigmoid(1.702 * x)
        B, S, D = src.shape
        emb = jax.nn.silu(_sin_emb(timestep)) @ W_ada + b_ada
        scale, shift = jnp.split(emb[:, None, :], 2, axis=-1)
        x = _ln(src) * (1.0 + scale) + shift
        q = (x @ Wq + bq).reshape(B, S, N_HEAD, HEAD_DIM).transpose(0, 2, 1, 3)
        k = (x @ Wk + bk).reshape(B, S, N_HEAD, HEAD_DIM).transpose(0, 2, 1, 3)
        v = (x @ Wv + bv).reshape(B, S, N_HEAD, HEAD_DIM).transpose(0, 2, 1, 3)
        scores = jnp.einsum('bhqd,bhkd->bhqk', q / math.sqrt(HEAD_DIM), k)
        scores = scores + attention_bias
        scores = jnp.where(src_mask, -jnp.inf, scores.astype(jnp.float32))
        probs = jax.nn.softmax(scores, axis=-1).astype(v.dtype)
        ctx = jnp.einsum('bhqk,bhkd->bhqd', probs, v)
        ctx = ctx.transpose(0, 2, 1, 3).reshape(B, S, D)
        x = x + (ctx @ Wo + bo)
        h = _ln(x) * g2 + beta2
        ff = _gelu2(h @ W1 + b1) @ W2 + b2
        return x + ff
    x = _L0_cond_ref(x, L0_cond_A_grid, L0_cond_B_grid, condB_dt)
    x = _L1_cond_ref(x, itok_B_0_15, L1_cond_down_W, L1_cond_down_b, L1_cond_up_W, L1_cond_up_b, L1_cond_expert_W, L1_cond_expert_b, L1_cond_domain_emb, L1_cond_ln_gamma, L1_cond_ln_beta)
    x = _L2_cond_ref(x, condB_t, L2_cond_W1, L2_cond_b1, L2_cond_W2, L2_cond_b2, L2_cond_Wsc, L2_cond_bsc, L2_cond_Wsh, L2_cond_bsh, L2_cond_gamma, L2_cond_beta, L2_cond_W_in, L2_cond_b_in, L2_cond_W_out, L2_cond_b_out)
    x = _L3_cond_ref(x, mask_Bx1xSxS_bk0, itok_B_34_63, fside_Bx16xSxS_0, L3_cond_W_ada, L3_cond_b_ada, L3_cond_Wq, L3_cond_bq, L3_cond_Wk, L3_cond_bk, L3_cond_Wv, L3_cond_bv, L3_cond_Wo, L3_cond_bo, L3_cond_W1, L3_cond_b1, L3_cond_W2, L3_cond_b2, L3_cond_g2, L3_cond_beta2)
    return x

_drawn_inputs = setup_inputs


def setup_inputs(seed=0):
    import zlib

    import numpy as np

    out = dict(_drawn_inputs(seed))
    spreads = {'L1_cond_ln_gamma': (1.0, 0.2),
     'L1_cond_ln_beta': (0.0, 0.1),
     'L2_cond_b1': (0.0, 0.1),
     'L2_cond_b2': (0.0, 0.1),
     'L2_cond_bsc': (0.0, 0.1),
     'L2_cond_bsh': (0.0, 0.1),
     'L2_cond_gamma': (1.0, 0.2),
     'L2_cond_beta': (0.0, 0.291),
     'L2_cond_b_in': (0.0, 0.1),
     'L2_cond_b_out': (0.0, 0.1),
     'L3_cond_b_ada': (0.0, 0.1),
     'L3_cond_bq': (0.0, 2.0),
     'L3_cond_bk': (0.0, 2.0),
     'L3_cond_bv': (0.0, 0.1),
     'L3_cond_bo': (0.0, 0.1),
     'L3_cond_b1': (0.0, 0.1),
     'L3_cond_b2': (0.0, 0.1),
     'L3_cond_g2': (1.0, 0.6),
     'L3_cond_beta2': (0.0, 0.782)}
    factors = {'fside_Bx16xSxS_0': 8.0, 'L1_cond_down_b': 5.484, 'L3_cond_Wq': 8.0, 'L3_cond_Wk': 8.0}
    for name, (base, spread) in spreads.items():
        noise = np.random.default_rng([zlib.crc32(name.encode()), seed]).standard_normal(out[name].shape)
        drawn = base * np.exp(spread * noise) if base else spread * noise
        out[name] = jnp.asarray(drawn.astype(out[name].dtype))
    for name, factor in factors.items():
        out[name] = (out[name] * factor).astype(out[name].dtype)
    return out
```

```python
from contextlib import ExitStack

import numpy as np

import concourse.bass as bass
from concourse import mybir

ALU = mybir.AluOpType
ACT = mybir.ActivationFunctionType
AXX = mybir.AxisListType.X
F32 = mybir.dt.float32
BF16 = mybir.dt.bfloat16
I32 = mybir.dt.int32
U8 = mybir.dt.uint8

P = 128
B, S, D = 16, 256, 256
PAIRS = B // 2
H, DH = 16, 16
A, E = 64, 16
EROW = 32
FF = 1024
FB = FF // P
C4 = 512
NC = 10
EPS = 1e-5
NEG = -1.0e30
BIG = 3.0e38
VW = DH + 1
CH = 2
NCH = 2 * H // CH
RING = 4
LEAD = 1
HEADS = 2 * H
Q_PART = [0, 0, 1, 0, 2, 1]
K_PART = [0, 1, 0, 2, 0, 1]
STACK = len(Q_PART) * DH
MAGIC = 12582912.0
PI2_A = 6.28125
PI2_B = float(np.float32(np.round((2 * np.pi - PI2_A) * 2.0**21) / 2.0**21))
PI2_C = float(2 * np.pi - PI2_A - PI2_B)
(C_SCALE, C_SHIFT, C_ONESC, C_SHIFT3, C_DT, C_EB) = (0, 2, 4, 6, 8, 9)
DVE_LINKS, POOL_LINKS = 39, 5


def wait_alone(eng, sem, value):
    eng.wait_ge(sem, value)
    eng.nop(nofuse=True)


def window(ap, offset, dims):
    first = list(ap.ap[0])
    return bass.AP(ap.tensor, ap.offset + offset, [first] + [list(d) for d in dims])


def adapter_to_attention_kernel(nc, i, out):
    with ExitStack() as keep:
        def sb(name, shape, dt=F32):
            return keep.enter_context(nc.sbuf_tensor(name, shape, dt))

        def sem(name):
            return keep.enter_context(nc.semaphore(name))

        ident = sb("ident", [P, P])
        mean_mat = sb("mean_mat", [P, P])
        half_neg = sb("half_neg", [P, 4])
        gradT = sb("gradT", [P, 2, S])
        lapT = sb("lapT", [P, 2, S])
        gA0, gB0, gB1, gB2, gU, gW = (sb(n, [P, 2, D]) for n in ("gA0", "gB0", "gB1", "gB2h", "gU", "gW"))
        edge1 = sb("edge1", [P, 2, 8])
        edge3 = sb("edge3", [P, 2, 8])
        downT = sb("downT", [P, 2, A])
        down_b = sb("down_b", [A, 1])
        upT = sb("upT", [A, D])
        gammaT = sb("gammaT", [P, 2, S])
        betaT = sb("betaT", [P, 2, S])
        w_in = sb("w_in", [P, 2, D])
        w_out = sb("w_out", [P, 2, D])
        wq, wk, wv, wo = (sb(n, [P, 2, D]) for n in ("wq", "wk", "wv", "wo"))
        w1 = sb("w1", [P, 2, FF])
        w2 = sb("w2", [P, FB, D])
        b_in, bq, bk, g2, beta2 = (sb(n, [P, 2]) for n in ("b_in", "bq", "bk", "g2", "beta2"))
        b1 = sb("b1", [P, FB])
        up_b, ln_g, ln_b, b_out, bv, bo, b2 = (
            sb(n, [P, D]) for n in ("up_b", "ln_g", "ln_b", "b_out", "bv", "bo", "b2"))
        cond = sb("cond", [P, B, NC])
        sel_dram = nc.dram_tensor("sel_dram", [B, A, A], F32, kind="Internal").ap()
        part_dram = nc.dram_tensor("part_dram", [2, 3, D, 2 * S], BF16, kind="Internal").ap()

        w_loaded = sem("w_loaded")
        bq_scaled = sem("bq_scaled")
        ones_set = sem("ones_set")

        WEIGHT_LOADS = [
            (gradT, "gradT"), (lapT, "lapT"), (downT, "downT"), (w_in, "L2_cond_W_in"),
            (w_out, "L2_cond_W_out"), (wq, "L3_cond_Wq"), (wk, "L3_cond_Wk"), (wv, "L3_cond_Wv"),
            (wo, "L3_cond_Wo"), (w1, "L3_cond_W1"), (w2, "L3_cond_W2"), (gammaT, "gammaT"),
            (betaT, "betaT"),
        ]
        COLUMN_LOADS = [(b_in, "L2_cond_b_in"), (bk, "L3_cond_bk"), (g2, "L3_cond_g2"),
                        (beta2, "L3_cond_beta2"), (b1, "L3_cond_b1")]
        ROW_LOADS = [(up_b, "L1_cond_up_b"), (ln_g, "L1_cond_ln_gamma"), (ln_b, "L1_cond_ln_beta"),
                     (b_out, "L2_cond_b_out"), (bv, "L3_cond_bv"), (bo, "L3_cond_bo"),
                     (b2, "L3_cond_b2")]
        N_LOADS = len(WEIGHT_LOADS) + len(COLUMN_LOADS) + len(ROW_LOADS) + 2

        setup(nc, i, locals())

        F = sb("F", [P, 4, D])
        buf = [sb(f"front{n}", [P, 4, D]) for n in range(9)]
        p_a0, p_b0, p_b1, p_b2, p_u, p_w, X1, X3, x1 = buf

        def as_feature(t):
            return t[:, :, :].rearrange("p (c b) s -> p c (b s)", c=2)

        x1T = as_feature(p_a0)
        hidT = p_b0[0:A, 0:2, :].rearrange("p b s -> p (b s)")
        expT = p_b0[0:A, 2:4, :].rearrange("p b s -> p (b s)")
        res1 = p_b1
        xs = p_b2
        x2 = p_u
        x2T = as_feature(p_a0)
        yT = as_feature(p_w)
        zT = as_feature(X1)
        x2b = X3
        x3 = x1
        xn3 = p_b1
        qkf = [as_feature(p_a0), as_feature(p_b0)]
        rest = [as_feature(p_b2), as_feature(p_u)]
        parts = [sb(n, [P, 3, 4 * D], BF16) for n in ("q_parts", "k_parts")]
        ew = sb("ew", [A, 2, A])
        cp = sb("cp", [P, 2, NC])
        qs = sb("q_stack", [P, H * 2 * S], BF16)
        ks = sb("k_stack", [P, H * 2 * S], BF16)
        stacks = [t[0:STACK, :].rearrange("p (h n) -> p h n", h=H) for t in (qs, ks)]
        ffT = qs[:, :].bitcast(F32).rearrange("p (f n) -> p f n", f=FB)
        x4T = sb("x4T", [P, 2, 2 * S])
        V = sb("V", [P, 4, H, VW])
        bias = sb("bias", [P, RING, CH * 2, S])
        mask_raw = sb("mask_raw", [P, 4, S], U8)
        mask_add = sb("mask_add", [P, 4, S])
        Sn = sb("Sn", [P, 2, 2, S])
        nmax = sb("nmax", [P, HEADS, 2])
        Pr = sb("Pr", [P, 2, 2, S])
        PT = sb("PT", [P, 2, 2, S])
        rsum = sb("rsum", [P, 2, H])
        ctxn = sb("ctxn", [P, 4, D])
        ctxT = sb("ctxT", [P, 2, 2 * S])
        x5 = sb("x5", [P, 4, D])
        x5b = sb("x5b", [P, 4, D])
        stats = sb("stats", [P, 4, 6])
        mv = sb("mv", [P, 4, 2])
        ms = sb("ms", [P, 2, 2])
        gs = sb("gs", [P, 2, 2])
        var = sb("var", [P, 4])
        rstd = sb("rstd", [P, 4])
        nmr = sb("nmr", [P, 2])
        edge_f = sb("edge_f", [P, 4, 8])
        edge_p = sb("edge_p", [P, 2, 4, 8])

        G, SP_, TP, CP = (keep.enter_context(nc.psum_tensor(n, [P, 2, 512], F32))
                          for n in ("G", "scores_ps", "PT_ps", "ctx_ps"))
        Gt = G[:, :, :].rearrange("p c (t n) -> p (c t) n", t=2)
        Ct = CP[:, :, :].rearrange("p c (t n) -> p (c t) n", t=2)

        f_loaded, cond_loaded, ew_loaded, mask_loaded = (
            sem(n) for n in ("f_loaded", "cond_loaded", "ew_loaded", "mask_loaded"))
        bias_loaded = [sem(f"bias_loaded{n}") for n in range(RING)]
        prods = sem("prods")
        l0_in, l0_mm, x1_pre, x1_ok, x1_tr, x1T_ok = (
            sem(n) for n in ("l0_in", "l0_mm", "x1_pre", "x1_ok", "x1_tr", "x1T_ok"))
        down_mm, hid_ok, exp_mm, expT_ok, up_mm, res1_ok = (
            sem(n) for n in ("down_mm", "hid_ok", "exp_mm", "expT_ok", "up_mm", "res1_ok"))
        var_ok, rstd_ok = sem("var_ok"), sem("rstd_ok")
        mstat_ok, mstat_mm, mstat_read = sem("mstat_ok"), sem("mstat_mm"), sem("mstat_read")
        x2_ok, x2_tr, norm_ok, xnT_ok, affine_ok, y_ok = (
            sem(n) for n in ("x2_ok", "x2_tr", "norm_ok", "xnT_ok", "affine_ok", "y_ok"))
        win_mm, x2b_ok, wout_mm, xn3_ok, x3_tr, x4T_ok = (
            sem(n) for n in ("win_mm", "x2b_ok", "wout_mm", "xn3_ok", "x3_tr", "x4T_ok"))
        qkv_mm, qk_ok, split_ok, part_written, stack_loaded, V_ok = (
            sem(n) for n in ("qkv_mm", "qk_ok", "split_ok", "part_written", "stack_loaded", "V_ok"))
        mask_ok, masked = sem("mask_ok"), sem("masked")
        score_mm, biased, prob_ok, pt_tr, pt_even, pt_odd, pv_mm, ctx_ok = (
            sem(n) for n in ("score_mm", "biased", "prob_ok", "pt_tr", "pt_even", "pt_odd", "pv_mm", "ctx_ok"))
        ctx_tr, ctxT_ok, wo_mm, hn_ok, hn_tr, hT_ok = (
            sem(n) for n in ("ctx_tr", "ctxT_ok", "wo_mm", "hn_ok", "hn_tr", "hT_ok"))
        x5b_ok, w1_mm, ff_ok, w2_mm, out_ok, stored = (
            sem(n) for n in ("x5b_ok", "w1_mm", "ff_ok", "w2_mm", "out_ok", "stored"))
        dve_done, pool_done = sem("dve_done"), sem("pool_done")

        x_in = i["x"].rearrange("(i b) (c p) y -> i p (b c) y", b=2, p=P)
        x_out = out.rearrange("(i b) (c p) y -> i p (b c) y", b=2, p=P)
        mask_in = i["mask_Bx1xSxS_bk0"].rearrange("(i b) o (c p) k -> i p (b o c) k", b=2, p=P)
        side_in = i["fside_Bx16xSxS_0"].rearrange("(i b) h (c p) k -> i p (b h c) k", b=2, p=P)
        sel_in = sel_dram.rearrange("(i b) a o -> i a b o", b=2)
        cond_in = cond[:, :, :].rearrange("p (i b) n -> p i (b n)", b=2)
        part_out = part_dram.rearrange("w j (c p) n -> w p j c n", p=P)
        part_in = part_dram.rearrange("w j (h d) n -> w j d h n", d=DH)

        def bc(ap, n):
            return window(ap, 0, [[0, n], list(ap.ap[1])])

        block = keep.enter_context(nc.Block())

        @block.sync
        def _(sp):
            with sp.Fori(0, PAIRS) as it:
                sp.wait_ge(x1_pre, LEAD + it)
                sp.dma_start(F[:, :, :], x_in[it]).then_inc(f_loaded, 16)
                sp.wait_ge(x4T_ok, LEAD + it)
                sp.dma_start(cp[:, :, :].rearrange("p b n -> p (b n)"), cond_in[:, it, :]).then_inc(cond_loaded, 16)
                sp.dma_start(ew[:, :, :], sel_in[it]).then_inc(ew_loaded, 16)
                sp.wait_ge(mask_ok, LEAD + it)
                sp.dma_start(mask_raw[:, :, :], mask_in[it]).then_inc(mask_loaded, 16)
                for c in range(NCH):
                    k = c - RING
                    if k >= 0:
                        sp.wait_ge(biased, LEAD + it * (2 * HEADS) + 2 * CH * (k + 1))
                    else:
                        sp.wait_ge(biased, LEAD + it * (2 * HEADS))
                    sp.dma_start(bias[:, c % RING, :, :],
                                 side_in[it, :, 2 * CH * c:2 * CH * (c + 1), :]).then_inc(bias_loaded[c % RING], 16)

        @block.gpsimd
        def _(pool):
            def add_mask(it, c):
                b = c * CH // H
                pool.wait_ge(bias_loaded[c % RING], (it * (NCH // RING) + c // RING + 1) * 16)
                t = bias[:, c % RING, :, :].rearrange("p (h q) k -> p h (q k)", h=CH)
                m = mask_add[:, 2 * b:2 * b + 2, :].rearrange("p q k -> p (q k)")
                nc.gpsimd.tensor_tensor(t, t, bc(m, CH), ALU.add).then_inc(masked, 1)

            nc.gpsimd.memset(V[:, :, :, DH:VW], 1.0).then_inc(ones_set, 1)
            for s in (mask_ok, masked):
                pool.sem_inc(s, LEAD)
            with pool.Fori(0, PAIRS) as it:
                done = [0]

                def link(ins):
                    done[0] += 1
                    ins.then_inc(pool_done, 1)
                    pool.wait_ge(pool_done, it * POOL_LINKS + done[0])

                def inv_std(n, k):
                    wait_alone(pool, var_ok, it * 5 + k + 1)
                    link(nc.gpsimd.tensor_scalar(rstd[:, 0:n], var[:, 0:n], EPS, None, ALU.add))
                    nc.gpsimd.tensor_tensor(rstd[:, 0:n], rstd[:, 0:n], half_neg[:, 0:n],
                                            ALU.pow).then_inc(rstd_ok, 1)

                pool.wait_ge(f_loaded, (it + 1) * 16)
                nc.gpsimd.tensor_tensor(p_a0[:, :, :].rearrange("p (b c) y -> p b (c y)", b=2),
                                        F[:, :, :].rearrange("p (b c) y -> p b (c y)", b=2),
                                        bc(gA0[:, :, :].rearrange("p c y -> p (c y)"), 2), ALU.mult).then_inc(prods, 1)
                nc.gpsimd.tensor_tensor(p_b1[:, :, :].rearrange("p (b c) y -> p b (c y)", b=2),
                                        F[:, :, :].rearrange("p (b c) y -> p b (c y)", b=2),
                                        bc(gB1[:, :, :].rearrange("p c y -> p (c y)"), 2), ALU.mult).then_inc(prods, 1)
                pool.wait_ge(mask_loaded, (it + 1) * 16)
                pool.wait_ge(masked, LEAD + it * NCH)
                pool.nop(nofuse=True)
                nc.gpsimd.tensor_scalar(mask_add[:, :, :], mask_raw[:, :, :], NEG, None, ALU.mult).then_inc(mask_ok, 1)
                pool.wait_ge(mask_ok, LEAD + it + 1)
                pool.wait_ge(x1_ok, it + 1)
                nc.gpsimd.tensor_tensor(res1[:, :, :], x1[:, :, :], bc(up_b[:, :], 4), ALU.add).then_inc(res1_ok, 1)
                inv_std(4, 0)
                inv_std(2, 1)
                pool.wait_ge(x2_ok, it + 1)
                nc.gpsimd.tensor_tensor(x2b[:, :, :], x2[:, :, :], bc(b_out[:, :], 4), ALU.add).then_inc(x2b_ok, 1)
                inv_std(2, 2)
                inv_std(4, 3)
                for c in range(NCH):
                    add_mask(it, c)
                inv_std(4, 4)
                nc.gpsimd.tensor_tensor(x5b[:, :, :], x5[:, :, :], bc(b2[:, :], 4), ALU.add).then_inc(x5b_ok, 1)
                pool.wait_ge(x5b_ok, it + 1)

        @block.vector
        def _(dve):
            for s in (x1_pre, biased, pt_odd, ctx_ok, out_ok):
                dve.sem_inc(s, LEAD)
            with dve.Fori(0, PAIRS) as it:
                done = [0]

                def link(ins, alone=False):
                    done[0] += 1
                    ins.then_inc(dve_done, 1)
                    dve.wait_ge(dve_done, it * DVE_LINKS + done[0])
                    if alone:
                        dve.nop(nofuse=True)

                def by_grid(out_, grid):
                    return nc.vector.tensor_tensor(
                        out_[:, :, :].rearrange("p (b c) y -> p b (c y)", b=2),
                        F[:, :, :].rearrange("p (b c) y -> p b (c y)", b=2),
                        bc(grid[:, :, :].rearrange("p c y -> p (c y)"), 2), ALU.mult)

                def row_stats(src, n):
                    for t in range(4):
                        ins = nc.vector.bn_stats(out=stats[:, t, :], in_=src[:, t, :])
                    link(ins, alone=True)
                    for t in range(4):
                        ins = nc.vector.bn_aggr(out=mv[:, t, :], in_=stats[:, t, :])
                    link(ins)
                    nc.vector.tensor_copy(var[:, 0:4], mv[:, :, 1]).then_inc(var_ok, 1)

                def row_norm(dst, src, k, done_sem=None):
                    dve.wait_ge(rstd_ok, it * 5 + k + 1)
                    for t in range(4):
                        ins = nc.vector.tensor_scalar(dst[:, t, :], src[:, t, :], mv[:, t, 0:1],
                                                      rstd[:, t:t + 1], ALU.subtract, ALU.mult)
                    if done_sem is None:
                        link(ins)
                    else:
                        ins.then_inc(done_sem, 1)

                def whole_stats(pieces, k):
                    for b in range(2):
                        for c in range(2):
                            ins = nc.vector.bn_stats(out=stats[:, 2 * b + c, :], in_=pieces[b][c])
                    link(ins, alone=True)
                    for b in range(2):
                        ins = nc.vector.bn_aggr(out=mv[:, b, :],
                                                in_=stats[:, 2 * b:2 * b + 2, :].rearrange("p c n -> p (c n)"))
                    link(ins)
                    nc.vector.tensor_copy(ms[:, :, 0], mv[:, 0:2, 0])
                    link(nc.vector.tensor_tensor(ms[:, :, 1], mv[:, 0:2, 0], mv[:, 0:2, 0], ALU.mult))
                    nc.vector.tensor_tensor(ms[:, :, 1], ms[:, :, 1], mv[:, 0:2, 1], ALU.add).then_inc(mstat_ok, 1)
                    dve.wait_ge(mstat_mm, it * 2 + k + 1)
                    nc.vector.tensor_copy(gs[:, :, :].rearrange("p b n -> p (b n)"), G[:, 0, 0:4]).then_inc(mstat_read, 1)
                    dve.wait_ge(mstat_read, it * 2 + k + 1)
                    link(nc.vector.tensor_tensor(nmr[:, :], gs[:, :, 0], gs[:, :, 0], ALU.mult))
                    nc.vector.tensor_tensor(var[:, 0:2], gs[:, :, 1], nmr[:, :], ALU.subtract).then_inc(var_ok, 1)
                    dve.wait_ge(rstd_ok, it * 5 + k + 2)
                    link(nc.vector.tensor_tensor(nmr[:, :], gs[:, :, 0], rstd[:, 0:2], ALU.mult))
                    nc.vector.tensor_scalar(nmr[:, :], nmr[:, :], -1.0, None, ALU.mult).then_inc(norm_ok, 1)

                def affine(t, k):
                    dve.wait_ge(xnT_ok, it * 2 + k + 1)
                    v = t.rearrange("p c (b s) -> p c b s", b=2)
                    g = window(gammaT[:, :, :], 0, [[S, 2], [0, 2], [1, S]])
                    be = window(betaT[:, :, :], 0, [[S, 2], [0, 2], [1, S]])
                    link(nc.vector.tensor_tensor(v, v, g, ALU.mult))
                    nc.vector.tensor_tensor(v, v, be, ALU.add).then_inc(affine_ok, 1)

                dve.wait_ge(f_loaded, (it + 1) * 16)
                by_grid(p_b0, gB0)
                link(by_grid(p_b2, gB2))
                by_grid(p_u, gU)
                link(by_grid(p_w, gW))
                inner, left, right = slice(1, D - 1), slice(0, D - 2), slice(2, D)
                link(nc.vector.tensor_tensor(X1[:, :, inner], p_b2[:, :, right], p_b2[:, :, left], ALU.subtract))
                link(nc.vector.tensor_tensor(X3[:, :, inner], p_u[:, :, right], p_w[:, :, left], ALU.add))
                dve.wait_ge(prods, 2 * it + 2)
                nc.vector.tensor_tensor(X1[:, :, inner], X1[:, :, inner], p_a0[:, :, inner], ALU.subtract)
                nc.vector.tensor_tensor(X3[:, :, inner], X3[:, :, inner], p_b1[:, :, inner], ALU.subtract)
                link(nc.vector.tensor_copy(edge_f[:, :, :].rearrange("p t (e j) -> p t e j", e=2),
                                           window(F[:, :, :], 0, [[D, 4], [D - 4, 2], [1, 4]])))
                for n, e in enumerate((edge1, edge3)):
                    ins = nc.vector.tensor_tensor(
                        edge_p[:, n, :, :].rearrange("p (b c) j -> p b (c j)", b=2),
                        edge_f[:, :, :].rearrange("p (b c) j -> p b (c j)", b=2),
                        bc(e[:, :, :].rearrange("p c j -> p (c j)"), 2), ALU.mult)
                link(ins)
                for n, x in enumerate((X1, X3)):
                    ins = nc.vector.tensor_reduce(window(x[:, :, :], 0, [[D, 4], [D - 1, 2]]),
                                                  edge_p[:, n, :, :].rearrange("p t (e j) -> p t e j", e=2),
                                                  AXX, ALU.add)
                ins.then_inc(l0_in, 1)
                dve.wait_ge(l0_in, it + 1)
                dve.wait_ge(l0_mm, it + 1)
                for c in range(2):
                    v = X3[:, :, :].rearrange("p (b c) y -> p c b y", b=2)[:, c]
                    ins = nc.vector.tensor_tensor(v, v, G[:, c, :].rearrange("p (b y) -> p b y", b=2), ALU.add)
                link(ins)
                dve.wait_ge(cond_loaded, (it + 1) * 16)
                for b in range(2):
                    ins = nc.vector.scalar_tensor_tensor(
                        out=x1[:, 2 * b:2 * b + 2, :], in0=X3[:, 2 * b:2 * b + 2, :],
                        scalar=cp[:, b, C_DT:C_DT + 1], in1=F[:, 2 * b:2 * b + 2, :],
                        op0=ALU.mult, op1=ALU.add)
                ins.then_inc(x1_pre, 1)
                dve.wait_ge(up_mm, it + 1)
                dve.wait_ge(res1_ok, it + 1)
                link(nc.vector.tensor_tensor(xs[:, :, :], Gt, res1[:, :, :], ALU.add))
                row_stats(xs, 4)
                row_norm(xs, xs, 0)
                link(nc.vector.tensor_tensor(x2[:, :, :], xs[:, :, :], bc(ln_g[:, :], 4), ALU.mult))
                nc.vector.tensor_tensor(x2[:, :, :], x2[:, :, :], bc(ln_b[:, :], 4), ALU.add).then_inc(x2_ok, 1)
                dve.wait_ge(x2_ok, it + 1)
                whole_stats([[x2[:, 2 * b + c, :] for c in range(2)] for b in range(2)], 0)
                affine(x2T, 0)
                dve.wait_ge(win_mm, it + 1)
                for c in range(2):
                    ins = nc.vector.tensor_scalar(zT[:, c, :], G[:, c, :], b_in[:, c:c + 1], None, ALU.add)
                link(ins)
                whole_stats([[zT[:, c, b * S:(b + 1) * S] for c in range(2)] for b in range(2)], 1)
                affine(zT, 1)
                dve.wait_ge(wout_mm, it + 1)
                dve.wait_ge(x2b_ok, it + 1)
                link(nc.vector.tensor_tensor(x3[:, :, :], Gt, x2b[:, :, :], ALU.add))
                row_stats(x3, 4)
                row_norm(xn3, x3, 3, xn3_ok)
                for w in range(2):
                    dve.wait_ge(qk_ok, 2 * it + w + 1)
                    pt = parts[w][:, :, :].rearrange("p j (c n) -> p j c n", c=2)
                    link(nc.vector.tensor_copy(pt[:, 0], qkf[w]))
                    link(nc.vector.tensor_tensor(rest[w], qkf[w], pt[:, 0], ALU.subtract))
                    link(nc.vector.tensor_copy(pt[:, 1], rest[w]))
                    nc.vector.tensor_tensor(pt[:, 2], rest[w], pt[:, 1], ALU.subtract).then_inc(split_ok, 1)
                dve.wait_ge(qkv_mm, 3 * it + 3)
                dve.wait_ge(ones_set, 1)
                nc.vector.tensor_tensor(V[:, :, :, 0:DH], Gt.rearrange("p t (h d) -> p t h d", h=H),
                                        window(bv[:, :], 0, [[0, 4], [DH, H], [1, DH]]), ALU.add).then_inc(V_ok, 1)

                def bias_and_max(n):
                    c = n // CH
                    dve.wait_ge(masked, LEAD + it * NCH + c + 1)
                    dve.wait_ge(score_mm, it * HEADS + n + 1)
                    dve.wait_ge(prob_ok, LEAD + it * HEADS + max(n - 1, 0))
                    dve.nop(nofuse=True)
                    for q in range(2):
                        nc.vector.tensor_tensor_reduce(
                            out=Sn[:, n % 2, q, :], in0=SP_[:, n % 2, q * S:(q + 1) * S],
                            in1=bias[:, c % RING, 2 * (n % CH) + q, :], scale=-1.0, scalar=BIG,
                            op0=ALU.add, op1=ALU.min, accum_out=nmax[:, n, q:q + 1]).then_inc(biased, 1)

                def finish_ctx(b):
                    dve.wait_ge(pv_mm, LEAD + it * HEADS + H * (b + 1))
                    v = CP[:, :, 0:H * VW].rearrange("p q (h w) -> p q h w", w=VW)
                    link(nc.vector.reciprocal(rsum[:, :, :], v[:, :, :, DH]))
                    for q in range(2):
                        ins = nc.vector.tensor_tensor(
                            ctxn[:, 2 * b + q, :].rearrange("p (h d) -> p h d", h=H), v[:, q, :, 0:DH],
                            window(rsum[:, q, :], 0, [[1, H], [0, DH]]), ALU.mult)
                    ins.then_inc(ctx_ok, 1)

                for n in range(HEADS + 1):
                    if n < HEADS:
                        bias_and_max(n)
                    m = n - 1
                    if m >= 0 and m % 2:
                        dve.wait_ge(pt_tr, LEAD + it * HEADS + m + 1)
                        dve.wait_ge(pv_mm, LEAD + it * HEADS + m - 1)
                        nc.vector.tensor_copy(PT[:, m % 2, :, :].rearrange("p c q -> p (c q)"),
                                              TP[:, m % 2, :]).then_inc(pt_odd, 1)
                    if n == H + 2:
                        finish_ctx(0)
                finish_ctx(1)

                dve.wait_ge(wo_mm, it + 1)
                link(nc.vector.tensor_tensor(x5[:, :, :], Gt, bc(bo[:, :], 4), ALU.add))
                row_stats(x5, 4)
                row_norm(ctxn, x5, 4, hn_ok)
                dve.wait_ge(w2_mm, LEAD + it + 1)
                dve.wait_ge(x5b_ok, it + 1)
                nc.vector.tensor_tensor(x5b[:, :, :], Ct, x5b[:, :, :], ALU.add).then_inc(out_ok, 1)
                assert done[0] == DVE_LINKS, done[0]

        @block.scalar
        def _(act):
            def evac(dst, src, done_sem, scale=1.0, b=0.0):
                ins = nc.scalar.activation(dst, src, ACT.Identity, bias=b, scale=scale)
                if done_sem is not None:
                    ins.then_inc(done_sem, 1)

            act.wait_ge(bq_scaled, 1)
            for s in (x4T_ok, prob_ok, pt_even):
                act.sem_inc(s, LEAD)
            with act.Fori(0, PAIRS) as it:
                act.wait_ge(x1_pre, LEAD + it + 1)
                nc.scalar.activation(x1[:, :, :], x1[:, :, :], ACT.Relu).then_inc(x1_ok, 1)
                act.wait_ge(x1_tr, it + 1)
                evac(x1T, G[:, :, :], x1T_ok)
                act.wait_ge(down_mm, it + 1)
                nc.scalar.activation(hidT, G[0:A, 0, :], ACT.Gelu, bias=down_b[:, 0:1]).then_inc(hid_ok, 1)
                act.wait_ge(exp_mm, it + 1)
                for b in range(2):
                    evac(expT[:, b * S:(b + 1) * S], G[0:A, 1, b * S:(b + 1) * S],
                         expT_ok if b else None, b=cp[0:A, b, C_EB:C_EB + 1])
                for k in range(2):
                    if k == 0:
                        act.wait_ge(x2_tr, it + 1)
                    act.wait_ge(norm_ok, 2 * it + k + 1)
                    dst = (x2T, zT)[k].rearrange("p c (b s) -> p b c s", b=2)
                    src = (G[:, :, :], zT)[k].rearrange("p c (b s) -> p b c s", b=2)
                    for b in range(2):
                        evac(dst[:, b], src[:, b], xnT_ok if b else None, scale=rstd[:, b:b + 1],
                             b=nmr[:, b:b + 1])
                    act.wait_ge(affine_ok, 2 * it + k + 1)
                    src = (x2T, zT)[k]
                    for c in range(2):
                        for b in range(2):
                            ins = nc.scalar.activation(
                                yT[:, c, b * S:(b + 1) * S], src[:, c, b * S:(b + 1) * S], ACT.Silu,
                                bias=cp[:, b, C_SHIFT + c:C_SHIFT + c + 1],
                                scale=cp[:, b, C_SCALE + c:C_SCALE + c + 1])
                    ins.then_inc(y_ok, 1)
                act.wait_ge(x3_tr, it + 1)
                for c in range(2):
                    for b in range(2):
                        evac(x4T[:, c, b * S:(b + 1) * S], G[:, c, b * S:(b + 1) * S],
                             x4T_ok if c and b else None, scale=cp[:, b, C_ONESC + c:C_ONESC + c + 1],
                             b=cp[:, b, C_SHIFT3 + c:C_SHIFT3 + c + 1])
                for w in range(2):
                    act.wait_ge(qkv_mm, 3 * it + w + 1)
                    for c in range(2):
                        evac(qkf[w][:, c, :], G[:, c, :], qk_ok if c else None,
                             scale=(DH ** -0.5, 1.0)[w], b=(bq, bk)[w][:, c:c + 1])
                act.wait_ge(w2_mm, LEAD + it)
                for w in range(2):
                    act.wait_ge(split_ok, 2 * it + w + 1)
                    act.dma_start(part_out[w], parts[w][:, :, :].rearrange("p j (c n) -> p j c n", c=2)
                                  ).then_inc(part_written, 16)
                act.wait_ge(part_written, (2 * it + 2) * 16)
                for w in range(2):
                    for j, part in enumerate((Q_PART, K_PART)[w]):
                        act.dma_start(stacks[w][j * DH:(j + 1) * DH, :, :], part_in[w, part]).then_inc(stack_loaded, 16)
                for n in range(HEADS + 1):
                    if n < HEADS:
                        act.wait_ge(pt_tr, LEAD + it * HEADS + max(n - 1, 0))
                        for q in range(2):
                            act.wait_ge(biased, LEAD + it * 2 * HEADS + 2 * n + q + 1)
                            ins = nc.scalar.activation(Pr[:, n % 2, q, :], Sn[:, n % 2, q, :], ACT.Exp,
                                                       bias=nmax[:, n, q:q + 1], scale=-1.0)
                        ins.then_inc(prob_ok, 1)
                    m = n - 1
                    if m >= 0 and m % 2 == 0:
                        act.wait_ge(pt_tr, LEAD + it * HEADS + m + 1)
                        act.wait_ge(pv_mm, LEAD + it * HEADS + max(m - 1, 0))
                        nc.scalar.activation(PT[:, m % 2, :, :].rearrange("p c q -> p (c q)"),
                                             TP[:, m % 2, :], ACT.Identity).then_inc(pt_even, 1)
                act.wait_ge(ctx_tr, it + 1)
                evac(ctxT[:, :, :], G[:, :, :], ctxT_ok)
                act.wait_ge(hn_tr, it + 1)
                for c in range(2):
                    evac(ctxT[:, c, :], G[:, c, :], hT_ok if c else None, scale=g2[:, c:c + 1],
                         b=beta2[:, c:c + 1])
                for f in range(FB):
                    act.wait_ge(w1_mm, it * FB + f + 1)
                    nc.scalar.activation(ffT[:, f, :], G[:, f % 2, :], ACT.Gelu_apprx_sigmoid,
                                         bias=b1[:, f:f + 1]).then_inc(ff_ok, 1)
                act.wait_ge(out_ok, LEAD + it + 1)
                act.dma_start(x_out[it], x5b[:, :, :]).then_inc(stored, 16)
            act.wait_ge(stored, 16 * PAIRS)

        @block.tensor
        def _(pe):
            def turn(src):
                for t in range(4):
                    for c in range(2):
                        ins = pe.transpose(G[:, c, t * P:(t + 1) * P], src[:, t, c * P:(c + 1) * P], ident[:, :])
                return ins

            def by_feature(w, xT):
                for m in range(2):
                    for c in range(2):
                        ins = pe.matmul(G[:, m, :], w[:, c, m * P:(m + 1) * P], xT[:, c, :],
                                        start=(c == 0), stop=(c == 1))
                return ins

            def by_token(w, xT):
                for t in range(4):
                    for c in range(2):
                        ins = pe.matmul(Gt[:, t, :], xT[:, c, t * P:(t + 1) * P], w[:, c, :],
                                        start=(c == 0), stop=(c == 1))
                return ins

            def average(it, k):
                pe.wait_ge(mstat_ok, 2 * it + k + 1)
                pe.matmul(G[:, 0, 0:4], mean_mat[:, :], ms[:, :, :].rearrange("p b n -> p (b n)"),
                          start=True, stop=True).then_inc(mstat_mm, 1)

            pe.wait_ge(w_loaded, N_LOADS * 16)
            for s in (pv_mm, pt_tr, w2_mm):
                pe.sem_inc(s, LEAD)
            with pe.Fori(0, PAIRS) as it:
                pe.wait_ge(l0_in, it + 1)
                for m in range(2):
                    for n, (mat, x) in enumerate(((gradT, X1), (lapT, p_b0))):
                        v = x[:, :, :].rearrange("p (b c) y -> p c b y", b=2)
                        for c in range(2):
                            ins = pe.matmul(G[:, m, :].rearrange("p (b y) -> p b y", b=2),
                                            mat[:, c, m * P:(m + 1) * P], v[:, c],
                                            start=(n == 0 and c == 0), stop=(n == 1 and c == 1))
                ins.then_inc(l0_mm, 1)
                pe.wait_ge(x1_ok, it + 1)
                turn(x1).then_inc(x1_tr, 1)
                pe.wait_ge(x1T_ok, it + 1)
                for c in range(2):
                    ins = pe.matmul(G[0:A, 0, :], downT[:, c, :], x1T[:, c, :], start=(c == 0), stop=(c == 1))
                ins.then_inc(down_mm, 1)
                pe.wait_ge(hid_ok, it + 1)
                wait_alone(pe, ew_loaded, (it + 1) * 16)
                for b in range(2):
                    ins = pe.matmul(G[0:A, 1, b * S:(b + 1) * S], ew[:, b, :], hidT[:, b * S:(b + 1) * S],
                                    start=True, stop=True)
                ins.then_inc(exp_mm, 1)
                pe.wait_ge(expT_ok, it + 1)
                for t in range(4):
                    ins = pe.matmul(Gt[:, t, :], expT[:, t * P:(t + 1) * P], upT[:, :], start=True, stop=True)
                ins.then_inc(up_mm, 1)
                average(it, 0)
                pe.wait_ge(mstat_read, 2 * it + 1)
                turn(x2).then_inc(x2_tr, 1)
                pe.wait_ge(y_ok, 2 * it + 1)
                by_feature(w_in, yT).then_inc(win_mm, 1)
                average(it, 1)
                pe.wait_ge(mstat_read, 2 * it + 2)
                pe.wait_ge(y_ok, 2 * it + 2)
                by_token(w_out, yT).then_inc(wout_mm, 1)
                pe.wait_ge(xn3_ok, it + 1)
                turn(xn3).then_inc(x3_tr, 1)
                pe.wait_ge(x4T_ok, LEAD + it + 1)
                by_feature(wq, x4T).then_inc(qkv_mm, 1)
                pe.wait_ge(qk_ok, 2 * it + 1)
                by_feature(wk, x4T).then_inc(qkv_mm, 1)
                pe.wait_ge(qk_ok, 2 * it + 2)
                by_token(wv, x4T).then_inc(qkv_mm, 1)
                pe.wait_ge(V_ok, it + 1)
                pe.wait_ge(stack_loaded, (it + 1) * 16 * len(Q_PART + K_PART))
                for n in range(HEADS + 2):
                    if n < HEADS:
                        b, h = divmod(n, H)
                        pe.wait_ge(biased, LEAD + it * 2 * HEADS + max(2 * (n - 1), 0))
                        for q in range(2):
                            ins = pe.matmul(SP_[:, n % 2, q * S:(q + 1) * S],
                                            stacks[0][:, h, b * S + q * P:b * S + (q + 1) * P],
                                            stacks[1][:, h, b * S:(b + 1) * S], start=True, stop=True)
                        ins.then_inc(score_mm, 1)
                    if 0 <= n - 1 < HEADS:
                        m = n - 1
                        pe.wait_ge(prob_ok, LEAD + it * HEADS + m + 1)
                        if m % 2:
                            pe.wait_ge(pt_odd, LEAD + it * H + m // 2)
                        else:
                            pe.wait_ge(pt_even, LEAD + it * H + m // 2)
                        for q in range(2):
                            for c in range(2):
                                ins = pe.transpose(TP[:, m % 2, c * S + q * P:c * S + (q + 1) * P],
                                                   Pr[:, m % 2, q, c * P:(c + 1) * P], ident[:, :])
                        ins.then_inc(pt_tr, 1)
                    if n - 2 >= 0:
                        m = n - 2
                        b, h = divmod(m, H)
                        if h == 0:
                            pe.wait_ge(ctx_ok, LEAD + 2 * it + b)
                            if b == 0:
                                pe.wait_ge(out_ok, LEAD + it)
                        if m % 2:
                            pe.wait_ge(pt_odd, LEAD + it * H + m // 2 + 1)
                        else:
                            pe.wait_ge(pt_even, LEAD + it * H + m // 2 + 1)
                        for q in range(2):
                            for c in range(2):
                                ins = pe.matmul(CP[:, q, h * VW:(h + 1) * VW],
                                                PT[:, m % 2, c, q * P:(q + 1) * P], V[:, 2 * b + c, h, :],
                                                start=(c == 0), stop=(c == 1))
                        ins.then_inc(pv_mm, 1)
                pe.wait_ge(ctx_ok, LEAD + 2 * it + 2)
                turn(ctxn).then_inc(ctx_tr, 1)
                pe.wait_ge(ctxT_ok, it + 1)
                for t in range(4):
                    for c in range(2):
                        pe.matmul(Gt[:, t, :], ctxT[:, c, t * P:(t + 1) * P], wo[:, c, :],
                                  start=(c == 0), stop=False)
                    for c in range(2):
                        ins = pe.matmul(Gt[:, t, c * P:(c + 1) * P], x4T[:, c, t * P:(t + 1) * P], ident[:, :],
                                        start=False, stop=(c == 1))
                ins.then_inc(wo_mm, 1)
                pe.wait_ge(hn_ok, it + 1)
                turn(ctxn).then_inc(hn_tr, 1)
                pe.wait_ge(hT_ok, it + 1)
                for f in range(FB):
                    if f >= 2:
                        pe.wait_ge(ff_ok, it * FB + f - 1)
                    for c in range(2):
                        ins = pe.matmul(G[:, f % 2, :], w1[:, c, f * P:(f + 1) * P], ctxT[:, c, :],
                                        start=(c == 0), stop=(c == 1))
                    ins.then_inc(w1_mm, 1)
                pe.wait_ge(ff_ok, (it + 1) * FB)
                for t in range(4):
                    for f in range(FB):
                        ins = pe.matmul(Ct[:, t, :], ffT[:, f, t * P:(t + 1) * P], w2[:, f, :],
                                        start=(f == 0), stop=(f == FB - 1))
                ins.then_inc(w2_mm, 1)


def setup(nc, i, k):
    with ExitStack() as ctx:
        def sb(name, shape, dt=F32):
            return ctx.enter_context(nc.sbuf_tensor(name, shape, dt))

        def sem(name):
            return ctx.enter_context(nc.semaphore(name))

        ident, mean_mat, half_neg, cond, sel_dram = (k[n] for n in ("ident", "mean_mat", "half_neg", "cond", "sel_dram"))
        w_loaded = k["w_loaded"]

        cW1 = sb("cW1", [P, C4])
        cW2 = sb("cW2", [P, 4, C4])
        cWsc, cWsh = sb("cWsc", [P, 4, D]), sb("cWsh", [P, 4, D])
        cWada = sb("cWada", [P, 2, 2 * D])
        cb1, cb2 = sb("cb1", [P, 4]), sb("cb2", [P, 4])
        cb = sb("cb", [P, 8])
        gA1 = sb("gA1", [P, 2, D])
        fc = sb("fc", [P, 4])
        rown = sb("rown", [EROW + 1, 1])
        ecoef = sb("ecoef", [P, 4, 8])
        tb = sb("tb", [P, B])
        t3i = sb("t3i", [P, B], I32)
        t3 = sb("t3", [P, B])
        dt_row = sb("dt_row", [P, B])
        idi = sb("idi", [EROW + 1, B], I32)
        idf, idc, one_c, one_v, ok = (sb(n, [EROW + 1, B]) for n in ("idf", "idc", "one_c", "one_v", "ok"))
        etab = sb("etab", [EROW + 1, A * A])
        ebt = sb("ebt", [EROW + 1, A])
        demb = sb("demb", [E, A])
        sel = sb("sel", [B, A * A])
        ang, turns, red, sn = (sb(n, [P, 3, B]) for n in ("ang", "turns", "red", "sn"))
        se = sb("se", [P, 2, B])
        h1, h2 = sb("h1", [P, 4, B]), sb("h2", [P, 4, B])
        edg = sb("edg", [P, 4, 2, 8])
        edt = sb("edt", [P, 2, 2, 8])
        ps = [ctx.enter_context(nc.psum_tensor(f"setup_ps{n}", [P, 512], F32)) for n in range(8)]

        tab_zero, c_loaded, small, id_ok, enc_ok, sin_ok, se_ok = (
            sem(n) for n in ("tab_zero", "c_loaded", "small", "id_ok", "enc_ok", "sin_ok", "se_ok"))
        h1_mm, h1_ok, h2_mm, h2_ok, cond_mm, sel_mm, sel_ok, sel_stored, chain, idn, acts = (
            sem(n) for n in ("h1_mm", "h1_ok", "h2_mm", "h2_ok", "cond_mm", "sel_mm", "sel_ok", "sel_stored", "chain", "idn", "acts"))
        cond_zero = sem("cond_zero")

        block = ctx.enter_context(nc.Block())

        def cols(name):
            return i[name]

        def mat(name):
            return i[name].rearrange("(c p) n -> p c n", p=P)

        C_LOADS = [
            (fc[:, :], i["enc_cols"]), (rown[:, :], i["row_number"]),
            (tb[:, :], i["condB_t"].partition_broadcast(P)),
            (t3i[:, :], i["itok_B_34_63"].partition_broadcast(P)),
            (idi[:, :], i["itok_B_0_15"].partition_broadcast(EROW + 1)),
            (cW1[:, :], i["L2_cond_W1"]), (cW2[:, :, :], mat("L2_cond_W2")),
            (cWsc[:, :, :], mat("L2_cond_Wsc")), (cWsh[:, :, :], mat("L2_cond_Wsh")),
            (cWada[:, :, :], mat("L3_cond_W_ada")),
            (cb1[:, :], cols("L2_cond_b1")), (cb2[:, :], cols("L2_cond_b2")),
            (cb[:, 0:2], cols("L2_cond_bsc")), (cb[:, 2:4], cols("L2_cond_bsh")),
            (cb[:, 4:8], cols("L3_cond_b_ada")), (demb[:, :], i["L1_cond_domain_emb"]),
            (ecoef[:, :, :].rearrange("p a b -> p (a b)"), i["edge_coef"].partition_broadcast(P)),
            (dt_row[:, :], i["condB_dt"].partition_broadcast(P)),
            (gA1[:, :, :], i["L0_cond_A_grid"][1].rearrange("(c p) y -> p c y", p=P)),
        ] + [(k[n][:, :, :], i[g][j].rearrange("(c p) y -> p c y", p=P)) for n, g, j in (
            ("gA0", "L0_cond_A_grid", 0), ("gB0", "L0_cond_B_grid", 0), ("gB1", "L0_cond_B_grid", 1),
            ("gB2", "L0_cond_B_grid", 2))]
        N_C = len(C_LOADS) + 3

        @block.sync
        def _(sp):
            for dst, src in C_LOADS:
                sp.dma_start(dst, src).then_inc(c_loaded, 16)
            sp.wait_ge(tab_zero, 3)
            sp.dma_start(etab[0:E, :], i["expertT"]).then_inc(c_loaded, 16)
            sp.dma_start(etab[EROW:EROW + 1, :], i["eye64"]).then_inc(c_loaded, 16)
            sp.dma_start(ebt[0:E, :], i["L1_cond_expert_b"]).then_inc(c_loaded, 16)
            sp.wait_ge(sel_ok, 8)
            sp.dma_start(sel_dram.rearrange("b a o -> b (a o)"), sel[:, :]).then_inc(sel_stored, 16)
            sp.wait_ge(sel_stored, 16)

        @block.gpsimd
        def _(pool):
            nc.gpsimd.memset(etab[:, :], 0.0).then_inc(tab_zero, 1)
            nc.gpsimd.memset(ebt[:, :], 0.0).then_inc(tab_zero, 1)
            nc.gpsimd.memset(cond[:, :, :], 0.0).then_inc(cond_zero, 1)
            nc.gpsimd.memset(half_neg[:, :], -0.5).then_inc(tab_zero, 1)
            nc.gpsimd.memset(mean_mat[:, :], 1.0 / P)
            nc.gpsimd.memset(ident[:, :], 0.0).then_inc(idn, 1)
            pool.wait_ge(idn, 1)
            nc.gpsimd.affine_select(out=ident[:, :], in_=ident[:, :], compare_op=ALU.not_equal, fill=1.0,
                                    base=0, pattern=[[-1, P]], channel_multiplier=1).then_inc(idn, 1)

        @block.scalar
        def _(act):
            for dst, name in k["WEIGHT_LOADS"]:
                act.dma_start(dst[:, :, :], mat(name)).then_inc(w_loaded, 16)
            for dst, name in k["COLUMN_LOADS"] + [(k["bq"], "L3_cond_bq")]:
                act.dma_start(dst[:, :], cols(name)).then_inc(w_loaded, 16)
            act.dma_start(k["upT"][:, :], i["upT"]).then_inc(w_loaded, 16)
            for dst, name in k["ROW_LOADS"]:
                act.dma_start(dst[:, :], i[name].partition_broadcast(P)).then_inc(w_loaded, 16)
            act.dma_start(k["down_b"][:, :], i["L1_cond_down_b"].rearrange("(a o) -> a o", o=1)).then_inc(w_loaded, 16)
            act.wait_ge(enc_ok, 1)
            nc.scalar.activation(sn[:, :, :], red[:, :, :], ACT.Sin).then_inc(sin_ok, 1)
            act.wait_ge(sin_ok, 1)
            nc.scalar.activation(se[:, :, :], sn[:, 1:3, :], ACT.Silu).then_inc(se_ok, 1)
            act.wait_ge(h1_mm, 1)
            for m in range(4):
                nc.scalar.activation(h1[:, m, :], ps[0][:, m * B:(m + 1) * B], ACT.Silu,
                                     bias=cb1[:, m:m + 1]).then_inc(h1_ok, 1)
            act.wait_ge(w_loaded, (k["N_LOADS"] + 1) * 16)
            nc.scalar.mul(k["bq"][:, :], k["bq"][:, :], DH ** -0.5).then_inc(k["bq_scaled"], 1)
            act.wait_ge(k["bq_scaled"], 1)

        @block.vector
        def _(dve):
            n = [0]

            def link(ins):
                n[0] += 1
                ins.then_inc(chain, 1)
                dve.wait_ge(chain, n[0])

            dve.wait_ge(c_loaded, N_C * 16)
            link(nc.vector.tensor_copy(idf[:, :], idi[:, :]))
            link(nc.vector.tensor_scalar(idc[:, :], idf[:, :], 0.0, float(E - 1), ALU.max, ALU.min))
            nc.vector.tensor_scalar(one_c[:, :], idc[:, :], rown[:, 0:1], None, ALU.is_equal)
            link(nc.vector.tensor_tensor(ok[:, :], idf[:, :], idc[:, :], ALU.is_equal))
            link(nc.vector.tensor_scalar(one_v[:, :], idf[:, :], rown[:, 0:1], None, ALU.is_equal))
            nc.vector.tensor_scalar(one_v[EROW:EROW + 1, :], ok[EROW:EROW + 1, :], -1.0, 1.0, ALU.mult,
                                    ALU.add).then_inc(id_ok, 1)
            link(nc.vector.tensor_copy(t3[:, :], t3i[:, :]))
            nc.vector.tensor_scalar(ang[:, 0, :], tb[:, :], 5000.0, fc[:, 0:1], ALU.mult, ALU.mult)
            link(nc.vector.tensor_scalar(t3[:, :], t3[:, :], 0.01, 4000.0, ALU.mult, ALU.mult))
            for j in (1, 2):
                ins = nc.vector.tensor_scalar(ang[:, j, :], t3[:, :], fc[:, 1:2], None, ALU.mult)
            link(ins)
            inv = float(1 / (2 * np.pi))
            nc.vector.tensor_scalar(turns[:, 0, :], ang[:, 0, :], inv, fc[:, 2:3], ALU.mult, ALU.add)
            nc.vector.tensor_scalar(turns[:, 1, :], ang[:, 1, :], inv, None, ALU.mult)
            link(nc.vector.tensor_scalar(turns[:, 2, :], ang[:, 2, :], inv, 0.25, ALU.mult, ALU.add))
            link(nc.vector.tensor_scalar(turns[:, :, :], turns[:, :, :], MAGIC, None, ALU.add))
            link(nc.vector.tensor_scalar(turns[:, :, :], turns[:, :, :], MAGIC, None, ALU.subtract))
            src = ang
            for part in (PI2_A, PI2_B, PI2_C):
                link(nc.vector.scalar_tensor_tensor(out=red[:, :, :], in0=turns[:, :, :], scalar=-part,
                                                    in1=src[:, :, :], op0=ALU.mult, op1=ALU.add))
                src = red
            nc.vector.tensor_scalar(red[:, 0, :], red[:, 0, :], fc[:, 3:4], None, ALU.add)
            link(nc.vector.tensor_scalar(red[:, 2, :], red[:, 2, :], float(np.pi / 2), None, ALU.add))
            nc.vector.tensor_scalar(red[:, :, :], red[:, :, :], 3.1415925, -3.1415925, ALU.min,
                                    ALU.max).then_inc(enc_ok, 1)
            g = {x: k[x][:, :, :] for x in ("gA0", "gB0", "gB1", "gB2", "gU", "gW")}
            link(nc.vector.tensor_scalar(g["gB2"], g["gB2"], 0.5, None, ALU.mult))
            nc.vector.tensor_tensor(g["gU"], g["gB1"], gA1[:, :, :], ALU.subtract)
            link(nc.vector.tensor_tensor(g["gW"], g["gB1"], gA1[:, :, :], ALU.add))
            nc.vector.tensor_scalar(g["gU"], g["gU"], 0.5, None, ALU.mult)
            nc.vector.tensor_scalar(g["gW"], g["gW"], 0.5, None, ALU.mult)
            for m, grid in enumerate((g["gB2"], g["gA0"], gA1[:, :, :], g["gB1"])):
                ins = nc.vector.tensor_copy(edg[:, m, :, :].rearrange("p c (e j) -> p c e j", e=2),
                                            window(grid, 0, [[D, 2], [D - 4, 2], [1, 4]]))
            link(ins)
            for m in range(4):
                ins = nc.vector.tensor_tensor(edg[:, m], edg[:, m],
                                              window(ecoef[:, m, :], 0, [[0, 2], [1, 8]]), ALU.mult)
            link(ins)
            nc.vector.tensor_tensor(k["edge1"][:, :, :], edg[:, 0], edg[:, 1], ALU.add)
            nc.vector.tensor_tensor(k["edge3"][:, :, :], edg[:, 2], edg[:, 3], ALU.add)
            dve.wait_ge(cond_zero, 1)
            dve.wait_ge(h2_mm, 1)
            for m in range(4):
                nc.vector.tensor_scalar(h2[:, m, :], ps[1][:, m * B:(m + 1) * B], cb2[:, m:m + 1], None,
                                        ALU.add).then_inc(h2_ok, 1)
            dve.wait_ge(cond_mm, 1)
            for m in range(8):
                one = 1.0 if C_ONESC <= m < C_SHIFT3 else 0.0
                nc.vector.tensor_scalar(cond[:, :, m], ps[2][:, m * B:(m + 1) * B], cb[:, m:m + 1], one,
                                        ALU.add, ALU.add)
            nc.vector.tensor_copy(cond[:, :, C_DT], dt_row[:, :])
            nc.vector.tensor_copy(cond[0:A, :, C_EB], ps[3][0:A, 0:B])
            for c in range(8):
                dve.wait_ge(sel_mm, c + 1)
                nc.vector.tensor_copy(sel[:, c * 512:(c + 1) * 512], ps[4 + c % 4][0:B, :]).then_inc(sel_ok, 1)

        @block.tensor
        def _(pe):
            pe.wait_ge(c_loaded, N_C * 16)
            pe.wait_ge(sin_ok, 1)
            for m in range(4):
                ins = pe.matmul(ps[0][:, m * B:(m + 1) * B], cW1[:, m * P:(m + 1) * P], sn[:, 0, :],
                                start=True, stop=True)
            ins.then_inc(h1_mm, 1)
            pe.wait_ge(h1_ok, 4)
            for m in range(4):
                for c in range(4):
                    ins = pe.matmul(ps[1][:, m * B:(m + 1) * B], cW2[:, c, m * P:(m + 1) * P], h1[:, c, :],
                                    start=(c == 0), stop=(c == 3))
            ins.then_inc(h2_mm, 1)
            pe.wait_ge(h2_ok, 4)
            pe.wait_ge(se_ok, 1)
            for m in range(8):
                w, x, kk, col = ((cWsc, h2, 4, m), (cWsh, h2, 4, m - 2), (cWada, se, 2, m - 4))[
                    0 if m < 2 else 1 if m < 4 else 2]
                for c in range(kk):
                    ins = pe.matmul(ps[2][:, m * B:(m + 1) * B], w[:, c, col * P:(col + 1) * P], x[:, c, :],
                                    start=(c == 0), stop=(c == kk - 1))
            pe.wait_ge(id_ok, 1)
            pe.matmul(ps[3][0:A, 0:B], ebt[:, :], one_v[:, :], start=True, stop=False)
            pe.matmul(ps[3][0:A, 0:B], demb[:, :], one_c[0:E, :], start=False, stop=True).then_inc(cond_mm, 1)
            for c in range(8):
                if c >= 4:
                    pe.wait_ge(sel_ok, c - 3)
                pe.matmul(ps[4 + c % 4][0:B, :], one_v[:, :], etab[:, c * 512:(c + 1) * 512],
                          start=True, stop=True).then_inc(sel_mm, 1)


_DIRECT = ['x', 'condB_dt', 'itok_B_0_15', 'condB_t', 'itok_B_34_63', 'fside_Bx16xSxS_0', 'mask_Bx1xSxS_bk0',
           'L0_cond_A_grid', 'L0_cond_B_grid', 'L1_cond_down_b', 'L1_cond_up_b', 'L1_cond_expert_b',
           'L1_cond_domain_emb', 'L1_cond_ln_gamma', 'L1_cond_ln_beta', 'L2_cond_W1', 'L2_cond_b1',
           'L2_cond_W2', 'L2_cond_b2', 'L2_cond_Wsc', 'L2_cond_bsc', 'L2_cond_Wsh', 'L2_cond_bsh',
           'L2_cond_W_in', 'L2_cond_b_in', 'L2_cond_W_out', 'L2_cond_b_out', 'L3_cond_W_ada', 'L3_cond_b_ada',
           'L3_cond_Wq', 'L3_cond_bq', 'L3_cond_Wk', 'L3_cond_bk', 'L3_cond_Wv', 'L3_cond_bv', 'L3_cond_Wo',
           'L3_cond_bo', 'L3_cond_W1', 'L3_cond_b1', 'L3_cond_W2', 'L3_cond_b2', 'L3_cond_g2', 'L3_cond_beta2']


_COLUMNS = ['L2_cond_b1', 'L2_cond_b2', 'L2_cond_bsc', 'L2_cond_bsh', 'L3_cond_b_ada', 'L2_cond_b_in', 'L3_cond_bq',
            'L3_cond_bk', 'L3_cond_g2', 'L3_cond_beta2', 'L3_cond_b1']


def _shape_constants():
    grad, lap = np.zeros((S, S), np.float32), np.zeros((S, S), np.float32)
    for r in range(1, S - 1):
        grad[r, r - 1], grad[r, r + 1] = -0.5, 0.5
        lap[r, r - 1:r + 2] = 0.5, -1.0, 0.5
    grad[0, 0:3], grad[S - 1, S - 3:] = (-1.5, 2.0, -0.5), (0.5, -2.0, 1.5)
    lap[0, 0:4], lap[S - 1, S - 4:] = (1.0, -2.5, 2.0, -0.5), (-0.5, 2.0, -2.5, 1.0)
    cols = np.zeros((P, 4), np.float32)

    def freqs(half):
        step = np.float32(-np.log(10000.0) / (half - 1))
        return np.exp(np.arange(half, dtype=np.float32) * step).astype(np.float32)

    cols[:, 0] = np.tile(freqs(P // 2), 2)
    cols[:, 1] = freqs(P)
    cols[P // 2:, 2] = 0.25
    cols[P // 2:, 3] = np.pi / 2
    edge = np.array([[-3, 4, -1, 0, 0, 1, -4, 3], [-1, 0, 0, 0, 0, 0, 0, -1],
                     [1.5, -2, 0.5, 0, 0, -0.5, 2, -1.5], [1, -2.5, 2, -0.5, -0.5, 2, -2.5, 1]], np.float32)
    return {"gradT": np.ascontiguousarray(grad.T), "lapT": np.ascontiguousarray(lap.T), "enc_cols": cols,
            "row_number": np.arange(EROW + 1, dtype=np.float32).reshape(-1, 1), "edge_coef": edge.reshape(-1),
            "eye64": np.eye(A, dtype=np.float32).reshape(1, -1)}


def kernel(**inputs):
    import numpy as _np
    import concourse.bacc as _bacc
    from concourse import mybir as _mybir
    from concourse.bass_utils import run_bass_kernel_spmd as _run

    nc = _bacc.Bacc("TRN2", target_bir_lowering=False, num_devices=1)
    data = {n: _np.ascontiguousarray(inputs[n]) for n in _DIRECT}
    data["downT"] = _np.ascontiguousarray(_np.asarray(inputs["L1_cond_down_W"]).T)
    data["upT"] = _np.ascontiguousarray(_np.asarray(inputs["L1_cond_up_W"]).T)
    data["expertT"] = _np.ascontiguousarray(
        _np.asarray(inputs["L1_cond_expert_W"]).transpose(0, 2, 1)).reshape(E, A * A)
    data["gammaT"] = _np.ascontiguousarray(_np.asarray(inputs["L2_cond_gamma"]).T)
    data["betaT"] = _np.ascontiguousarray(_np.asarray(inputs["L2_cond_beta"]).T)
    for n in _COLUMNS:
        data[n] = _np.ascontiguousarray(data[n].reshape(-1, P).T)
    data.update(_shape_constants())
    arrays, aps = {}, {}
    for name, a in data.items():
        arrays[f"in_{name}_dram"] = a
        aps[name] = nc.dram_tensor(f"in_{name}_dram", a.shape, _mybir.dt.from_np(a.dtype), kind="ExternalInput").ap()
    out = nc.dram_tensor("out_0_dram", (B, S, D), _mybir.dt.float32, kind="ExternalOutput").ap()
    adapter_to_attention_kernel(nc, aps, out)
    r = _run(nc, [arrays], core_ids=[0])
    return r.results[0]["out_0_dram"]
```

```python
from contextlib import ExitStack

import numpy as np

import concourse.bass as bass
from concourse import mybir

ALU = mybir.AluOpType
ACT = mybir.ActivationFunctionType
AXX = mybir.AxisListType.X
F32 = mybir.dt.float32
BF16 = mybir.dt.bfloat16
I32 = mybir.dt.int32
U8 = mybir.dt.uint8

P = 128
B, S, D = 16, 256, 256
PAIRS = B // 2
H, DH = 16, 16
A, E = 64, 16
EROW = 32
FF = 1024
FB = FF // P
C4 = 512
NC = 10
EPS = 1e-5
NEG = -1.0e30
BIG = 3.0e38
VW = DH + 1
CH = 2
NCH = 2 * H // CH
RING = 4
LEAD = 1
HEADS = 2 * H
Q_PART = [0, 0, 1, 0, 2, 1]
K_PART = [0, 1, 0, 2, 0, 1]
STACK = len(Q_PART) * DH
MAGIC = 12582912.0
PI2_A = 6.28125
PI2_B = float(np.float32(np.round((2 * np.pi - PI2_A) * 2.0**21) / 2.0**21))
PI2_C = float(2 * np.pi - PI2_A - PI2_B)
(C_SCALE, C_SHIFT, C_ONESC, C_SHIFT3, C_DT, C_EB) = (0, 2, 4, 6, 8, 9)
LINKS = {"front": 32, "heads": 2, "back": 3, "pool": 4, "pool_back": 1}

LAG_T, LAG_V = 2, 3
HEAD0 = 1
SLOTS = HEAD0 + HEADS + LAG_V
AT = {"ctx": 0, "wo": 1, "x5": 2, "hn": 3, "hn_turn": 4, "w1": 5, "w2a": 6, "w2b": 7, "out": 8, "hold": 9,
      "prods": 4, "diffs": 6, "edges": 7, "l0": 9, "x1": 10, "x1_turn": 11, "down": 12, "expert": 13,
      "up": 14, "xs": 15, "x2": 16, "avg0": 17, "var0": 18, "nmr0": 19, "x2_turn": 19, "aff0": 20,
      "w_in": 21, "z": 22, "avg1": 23, "var1": 24, "nmr1": 25, "zn": 25, "aff1": 26, "w_out": 27,
      "x3": 28, "xn3": 29, "x3_turn": 30, "q": 31, "k": 32, "v": 33, "parts": 33}


def wait_alone(eng, sem, value):
    eng.wait_ge(sem, value)
    eng.nop(nofuse=True)


def window(ap, offset, dims):
    first = list(ap.ap[0])
    return bass.AP(ap.tensor, ap.offset + offset, [first] + [list(d) for d in dims])


def adapter_to_attention_kernel(nc, i, out):
    with ExitStack() as keep:
        def sb(name, shape, dt=F32):
            return keep.enter_context(nc.sbuf_tensor(name, shape, dt))

        def sem(name):
            return keep.enter_context(nc.semaphore(name))

        ident = sb("ident", [P, P])
        mean_mat = sb("mean_mat", [P, P])
        half_neg = sb("half_neg", [P, 4])
        gradT = sb("gradT", [P, 2, S])
        lapT = sb("lapT", [P, 2, S])
        gA0, gB0, gB1, gB2, gU, gW = (sb(n, [P, 2, D]) for n in ("gA0", "gB0", "gB1", "gB2h", "gU", "gW"))
        edge1 = sb("edge1", [P, 2, 8])
        edge3 = sb("edge3", [P, 2, 8])
        downT = sb("downT", [P, 2, A])
        down_b = sb("down_b", [A, 1])
        upT = sb("upT", [A, D])
        gammaT = sb("gammaT", [P, 2, S])
        betaT = sb("betaT", [P, 2, S])
        w_in = sb("w_in", [P, 2, D])
        w_out = sb("w_out", [P, 2, D])
        wq, wk, wv, wo = (sb(n, [P, 2, D]) for n in ("wq", "wk", "wv", "wo"))
        w1 = sb("w1", [P, 2, FF])
        w2 = sb("w2", [P, FB, D])
        b_in, bq, bk, g2, beta2 = (sb(n, [P, 2]) for n in ("b_in", "bq", "bk", "g2", "beta2"))
        b1 = sb("b1", [P, FB])
        up_b, ln_g, ln_b, b_out, bv, bo, b2 = (
            sb(n, [P, D]) for n in ("up_b", "ln_g", "ln_b", "b_out", "bv", "bo", "b2"))
        cond = sb("cond", [P, B, NC])
        sel_dram = nc.dram_tensor("sel_dram", [B, A, A], F32, kind="Internal").ap()
        part_dram = nc.dram_tensor("part_dram", [2, 3, D, 2 * S], BF16, kind="Internal").ap()

        w_loaded = sem("w_loaded")
        bq_scaled = sem("bq_scaled")
        ones_set = sem("ones_set")

        WEIGHT_LOADS = [
            (gradT, "gradT"), (lapT, "lapT"), (downT, "downT"), (w_in, "L2_cond_W_in"),
            (w_out, "L2_cond_W_out"), (wq, "L3_cond_Wq"), (wk, "L3_cond_Wk"), (wv, "L3_cond_Wv"),
            (wo, "L3_cond_Wo"), (w1, "L3_cond_W1"), (w2, "L3_cond_W2"), (gammaT, "gammaT"),
            (betaT, "betaT"),
        ]
        COLUMN_LOADS = [(b_in, "L2_cond_b_in"), (bk, "L3_cond_bk"), (g2, "L3_cond_g2"),
                        (beta2, "L3_cond_beta2"), (b1, "L3_cond_b1")]
        ROW_LOADS = [(up_b, "L1_cond_up_b"), (ln_g, "L1_cond_ln_gamma"), (ln_b, "L1_cond_ln_beta"),
                     (b_out, "L2_cond_b_out"), (bv, "L3_cond_bv"), (bo, "L3_cond_bo"),
                     (b2, "L3_cond_b2")]
        N_LOADS = len(WEIGHT_LOADS) + len(COLUMN_LOADS) + len(ROW_LOADS) + 2

        setup(nc, i, locals())

        F = sb("F", [P, 4, D])
        bufs = sb("front", [P, 9, 4, D])
        p_a0, p_b0, p_b1, p_b2, p_u, p_w, X1, X3, x1 = (bufs[:, n] for n in range(9))

        def as_feature(t):
            return t[:, :, :].rearrange("p (c b) s -> p c (b s)", c=2)

        x1T = as_feature(p_a0)
        hidT = p_b0[0:A, 0:2, :].rearrange("p b s -> p (b s)")
        expT = p_b0[0:A, 2:4, :].rearrange("p b s -> p (b s)")
        res1 = p_b1
        xs = p_b2
        x2 = p_u
        x2T = as_feature(p_a0)
        yT = as_feature(p_w)
        zT = as_feature(X1)
        x2b = X3
        x3 = x1
        xn3 = p_b1
        qkf = [as_feature(p_a0), as_feature(p_b0)]
        rest = [as_feature(p_b2), as_feature(p_u)]
        part_room = bufs[:, 5:8].rearrange("p n t s -> p (n t s)").bitcast(BF16)
        parts = [part_room[:, w * 12 * D:(w + 1) * 12 * D].rearrange("p (j n) -> p j n", j=3) for w in range(2)]
        V_next = x1
        ew = sb("ew", [A, 2, A])
        cp = sb("cp", [P, 2, NC])
        qs = sb("q_stack", [P, H * 2 * S], BF16)
        ks = sb("k_stack", [P, H * 2 * S], BF16)
        stacks = [t[0:STACK, :].rearrange("p (h n) -> p h n", h=H) for t in (qs, ks)]
        ffT = sb("ffT", [P, FB, 2 * S])
        x4T_hold = sb("x4T_hold", [P, 2, 2 * S])
        x4T = sb("x4T", [P, 2, 2 * S])
        V = sb("V", [P, 4, H, VW])
        bias = sb("bias", [P, RING, CH * 2, S])
        mask_raw = sb("mask_raw", [P, 4, S], U8)
        mask_add = sb("mask_add", [P, 4, S], BF16)
        Sn = sb("Sn", [P, 2, 2, S])
        nmax = sb("nmax", [P, HEADS, 2])
        Pr = sb("Pr", [P, 3, 2, S])
        PT = sb("PT", [P, 2, 2, S])
        rsum = sb("rsum", [P, 2, H])
        ctxn = sb("ctxn", [P, 4, D])
        ctxT = sb("ctxT", [P, 2, 2 * S])
        x5 = sb("x5", [P, 4, D])
        x5b = x5
        hn = ctxn
        stats = sb("stats", [P, 4, 6])
        mv = sb("mv", [P, 4, 2])
        ms = sb("ms", [P, 2, 2])
        gs = sb("gs", [P, 2, 2])
        var = sb("var", [P, 4])
        rstd = sb("rstd", [P, 4])
        nmr = sb("nmr", [P, 2])
        back_stats, back_mv, back_var, back_rstd = (
            sb(n, [P, 4, m]) for n, m in (("back_stats", 6), ("back_mv", 2), ("back_var", 1), ("back_rstd", 1)))
        edge_f = sb("edge_f", [P, 4, 8])
        edge_p = sb("edge_p", [P, 2, 4, 8])

        G, SP_, TP, CP = (keep.enter_context(nc.psum_tensor(n, [P, 2, 512], F32))
                          for n in ("G", "scores_ps", "PT_ps", "ctx_ps"))
        Gt = G[:, :, :].rearrange("p c (t n) -> p (c t) n", t=2)
        Ct = CP[:, :, :].rearrange("p c (t n) -> p (c t) n", t=2)

        f_loaded, cond_loaded, ew_loaded, mask_loaded = (
            sem(n) for n in ("f_loaded", "cond_loaded", "ew_loaded", "mask_loaded"))
        bias_loaded = [sem(f"bias_loaded{n}") for n in range(RING)]
        prods = sem("prods")
        l0_in, l0_mm, x1_pre, x1_ok, x1_tr, x1T_ok = (
            sem(n) for n in ("l0_in", "l0_mm", "x1_pre", "x1_ok", "x1_tr", "x1T_ok"))
        down_mm, hid_ok, exp_mm, expT_ok, up_mm, res1_ok = (
            sem(n) for n in ("down_mm", "hid_ok", "exp_mm", "expT_ok", "up_mm", "res1_ok"))
        var_ok, rstd_ok = sem("var_ok"), sem("rstd_ok")
        back_var_ok, back_rstd_ok = sem("back_var_ok"), sem("back_rstd_ok")
        V_moved, held = sem("V_moved"), sem("held")
        mstat_ok, mstat_mm, mstat_read = sem("mstat_ok"), sem("mstat_mm"), sem("mstat_read")
        x2_ok, x2_tr, norm_ok, xnT_ok, affine_ok, y_ok = (
            sem(n) for n in ("x2_ok", "x2_tr", "norm_ok", "xnT_ok", "affine_ok", "y_ok"))
        win_mm, x2b_ok, wout_mm, xn3_ok, x3_tr, x4T_ok = (
            sem(n) for n in ("win_mm", "x2b_ok", "wout_mm", "xn3_ok", "x3_tr", "x4T_ok"))
        qkv_mm, qk_ok, split_ok, part_written, stack_loaded, V_ok = (
            sem(n) for n in ("qkv_mm", "qk_ok", "split_ok", "part_written", "stack_loaded", "V_ok"))
        mask_ok, masked = sem("mask_ok"), sem("masked")
        score_mm, biased, prob_ok, pt_tr, pt_even, pt_odd, pv_mm, ctx_ok = (
            sem(n) for n in ("score_mm", "biased", "prob_ok", "pt_tr", "pt_even", "pt_odd", "pv_mm", "ctx_ok"))
        ctx_tr, ctxT_ok, wo_mm, hn_ok, hn_tr, hT_ok = (
            sem(n) for n in ("ctx_tr", "ctxT_ok", "wo_mm", "hn_ok", "hn_tr", "hT_ok"))
        x5b_ok, w1_mm, ff_ok, w2_mm, out_ok, stored = (
            sem(n) for n in ("x5b_ok", "w1_mm", "ff_ok", "w2_mm", "out_ok", "stored"))
        done = {n: sem(f"{n}_links") for n in LINKS}

        x_in = i["x"].rearrange("(i b) (c p) y -> i p (b c) y", b=2, p=P)
        x_out = out.rearrange("(i b) (c p) y -> i p (b c) y", b=2, p=P)
        mask_in = i["mask_Bx1xSxS_bk0"].rearrange("(i b) o (c p) k -> i p (b o c) k", b=2, p=P)
        side_in = i["fside_Bx16xSxS_0"].rearrange("(i b) h (c p) k -> i p (b h c) k", b=2, p=P)
        sel_in = sel_dram.rearrange("(i b) a o -> i a b o", b=2)
        cond_in = cond[:, :, :].rearrange("p (i b) n -> p i (b n)", b=2)
        part_out = part_dram.rearrange("w j (c p) n -> w p j c n", p=P)
        part_in = part_dram.rearrange("w j (h d) n -> w j d h n", d=DH)

        def bc(ap, n):
            return window(ap, 0, [[0, n], list(ap.ap[1])])

        block = keep.enter_context(nc.Block())

        def run(eng, turn, front, back):
            front(0, None)
            turn(0, False, True)
            with eng.Fori(1, PAIRS - 1) as j:
                turn(j, True, True)
            turn(PAIRS - 1, True, False)
            back(PAIRS - 1, None)

        class Links:

            def __init__(self, eng, name, j):
                self.eng, self.name, self.j, self.n = eng, name, j, 0

            def __call__(self, ins, alone=False):
                self.n += 1
                ins.then_inc(done[self.name], 1)
                value = self.j * LINKS[self.name] + self.n
                if alone:
                    wait_alone(self.eng, done[self.name], value)
                else:
                    self.eng.wait_ge(done[self.name], value)

            def end(self):
                assert self.n == LINKS[self.name], (self.name, self.n)

        @block.sync
        def _(sp):
            def load_front(j):
                sp.dma_start(F[:, :, :], x_in[j]).then_inc(f_loaded, 16)

            def load_small(j):
                sp.dma_start(cp[:, :, :].rearrange("p b n -> p (b n)"), cond_in[:, j, :]).then_inc(cond_loaded, 16)
                sp.dma_start(ew[:, :, :], sel_in[j]).then_inc(ew_loaded, 16)
                sp.dma_start(mask_raw[:, :, :], mask_in[j]).then_inc(mask_loaded, 16)

            def turn(j, first, last):
                for c in range(NCH):
                    if c == 2 and not last:
                        sp.wait_ge(x1_pre, LEAD + j + 1)
                        load_front(j + 1)
                    if c == RING and not last:
                        sp.wait_ge(x4T_ok, LEAD + j + 1)
                        sp.wait_ge(mask_ok, LEAD + j + 1)
                        load_small(j + 1)
                    if not first or c >= RING:
                        sp.wait_ge(biased, LEAD + j * (2 * HEADS) + 2 * CH * (c - RING + 1))
                    sp.dma_start(bias[:, c % RING, :, :],
                                 side_in[j, :, 2 * CH * c:2 * CH * (c + 1), :]).then_inc(bias_loaded[c % RING], 16)

            load_front(0)
            load_small(0)
            turn(0, True, False)
            with sp.Fori(1, PAIRS - 1) as j:
                turn(j, False, False)
            turn(PAIRS - 1, False, True)

        @block.gpsimd
        def _(pool):
            links = {}

            def add_mask(j, c):
                b = c * CH // H
                pool.wait_ge(bias_loaded[c % RING], (j * (NCH // RING) + c // RING + 1) * 16)
                t = bias[:, c % RING, :, :].rearrange("p (h q) k -> p h (q k)", h=CH)
                m = mask_add[:, 2 * b:2 * b + 2, :].rearrange("p q k -> p (q k)")
                nc.gpsimd.tensor_tensor(t, t, bc(m, CH), ALU.add).then_inc(masked, 1)

            def next_mask(j):
                pool.wait_ge(mask_loaded, (j + 1) * 16)
                pool.wait_ge(masked, LEAD + j * NCH)
                pool.nop(nofuse=True)
                nc.gpsimd.tensor_scalar(mask_add[:, :, :], mask_raw[:, :, :], NEG, None, ALU.mult).then_inc(mask_ok, 1)
                pool.wait_ge(mask_ok, LEAD + j + 1)
                add_mask(j, 0)
                add_mask(j, 1)

            def inv_std(link, v, r, v_ok, r_ok, count):
                wait_alone(pool, v_ok, count)
                link(nc.gpsimd.tensor_scalar(r, v, EPS, None, ALU.add))
                nc.gpsimd.tensor_tensor(r, r, half_neg[:, 0:r.shape[1]], ALU.pow).then_inc(r_ok, 1)

            def front(j, n):
                def at(step):
                    return n is None or AT[step] == n
                if n is None or n == 0:
                    links["f"] = Links(pool, "pool", j)
                link = links["f"]

                def inv(m, k):
                    inv_std(link, var[:, 0:m], rstd[:, 0:m], var_ok, rstd_ok, j * 4 + k + 1)
                if at("prods"):
                    pool.wait_ge(f_loaded, (j + 1) * 16)
                    if not isinstance(j, int) or j > 0:
                        pool.wait_ge(V_ok, j)
                    for dst, grid in ((p_a0, gA0), (p_b1, gB1)):
                        nc.gpsimd.tensor_tensor(dst[:, :, :].rearrange("p (b c) y -> p b (c y)", b=2),
                                                F[:, :, :].rearrange("p (b c) y -> p b (c y)", b=2),
                                                bc(grid[:, :, :].rearrange("p c y -> p (c y)"), 2),
                                                ALU.mult).then_inc(prods, 1)
                if at("down"):
                    pool.wait_ge(x1_ok, j + 1)
                    nc.gpsimd.tensor_tensor(res1[:, :, :], x1[:, :, :], bc(up_b[:, :], 4), ALU.add).then_inc(res1_ok, 1)
                if at("xs"):
                    inv(4, 0)
                if at("var0"):
                    inv(2, 1)
                if at("aff0"):
                    pool.wait_ge(x2_ok, j + 1)
                    nc.gpsimd.tensor_tensor(x2b[:, :, :], x2[:, :, :], bc(b_out[:, :], 4), ALU.add).then_inc(x2b_ok, 1)
                if at("var1"):
                    inv(2, 2)
                if at("x3"):
                    inv(4, 3)
                    link.end()

            def back(j, n):
                def at(step):
                    return n is None or AT[step] == n
                if at("x5"):
                    link = Links(pool, "pool_back", j)
                    inv_std(link, back_var[:, :, 0], back_rstd[:, :, 0], back_var_ok, back_rstd_ok, j + 1)
                    link.end()
                if at("w1"):
                    pool.wait_ge(hn_ok, j + 1)
                    nc.gpsimd.tensor_tensor(x5b[:, :, :], x5[:, :, :], bc(b2[:, :], 4), ALU.add).then_inc(x5b_ok, 1)

            def turn(j, with_back, with_front):
                for n in range(SLOTS):
                    if n % CH == 1 and 2 <= n // CH + 2 < NCH:
                        add_mask(j, n // CH + 2)
                    if with_back:
                        back(j - 1, n)
                    if with_front:
                        front(j + 1, n)
                if with_front:
                    next_mask(j + 1)

            nc.gpsimd.memset(V[:, :, :, DH:VW], 1.0).then_inc(ones_set, 1)
            for s in (mask_ok, masked):
                pool.sem_inc(s, LEAD)
            next_mask(0)
            run(pool, turn, front, back)

        @block.vector
        def _(dve):
            links = {}

            def by_grid(out_, grid):
                return nc.vector.tensor_tensor(
                    out_[:, :, :].rearrange("p (b c) y -> p b (c y)", b=2),
                    F[:, :, :].rearrange("p (b c) y -> p b (c y)", b=2),
                    bc(grid[:, :, :].rearrange("p c y -> p (c y)"), 2), ALU.mult)

            def row_stats(link, src, st, m, v, v_ok):
                for t in range(4):
                    ins = nc.vector.bn_stats(out=st[:, t, :], in_=src[:, t, :])
                link(ins, alone=True)
                for t in range(4):
                    ins = nc.vector.bn_aggr(out=m[:, t, :], in_=st[:, t, :])
                link(ins)
                nc.vector.tensor_copy(v, m[:, :, 1]).then_inc(v_ok, 1)

            def row_norm(dst, src, m, r):
                for t in range(4):
                    ins = nc.vector.tensor_scalar(dst[:, t, :], src[:, t, :], m[:, t, 0:1], r[:, t:t + 1],
                                                  ALU.subtract, ALU.mult)
                return ins

            def whole_stats(link, pieces):
                for b in range(2):
                    for c in range(2):
                        ins = nc.vector.bn_stats(out=stats[:, 2 * b + c, :], in_=pieces[b][c])
                link(ins, alone=True)
                for b in range(2):
                    ins = nc.vector.bn_aggr(out=mv[:, b, :],
                                            in_=stats[:, 2 * b:2 * b + 2, :].rearrange("p c n -> p (c n)"))
                link(ins)
                nc.vector.tensor_copy(ms[:, :, 0], mv[:, 0:2, 0])
                link(nc.vector.tensor_tensor(ms[:, :, 1], mv[:, 0:2, 0], mv[:, 0:2, 0], ALU.mult))
                nc.vector.tensor_tensor(ms[:, :, 1], ms[:, :, 1], mv[:, 0:2, 1], ALU.add).then_inc(mstat_ok, 1)

            def whole_var(link, j, k):
                dve.wait_ge(mstat_mm, j * 2 + k + 1)
                nc.vector.tensor_copy(gs[:, :, :].rearrange("p b n -> p (b n)"), G[:, 0, 0:4]).then_inc(mstat_read, 1)
                dve.wait_ge(mstat_read, j * 2 + k + 1)
                link(nc.vector.tensor_tensor(nmr[:, :], gs[:, :, 0], gs[:, :, 0], ALU.mult))
                nc.vector.tensor_tensor(var[:, 0:2], gs[:, :, 1], nmr[:, :], ALU.subtract).then_inc(var_ok, 1)

            def whole_nmr(link, j, k):
                dve.wait_ge(rstd_ok, j * 4 + k + 2)
                link(nc.vector.tensor_tensor(nmr[:, :], gs[:, :, 0], rstd[:, 0:2], ALU.mult))
                nc.vector.tensor_scalar(nmr[:, :], nmr[:, :], -1.0, None, ALU.mult).then_inc(norm_ok, 1)

            def affine(link, t, j, k):
                dve.wait_ge(xnT_ok, j * 2 + k + 1)
                v = t.rearrange("p c (b s) -> p c b s", b=2)
                g = window(gammaT[:, :, :], 0, [[S, 2], [0, 2], [1, S]])
                be = window(betaT[:, :, :], 0, [[S, 2], [0, 2], [1, S]])
                link(nc.vector.tensor_tensor(v, v, g, ALU.mult))
                nc.vector.tensor_tensor(v, v, be, ALU.add).then_inc(affine_ok, 1)

            inner, left, right = slice(1, D - 1), slice(0, D - 2), slice(2, D)

            def front(j, n):
                def at(step):
                    return n is None or AT[step] == n
                if n is None or n == 0:
                    links["f"] = Links(dve, "front", j)
                link = links["f"]
                if at("prods"):
                    dve.wait_ge(f_loaded, (j + 1) * 16)
                    if not isinstance(j, int) or j > 0:
                        dve.wait_ge(part_written, j * 32)
                    by_grid(p_b0, gB0)
                    by_grid(p_b2, gB2)
                    by_grid(p_u, gU)
                    link(by_grid(p_w, gW))
                if at("diffs"):
                    nc.vector.tensor_tensor(X1[:, :, inner], p_b2[:, :, right], p_b2[:, :, left], ALU.subtract)
                    link(nc.vector.tensor_tensor(X3[:, :, inner], p_u[:, :, right], p_w[:, :, left], ALU.add))
                    dve.wait_ge(prods, 2 * j + 2)
                    nc.vector.tensor_tensor(X1[:, :, inner], X1[:, :, inner], p_a0[:, :, inner], ALU.subtract)
                    nc.vector.tensor_tensor(X3[:, :, inner], X3[:, :, inner], p_b1[:, :, inner], ALU.subtract)
                if at("edges"):
                    link(nc.vector.tensor_copy(edge_f[:, :, :].rearrange("p t (e j) -> p t e j", e=2),
                                               window(F[:, :, :], 0, [[D, 4], [D - 4, 2], [1, 4]])))
                    for m, e in enumerate((edge1, edge3)):
                        ins = nc.vector.tensor_tensor(
                            edge_p[:, m, :, :].rearrange("p (b c) j -> p b (c j)", b=2),
                            edge_f[:, :, :].rearrange("p (b c) j -> p b (c j)", b=2),
                            bc(e[:, :, :].rearrange("p c j -> p (c j)"), 2), ALU.mult)
                    link(ins)
                    for m, x in enumerate((X1, X3)):
                        ins = nc.vector.tensor_reduce(window(x[:, :, :], 0, [[D, 4], [D - 1, 2]]),
                                                      edge_p[:, m, :, :].rearrange("p t (e j) -> p t e j", e=2),
                                                      AXX, ALU.add)
                    ins.then_inc(l0_in, 1)
                if at("x1"):
                    dve.wait_ge(l0_in, j + 1)
                    dve.wait_ge(l0_mm, j + 1)
                    for c in range(2):
                        v = X3[:, :, :].rearrange("p (b c) y -> p c b y", b=2)[:, c]
                        ins = nc.vector.tensor_tensor(v, v, G[:, c, :].rearrange("p (b y) -> p b y", b=2), ALU.add)
                    link(ins)
                    dve.wait_ge(cond_loaded, (j + 1) * 16)
                    for b in range(2):
                        ins = nc.vector.scalar_tensor_tensor(
                            out=x1[:, 2 * b:2 * b + 2, :], in0=X3[:, 2 * b:2 * b + 2, :],
                            scalar=cp[:, b, C_DT:C_DT + 1], in1=F[:, 2 * b:2 * b + 2, :],
                            op0=ALU.mult, op1=ALU.add)
                    ins.then_inc(x1_pre, 1)
                if at("xs"):
                    dve.wait_ge(up_mm, j + 1)
                    dve.wait_ge(res1_ok, j + 1)
                    link(nc.vector.tensor_tensor(xs[:, :, :], Gt, res1[:, :, :], ALU.add))
                    row_stats(link, xs, stats, mv, var[:, 0:4], var_ok)
                if at("x2"):
                    dve.wait_ge(rstd_ok, j * 4 + 1)
                    link(row_norm(xs, xs, mv, rstd))
                    link(nc.vector.tensor_tensor(x2[:, :, :], xs[:, :, :], bc(ln_g[:, :], 4), ALU.mult))
                    nc.vector.tensor_tensor(x2[:, :, :], x2[:, :, :], bc(ln_b[:, :], 4), ALU.add).then_inc(x2_ok, 1)
                if at("avg0"):
                    dve.wait_ge(x2_ok, j + 1)
                    whole_stats(link, [[x2[:, 2 * b + c, :] for c in range(2)] for b in range(2)])
                if at("var0"):
                    whole_var(link, j, 0)
                if at("nmr0"):
                    whole_nmr(link, j, 0)
                if at("aff0"):
                    affine(link, x2T, j, 0)
                if at("z"):
                    dve.wait_ge(win_mm, j + 1)
                    for c in range(2):
                        ins = nc.vector.tensor_scalar(zT[:, c, :], G[:, c, :], b_in[:, c:c + 1], None, ALU.add)
                    link(ins)
                    whole_stats(link, [[zT[:, c, b * S:(b + 1) * S] for c in range(2)] for b in range(2)])
                if at("var1"):
                    whole_var(link, j, 1)
                if at("nmr1"):
                    whole_nmr(link, j, 1)
                if at("aff1"):
                    affine(link, zT, j, 1)
                if at("x3"):
                    dve.wait_ge(wout_mm, j + 1)
                    dve.wait_ge(x2b_ok, j + 1)
                    link(nc.vector.tensor_tensor(x3[:, :, :], Gt, x2b[:, :, :], ALU.add))
                    row_stats(link, x3, stats, mv, var[:, 0:4], var_ok)
                if at("xn3"):
                    dve.wait_ge(rstd_ok, j * 4 + 4)
                    row_norm(xn3, x3, mv, rstd).then_inc(xn3_ok, 1)
                for w in range(2):
                    if at("qk"[w]):
                        dve.wait_ge(qk_ok, 2 * j + w + 1)
                        pt = parts[w][:, :, :].rearrange("p j (c n) -> p j c n", c=2)
                        link(nc.vector.tensor_copy(pt[:, 0], qkf[w]))
                        link(nc.vector.tensor_tensor(rest[w], qkf[w], pt[:, 0], ALU.subtract))
                        link(nc.vector.tensor_copy(pt[:, 1], rest[w]))
                        nc.vector.tensor_tensor(pt[:, 2], rest[w], pt[:, 1], ALU.subtract).then_inc(split_ok, 1)
                if at("v"):
                    dve.wait_ge(qkv_mm, 3 * j + 3)
                    nc.vector.tensor_tensor(V_next[:, :, :], Gt, bc(bv[:, :], 4), ALU.add).then_inc(V_ok, 1)
                    link.end()

            def back(j, n):
                def at(step):
                    return n is None or AT[step] == n
                if n is None or n == 0:
                    links["b"] = Links(dve, "back", j)
                link = links["b"]
                if at("x5"):
                    dve.wait_ge(wo_mm, LEAD + j + 1)
                    dve.wait_ge(stored, LEAD + 16 * j)
                    link(nc.vector.tensor_tensor(x5[:, :, :], Gt, bc(bo[:, :], 4), ALU.add))
                    row_stats(link, x5, back_stats, back_mv, back_var[:, :, 0], back_var_ok)
                if at("hn"):
                    dve.wait_ge(back_rstd_ok, j + 1)
                    row_norm(hn, x5, back_mv, back_rstd[:, :, 0]).then_inc(hn_ok, 1)
                if at("out"):
                    dve.wait_ge(w2_mm, j + 1)
                    dve.wait_ge(x5b_ok, j + 1)
                    nc.vector.tensor_tensor(x5b[:, :, :], Gt, x5b[:, :, :], ALU.add).then_inc(out_ok, 1)
                    link.end()

            def bias_and_max(j, n):
                c = n // CH
                dve.wait_ge(masked, LEAD + j * NCH + c + 1)
                dve.wait_ge(score_mm, j * HEADS + n + 1)
                dve.wait_ge(prob_ok, LEAD + j * HEADS + max(n - 1, 0))
                dve.nop(nofuse=True)
                for q in range(2):
                    nc.vector.tensor_tensor_reduce(
                        out=Sn[:, n % 2, q, :], in0=SP_[:, n % 2, q * S:(q + 1) * S],
                        in1=bias[:, c % RING, 2 * (n % CH) + q, :], scale=-1.0, scalar=BIG,
                        op0=ALU.add, op1=ALU.min, accum_out=nmax[:, n, q:q + 1]).then_inc(biased, 1)

            def finish_ctx(link, j, b):
                dve.wait_ge(pv_mm, LEAD + j * HEADS + H * (b + 1))
                if b == 0:
                    dve.wait_ge(ctx_tr, LEAD + j)
                v = CP[:, :, 0:H * VW].rearrange("p q (h w) -> p q h w", w=VW)
                link(nc.vector.reciprocal(rsum[:, :, :], v[:, :, :, DH]))
                for q in range(2):
                    ins = nc.vector.tensor_tensor(
                        ctxn[:, 2 * b + q, :].rearrange("p (h d) -> p h d", h=H), v[:, q, :, 0:DH],
                        window(rsum[:, q, :], 0, [[1, H], [0, DH]]), ALU.mult)
                ins.then_inc(ctx_ok, 1)

            def turn(j, with_back, with_front):
                link = Links(dve, "heads", j)
                for n in range(SLOTS):
                    h = n - HEAD0
                    if n == 0:
                        dve.wait_ge(V_ok, j + 1)
                        dve.wait_ge(pv_mm, LEAD + j * HEADS)
                        nc.vector.tensor_copy(V[:, :, :, 0:DH],
                                              V_next[:, :, :].rearrange("p t (h d) -> p t h d", h=H)).then_inc(V_moved, 1)
                    if h == H + LAG_V:
                        finish_ctx(link, j, 0)
                    if 0 <= h < HEADS:
                        bias_and_max(j, h)
                    m = h - LAG_T
                    if 0 <= m < HEADS and m % 2:
                        dve.wait_ge(pt_tr, LEAD + j * HEADS + m + 1)
                        dve.wait_ge(pv_mm, LEAD + j * HEADS + m - 1)
                        nc.vector.tensor_copy(PT[:, m % 2, :, :].rearrange("p c q -> p (c q)"),
                                              TP[:, m % 2, :]).then_inc(pt_odd, 1)
                    if with_back:
                        back(j - 1, n)
                    if n == AT["hold"]:
                        dve.wait_ge(x4T_ok, LEAD + j + 1)
                        dve.wait_ge(wo_mm, LEAD + j)
                        nc.vector.tensor_copy(x4T_hold[:, :, :], x4T[:, :, :]).then_inc(held, 1)
                    if with_front:
                        front(j + 1, n)
                finish_ctx(link, j, 1)
                link.end()

            for s in (x1_pre, biased, pt_odd, ctx_ok, out_ok):
                dve.sem_inc(s, LEAD)
            dve.wait_ge(ones_set, 1)
            run(dve, turn, front, back)

        @block.scalar
        def _(act):
            def evac(dst, src, done_sem, scale=1.0, b=0.0):
                ins = nc.scalar.activation(dst, src, ACT.Identity, bias=b, scale=scale)
                if done_sem is not None:
                    ins.then_inc(done_sem, 1)

            def front(j, n):
                def at(step):
                    return n is None or AT[step] == n
                if at("x1"):
                    act.wait_ge(x1_pre, LEAD + j + 1)
                    nc.scalar.activation(x1[:, :, :], x1[:, :, :], ACT.Relu).then_inc(x1_ok, 1)
                if at("x1_turn"):
                    act.wait_ge(x1_tr, j + 1)
                    evac(x1T, G[:, :, :], x1T_ok)
                if at("down"):
                    act.wait_ge(down_mm, j + 1)
                    nc.scalar.activation(hidT, G[0:A, 0, :], ACT.Gelu, bias=down_b[:, 0:1]).then_inc(hid_ok, 1)
                if at("expert"):
                    act.wait_ge(exp_mm, j + 1)
                    for b in range(2):
                        evac(expT[:, b * S:(b + 1) * S], G[0:A, 1, b * S:(b + 1) * S],
                             expT_ok if b else None, b=cp[0:A, b, C_EB:C_EB + 1])
                for k in range(2):
                    if at(("x2_turn", "zn")[k]):
                        if k == 0:
                            act.wait_ge(x2_tr, j + 1)
                        act.wait_ge(norm_ok, 2 * j + k + 1)
                        dst = (x2T, zT)[k].rearrange("p c (b s) -> p b c s", b=2)
                        src = (G[:, :, :], zT)[k].rearrange("p c (b s) -> p b c s", b=2)
                        for b in range(2):
                            evac(dst[:, b], src[:, b], xnT_ok if b else None, scale=rstd[:, b:b + 1],
                                 b=nmr[:, b:b + 1])
                    if at(("aff0", "aff1")[k]):
                        act.wait_ge(affine_ok, 2 * j + k + 1)
                        src = (x2T, zT)[k]
                        for c in range(2):
                            for b in range(2):
                                ins = nc.scalar.activation(
                                    yT[:, c, b * S:(b + 1) * S], src[:, c, b * S:(b + 1) * S], ACT.Silu,
                                    bias=cp[:, b, C_SHIFT + c:C_SHIFT + c + 1],
                                    scale=cp[:, b, C_SCALE + c:C_SCALE + c + 1])
                        ins.then_inc(y_ok, 1)
                if at("x3_turn"):
                    act.wait_ge(x3_tr, j + 1)
                    if not isinstance(j, int) or j > 0:
                        act.wait_ge(held, j)
                    for c in range(2):
                        for b in range(2):
                            evac(x4T[:, c, b * S:(b + 1) * S], G[:, c, b * S:(b + 1) * S],
                                 x4T_ok if c and b else None, scale=cp[:, b, C_ONESC + c:C_ONESC + c + 1],
                                 b=cp[:, b, C_SHIFT3 + c:C_SHIFT3 + c + 1])
                for w in range(2):
                    if at("qk"[w]):
                        act.wait_ge(qkv_mm, 3 * j + w + 1)
                        for c in range(2):
                            evac(qkf[w][:, c, :], G[:, c, :], qk_ok if c else None,
                                 scale=(DH ** -0.5, 1.0)[w], b=(bq, bk)[w][:, c:c + 1])
                if at("parts"):
                    for w in range(2):
                        act.wait_ge(split_ok, 2 * j + w + 1)
                        act.dma_start(part_out[w], parts[w][:, :, :].rearrange("p j (c n) -> p j c n", c=2)
                                      ).then_inc(part_written, 16)
                if n is None:
                    load_stacks(j)

            def load_stacks(j):
                act.wait_ge(part_written, (2 * j + 2) * 16)
                for w in range(2):
                    for s, part in enumerate((Q_PART, K_PART)[w]):
                        act.dma_start(stacks[w][s * DH:(s + 1) * DH, :, :], part_in[w, part]).then_inc(stack_loaded, 16)

            def back(j, n):
                def at(step):
                    return n is None or AT[step] == n
                if at("ctx"):
                    act.wait_ge(ctx_tr, LEAD + j + 1)
                    evac(ctxT[:, :, :], G[:, :, :], ctxT_ok)
                if at("hn_turn"):
                    act.wait_ge(hn_tr, j + 1)
                    for c in range(2):
                        evac(ctxT[:, c, :], G[:, c, :], hT_ok if c else None, scale=g2[:, c:c + 1],
                             b=beta2[:, c:c + 1])
                if at("w1"):
                    for f in range(FB):
                        act.wait_ge(w1_mm, j * FB + f + 1)
                        nc.scalar.activation(ffT[:, f, :], G[:, f % 2, :], ACT.Gelu_apprx_sigmoid,
                                             bias=b1[:, f:f + 1]).then_inc(ff_ok, 1)
                if at("out"):
                    act.wait_ge(out_ok, LEAD + j + 1)
                    act.dma_start(x_out[j], x5b[:, :, :]).then_inc(stored, 16)

            def turn(j, with_back, with_front):
                for n in range(SLOTS):
                    h = n - HEAD0
                    if 0 <= h < HEADS:
                        act.wait_ge(pt_tr, LEAD + j * HEADS + max(h - 2, 0))
                        for q in range(2):
                            act.wait_ge(biased, LEAD + j * 2 * HEADS + 2 * h + q + 1)
                            ins = nc.scalar.activation(Pr[:, h % 3, q, :], Sn[:, h % 2, q, :], ACT.Exp,
                                                       bias=nmax[:, h, q:q + 1], scale=-1.0)
                        ins.then_inc(prob_ok, 1)
                    m = h - LAG_T
                    if 0 <= m < HEADS and m % 2 == 0:
                        act.wait_ge(pt_tr, LEAD + j * HEADS + m + 1)
                        act.wait_ge(pv_mm, LEAD + j * HEADS + max(m - 1, 0))
                        nc.scalar.activation(PT[:, m % 2, :, :].rearrange("p c q -> p (c q)"),
                                             TP[:, m % 2, :], ACT.Identity).then_inc(pt_even, 1)
                    if with_back:
                        back(j - 1, n)
                    if with_front:
                        front(j + 1, n)
                if with_front:
                    act.wait_ge(score_mm, (j + 1) * HEADS)
                    load_stacks(j + 1)

            for s in (x4T_ok, prob_ok, pt_even, stored):
                act.sem_inc(s, LEAD)
            act.wait_ge(bq_scaled, 1)
            run(act, turn, front, back)
            act.wait_ge(stored, LEAD + 16 * PAIRS)

        @block.tensor
        def _(pe):
            def turned(src):
                for t in range(4):
                    for c in range(2):
                        ins = pe.transpose(G[:, c, t * P:(t + 1) * P], src[:, t, c * P:(c + 1) * P], ident[:, :])
                return ins

            def by_feature(w, xT):
                for m in range(2):
                    for c in range(2):
                        ins = pe.matmul(G[:, m, :], w[:, c, m * P:(m + 1) * P], xT[:, c, :],
                                        start=(c == 0), stop=(c == 1))
                return ins

            def by_token(w, xT):
                for t in range(4):
                    for c in range(2):
                        ins = pe.matmul(Gt[:, t, :], xT[:, c, t * P:(t + 1) * P], w[:, c, :],
                                        start=(c == 0), stop=(c == 1))
                return ins

            def average(j, k):
                pe.wait_ge(mstat_ok, 2 * j + k + 1)
                pe.matmul(G[:, 0, 0:4], mean_mat[:, :], ms[:, :, :].rearrange("p b n -> p (b n)"),
                          start=True, stop=True).then_inc(mstat_mm, 1)

            def front(j, n):
                def at(step):
                    return n is None or AT[step] == n
                if at("l0"):
                    pe.wait_ge(l0_in, j + 1)
                    if not isinstance(j, int) or j > 1:
                        pe.wait_ge(out_ok, LEAD + j - 1)
                    for m in range(2):
                        for s, (mat, x) in enumerate(((gradT, X1), (lapT, p_b0))):
                            v = x[:, :, :].rearrange("p (b c) y -> p c b y", b=2)
                            for c in range(2):
                                ins = pe.matmul(G[:, m, :].rearrange("p (b y) -> p b y", b=2),
                                                mat[:, c, m * P:(m + 1) * P], v[:, c],
                                                start=(s == 0 and c == 0), stop=(s == 1 and c == 1))
                    ins.then_inc(l0_mm, 1)
                if at("x1_turn"):
                    pe.wait_ge(x1_ok, j + 1)
                    turned(x1).then_inc(x1_tr, 1)
                if at("down"):
                    pe.wait_ge(x1T_ok, j + 1)
                    for c in range(2):
                        ins = pe.matmul(G[0:A, 0, :], downT[:, c, :], x1T[:, c, :], start=(c == 0), stop=(c == 1))
                    ins.then_inc(down_mm, 1)
                if at("expert"):
                    pe.wait_ge(hid_ok, j + 1)
                    wait_alone(pe, ew_loaded, (j + 1) * 16)
                    for b in range(2):
                        ins = pe.matmul(G[0:A, 1, b * S:(b + 1) * S], ew[:, b, :], hidT[:, b * S:(b + 1) * S],
                                        start=True, stop=True)
                    ins.then_inc(exp_mm, 1)
                if at("up"):
                    pe.wait_ge(expT_ok, j + 1)
                    for t in range(4):
                        ins = pe.matmul(Gt[:, t, :], expT[:, t * P:(t + 1) * P], upT[:, :], start=True, stop=True)
                    ins.then_inc(up_mm, 1)
                if at("avg0"):
                    average(j, 0)
                if at("x2_turn"):
                    pe.wait_ge(mstat_read, 2 * j + 1)
                    turned(x2).then_inc(x2_tr, 1)
                if at("w_in"):
                    pe.wait_ge(y_ok, 2 * j + 1)
                    by_feature(w_in, yT).then_inc(win_mm, 1)
                if at("avg1"):
                    average(j, 1)
                if at("w_out"):
                    pe.wait_ge(mstat_read, 2 * j + 2)
                    pe.wait_ge(y_ok, 2 * j + 2)
                    by_token(w_out, yT).then_inc(wout_mm, 1)
                if at("x3_turn"):
                    pe.wait_ge(xn3_ok, j + 1)
                    turned(xn3).then_inc(x3_tr, 1)
                if at("q"):
                    pe.wait_ge(x4T_ok, LEAD + j + 1)
                    by_feature(wq, x4T).then_inc(qkv_mm, 1)
                if at("k"):
                    pe.wait_ge(qk_ok, 2 * j + 1)
                    by_feature(wk, x4T).then_inc(qkv_mm, 1)
                if at("v"):
                    pe.wait_ge(qk_ok, 2 * j + 2)
                    by_token(wv, x4T).then_inc(qkv_mm, 1)

            def back(j, n):
                def at(step):
                    return n is None or AT[step] == n
                if at("ctx"):
                    pe.wait_ge(ctx_ok, LEAD + 2 * j + 2)
                    pe.wait_ge(V_ok, PAIRS if n is None else j + 2)
                    turned(ctxn).then_inc(ctx_tr, 1)
                if at("wo"):
                    pe.wait_ge(ctxT_ok, j + 1)
                    pe.wait_ge(held, j + 1)
                    for t in range(4):
                        for c in range(2):
                            pe.matmul(Gt[:, t, :], ctxT[:, c, t * P:(t + 1) * P], wo[:, c, :],
                                      start=(c == 0), stop=False)
                        for c in range(2):
                            ins = pe.matmul(Gt[:, t, c * P:(c + 1) * P], x4T_hold[:, c, t * P:(t + 1) * P],
                                            ident[:, :], start=False, stop=(c == 1))
                    ins.then_inc(wo_mm, 1)
                if at("hn_turn"):
                    pe.wait_ge(hn_ok, j + 1)
                    turned(hn).then_inc(hn_tr, 1)
                if at("w1"):
                    pe.wait_ge(hT_ok, j + 1)
                    for f in range(FB):
                        if f >= 2:
                            pe.wait_ge(ff_ok, j * FB + f - 1)
                        for c in range(2):
                            ins = pe.matmul(G[:, f % 2, :], w1[:, c, f * P:(f + 1) * P], ctxT[:, c, :],
                                            start=(c == 0), stop=(c == 1))
                        ins.then_inc(w1_mm, 1)
                for t in range(4):
                    if at(("w2a", "w2b")[t // 2]):
                        if t == 0:
                            pe.wait_ge(ff_ok, (j + 1) * FB)
                        for f in range(FB):
                            ins = pe.matmul(Gt[:, t, :], ffT[:, f, t * P:(t + 1) * P], w2[:, f, :],
                                            start=(f == 0), stop=(f == FB - 1))
                        if t == 3:
                            ins.then_inc(w2_mm, 1)

            def scores(j, h):
                b, hh = divmod(h, H)
                pe.wait_ge(biased, LEAD + j * 2 * HEADS + 2 * max(h - 1, 0))
                for q in range(2):
                    ins = pe.matmul(SP_[:, h % 2, q * S:(q + 1) * S],
                                    stacks[0][:, hh, b * S + q * P:b * S + (q + 1) * P],
                                    stacks[1][:, hh, b * S:(b + 1) * S], start=True, stop=True)
                ins.then_inc(score_mm, 1)

            def turn_p(j, m):
                pe.wait_ge(prob_ok, LEAD + j * HEADS + m + 1)
                pe.wait_ge(pt_odd if m % 2 else pt_even, LEAD + j * H + m // 2)
                for q in range(2):
                    for c in range(2):
                        ins = pe.transpose(TP[:, m % 2, c * S + q * P:c * S + (q + 1) * P],
                                           Pr[:, m % 3, q, c * P:(c + 1) * P], ident[:, :])
                ins.then_inc(pt_tr, 1)

            def times_v(j, m):
                b, h = divmod(m, H)
                if h == 0:
                    pe.wait_ge(ctx_ok, LEAD + 2 * j + b)
                    if b == 0:
                        pe.wait_ge(V_moved, j + 1)
                pe.wait_ge(pt_odd if m % 2 else pt_even, LEAD + j * H + m // 2 + 1)
                for q in range(2):
                    for c in range(2):
                        ins = pe.matmul(CP[:, q, h * VW:(h + 1) * VW],
                                        PT[:, m % 2, c, q * P:(q + 1) * P], V[:, 2 * b + c, h, :],
                                        start=(c == 0), stop=(c == 1))
                ins.then_inc(pv_mm, 1)

            def turn(j, with_back, with_front):
                for n in range(SLOTS):
                    h = n - HEAD0
                    if h == 0:
                        pe.wait_ge(stack_loaded, (j + 1) * 16 * len(Q_PART + K_PART))
                    if 0 <= h < HEADS:
                        scores(j, h)
                    if 0 <= h - LAG_T < HEADS:
                        turn_p(j, h - LAG_T)
                    if with_back:
                        back(j - 1, n)
                    if with_front:
                        front(j + 1, n)
                    if 0 <= h - LAG_V < HEADS:
                        times_v(j, h - LAG_V)

            for s in (pv_mm, pt_tr, wo_mm, ctx_tr):
                pe.sem_inc(s, LEAD)
            pe.wait_ge(w_loaded, N_LOADS * 16)
            run(pe, turn, front, back)


def setup(nc, i, k):
    with ExitStack() as ctx:
        def sb(name, shape, dt=F32):
            return ctx.enter_context(nc.sbuf_tensor(name, shape, dt))

        def sem(name):
            return ctx.enter_context(nc.semaphore(name))

        ident, mean_mat, half_neg, cond, sel_dram = (k[n] for n in ("ident", "mean_mat", "half_neg", "cond", "sel_dram"))
        w_loaded = k["w_loaded"]

        cW1 = sb("cW1", [P, C4])
        cW2 = sb("cW2", [P, 4, C4])
        cWsc, cWsh = sb("cWsc", [P, 4, D]), sb("cWsh", [P, 4, D])
        cWada = sb("cWada", [P, 2, 2 * D])
        cb1, cb2 = sb("cb1", [P, 4]), sb("cb2", [P, 4])
        cb = sb("cb", [P, 8])
        gA1 = sb("gA1", [P, 2, D])
        fc = sb("fc", [P, 4])
        rown = sb("rown", [EROW + 1, 1])
        ecoef = sb("ecoef", [P, 4, 8])
        tb = sb("tb", [P, B])
        t3i = sb("t3i", [P, B], I32)
        t3 = sb("t3", [P, B])
        dt_row = sb("dt_row", [P, B])
        idi = sb("idi", [EROW + 1, B], I32)
        idf, idc, one_c, one_v, ok = (sb(n, [EROW + 1, B]) for n in ("idf", "idc", "one_c", "one_v", "ok"))
        etab = sb("etab", [EROW + 1, A * A])
        ebt = sb("ebt", [EROW + 1, A])
        demb = sb("demb", [E, A])
        sel = sb("sel", [B, A * A])
        ang, turns, red, sn = (sb(n, [P, 3, B]) for n in ("ang", "turns", "red", "sn"))
        se = sb("se", [P, 2, B])
        h1, h2 = sb("h1", [P, 4, B]), sb("h2", [P, 4, B])
        edg = sb("edg", [P, 4, 2, 8])
        edt = sb("edt", [P, 2, 2, 8])
        ps = [ctx.enter_context(nc.psum_tensor(f"setup_ps{n}", [P, 512], F32)) for n in range(8)]

        tab_zero, c_loaded, small, id_ok, enc_ok, sin_ok, se_ok = (
            sem(n) for n in ("tab_zero", "c_loaded", "small", "id_ok", "enc_ok", "sin_ok", "se_ok"))
        h1_mm, h1_ok, h2_mm, h2_ok, cond_mm, sel_mm, sel_ok, sel_stored, chain, idn, acts = (
            sem(n) for n in ("h1_mm", "h1_ok", "h2_mm", "h2_ok", "cond_mm", "sel_mm", "sel_ok", "sel_stored", "chain", "idn", "acts"))
        cond_zero = sem("cond_zero")

        block = ctx.enter_context(nc.Block())

        def cols(name):
            return i[name]

        def mat(name):
            return i[name].rearrange("(c p) n -> p c n", p=P)

        C_LOADS = [
            (fc[:, :], i["enc_cols"]), (rown[:, :], i["row_number"]),
            (tb[:, :], i["condB_t"].partition_broadcast(P)),
            (t3i[:, :], i["itok_B_34_63"].partition_broadcast(P)),
            (idi[:, :], i["itok_B_0_15"].partition_broadcast(EROW + 1)),
            (cW1[:, :], i["L2_cond_W1"]), (cW2[:, :, :], mat("L2_cond_W2")),
            (cWsc[:, :, :], mat("L2_cond_Wsc")), (cWsh[:, :, :], mat("L2_cond_Wsh")),
            (cWada[:, :, :], mat("L3_cond_W_ada")),
            (cb1[:, :], cols("L2_cond_b1")), (cb2[:, :], cols("L2_cond_b2")),
            (cb[:, 0:2], cols("L2_cond_bsc")), (cb[:, 2:4], cols("L2_cond_bsh")),
            (cb[:, 4:8], cols("L3_cond_b_ada")), (demb[:, :], i["L1_cond_domain_emb"]),
            (ecoef[:, :, :].rearrange("p a b -> p (a b)"), i["edge_coef"].partition_broadcast(P)),
            (dt_row[:, :], i["condB_dt"].partition_broadcast(P)),
            (gA1[:, :, :], i["L0_cond_A_grid"][1].rearrange("(c p) y -> p c y", p=P)),
        ] + [(k[n][:, :, :], i[g][j].rearrange("(c p) y -> p c y", p=P)) for n, g, j in (
            ("gA0", "L0_cond_A_grid", 0), ("gB0", "L0_cond_B_grid", 0), ("gB1", "L0_cond_B_grid", 1),
            ("gB2", "L0_cond_B_grid", 2))]
        N_C = len(C_LOADS) + 3

        @block.sync
        def _(sp):
            for dst, src in C_LOADS:
                sp.dma_start(dst, src).then_inc(c_loaded, 16)
            sp.wait_ge(tab_zero, 3)
            sp.dma_start(etab[0:E, :], i["expertT"]).then_inc(c_loaded, 16)
            sp.dma_start(etab[EROW:EROW + 1, :], i["eye64"]).then_inc(c_loaded, 16)
            sp.dma_start(ebt[0:E, :], i["L1_cond_expert_b"]).then_inc(c_loaded, 16)
            sp.wait_ge(sel_ok, 8)
            sp.dma_start(sel_dram.rearrange("b a o -> b (a o)"), sel[:, :]).then_inc(sel_stored, 16)
            sp.wait_ge(sel_stored, 16)

        @block.gpsimd
        def _(pool):
            nc.gpsimd.memset(etab[:, :], 0.0).then_inc(tab_zero, 1)
            nc.gpsimd.memset(ebt[:, :], 0.0).then_inc(tab_zero, 1)
            nc.gpsimd.memset(cond[:, :, :], 0.0).then_inc(cond_zero, 1)
            nc.gpsimd.memset(half_neg[:, :], -0.5).then_inc(tab_zero, 1)
            nc.gpsimd.memset(mean_mat[:, :], 1.0 / P)
            nc.gpsimd.memset(ident[:, :], 0.0).then_inc(idn, 1)
            pool.wait_ge(idn, 1)
            nc.gpsimd.affine_select(out=ident[:, :], in_=ident[:, :], compare_op=ALU.not_equal, fill=1.0,
                                    base=0, pattern=[[-1, P]], channel_multiplier=1).then_inc(idn, 1)

        @block.scalar
        def _(act):
            for dst, name in k["WEIGHT_LOADS"]:
                act.dma_start(dst[:, :, :], mat(name)).then_inc(w_loaded, 16)
            for dst, name in k["COLUMN_LOADS"] + [(k["bq"], "L3_cond_bq")]:
                act.dma_start(dst[:, :], cols(name)).then_inc(w_loaded, 16)
            act.dma_start(k["upT"][:, :], i["upT"]).then_inc(w_loaded, 16)
            for dst, name in k["ROW_LOADS"]:
                act.dma_start(dst[:, :], i[name].partition_broadcast(P)).then_inc(w_loaded, 16)
            act.dma_start(k["down_b"][:, :], i["L1_cond_down_b"].rearrange("(a o) -> a o", o=1)).then_inc(w_loaded, 16)
            act.wait_ge(enc_ok, 1)
            nc.scalar.activation(sn[:, :, :], red[:, :, :], ACT.Sin).then_inc(sin_ok, 1)
            act.wait_ge(sin_ok, 1)
            nc.scalar.activation(se[:, :, :], sn[:, 1:3, :], ACT.Silu).then_inc(se_ok, 1)
            act.wait_ge(h1_mm, 1)
            for m in range(4):
                nc.scalar.activation(h1[:, m, :], ps[0][:, m * B:(m + 1) * B], ACT.Silu,
                                     bias=cb1[:, m:m + 1]).then_inc(h1_ok, 1)
            act.wait_ge(w_loaded, (k["N_LOADS"] + 1) * 16)
            nc.scalar.mul(k["bq"][:, :], k["bq"][:, :], DH ** -0.5).then_inc(k["bq_scaled"], 1)
            act.wait_ge(k["bq_scaled"], 1)

        @block.vector
        def _(dve):
            n = [0]

            def link(ins):
                n[0] += 1
                ins.then_inc(chain, 1)
                dve.wait_ge(chain, n[0])

            dve.wait_ge(c_loaded, N_C * 16)
            link(nc.vector.tensor_copy(idf[:, :], idi[:, :]))
            link(nc.vector.tensor_scalar(idc[:, :], idf[:, :], 0.0, float(E - 1), ALU.max, ALU.min))
            nc.vector.tensor_scalar(one_c[:, :], idc[:, :], rown[:, 0:1], None, ALU.is_equal)
            link(nc.vector.tensor_tensor(ok[:, :], idf[:, :], idc[:, :], ALU.is_equal))
            link(nc.vector.tensor_scalar(one_v[:, :], idf[:, :], rown[:, 0:1], None, ALU.is_equal))
            nc.vector.tensor_scalar(one_v[EROW:EROW + 1, :], ok[EROW:EROW + 1, :], -1.0, 1.0, ALU.mult,
                                    ALU.add).then_inc(id_ok, 1)
            link(nc.vector.tensor_copy(t3[:, :], t3i[:, :]))
            nc.vector.tensor_scalar(ang[:, 0, :], tb[:, :], 5000.0, fc[:, 0:1], ALU.mult, ALU.mult)
            link(nc.vector.tensor_scalar(t3[:, :], t3[:, :], 0.01, 4000.0, ALU.mult, ALU.mult))
            for j in (1, 2):
                ins = nc.vector.tensor_scalar(ang[:, j, :], t3[:, :], fc[:, 1:2], None, ALU.mult)
            link(ins)
            inv = float(1 / (2 * np.pi))
            nc.vector.tensor_scalar(turns[:, 0, :], ang[:, 0, :], inv, fc[:, 2:3], ALU.mult, ALU.add)
            nc.vector.tensor_scalar(turns[:, 1, :], ang[:, 1, :], inv, None, ALU.mult)
            link(nc.vector.tensor_scalar(turns[:, 2, :], ang[:, 2, :], inv, 0.25, ALU.mult, ALU.add))
            link(nc.vector.tensor_scalar(turns[:, :, :], turns[:, :, :], MAGIC, None, ALU.add))
            link(nc.vector.tensor_scalar(turns[:, :, :], turns[:, :, :], MAGIC, None, ALU.subtract))
            src = ang
            for part in (PI2_A, PI2_B, PI2_C):
                link(nc.vector.scalar_tensor_tensor(out=red[:, :, :], in0=turns[:, :, :], scalar=-part,
                                                    in1=src[:, :, :], op0=ALU.mult, op1=ALU.add))
                src = red
            nc.vector.tensor_scalar(red[:, 0, :], red[:, 0, :], fc[:, 3:4], None, ALU.add)
            link(nc.vector.tensor_scalar(red[:, 2, :], red[:, 2, :], float(np.pi / 2), None, ALU.add))
            nc.vector.tensor_scalar(red[:, :, :], red[:, :, :], 3.1415925, -3.1415925, ALU.min,
                                    ALU.max).then_inc(enc_ok, 1)
            g = {x: k[x][:, :, :] for x in ("gA0", "gB0", "gB1", "gB2", "gU", "gW")}
            link(nc.vector.tensor_scalar(g["gB2"], g["gB2"], 0.5, None, ALU.mult))
            nc.vector.tensor_tensor(g["gU"], g["gB1"], gA1[:, :, :], ALU.subtract)
            link(nc.vector.tensor_tensor(g["gW"], g["gB1"], gA1[:, :, :], ALU.add))
            nc.vector.tensor_scalar(g["gU"], g["gU"], 0.5, None, ALU.mult)
            nc.vector.tensor_scalar(g["gW"], g["gW"], 0.5, None, ALU.mult)
            for m, grid in enumerate((g["gB2"], g["gA0"], gA1[:, :, :], g["gB1"])):
                ins = nc.vector.tensor_copy(edg[:, m, :, :].rearrange("p c (e j) -> p c e j", e=2),
                                            window(grid, 0, [[D, 2], [D - 4, 2], [1, 4]]))
            link(ins)
            for m in range(4):
                ins = nc.vector.tensor_tensor(edg[:, m], edg[:, m],
                                              window(ecoef[:, m, :], 0, [[0, 2], [1, 8]]), ALU.mult)
            link(ins)
            nc.vector.tensor_tensor(k["edge1"][:, :, :], edg[:, 0], edg[:, 1], ALU.add)
            nc.vector.tensor_tensor(k["edge3"][:, :, :], edg[:, 2], edg[:, 3], ALU.add)
            dve.wait_ge(cond_zero, 1)
            dve.wait_ge(h2_mm, 1)
            for m in range(4):
                nc.vector.tensor_scalar(h2[:, m, :], ps[1][:, m * B:(m + 1) * B], cb2[:, m:m + 1], None,
                                        ALU.add).then_inc(h2_ok, 1)
            dve.wait_ge(cond_mm, 1)
            for m in range(8):
                one = 1.0 if C_ONESC <= m < C_SHIFT3 else 0.0
                nc.vector.tensor_scalar(cond[:, :, m], ps[2][:, m * B:(m + 1) * B], cb[:, m:m + 1], one,
                                        ALU.add, ALU.add)
            nc.vector.tensor_copy(cond[:, :, C_DT], dt_row[:, :])
            nc.vector.tensor_copy(cond[0:A, :, C_EB], ps[3][0:A, 0:B])
            for c in range(8):
                dve.wait_ge(sel_mm, c + 1)
                nc.vector.tensor_copy(sel[:, c * 512:(c + 1) * 512], ps[4 + c % 4][0:B, :]).then_inc(sel_ok, 1)

        @block.tensor
        def _(pe):
            pe.wait_ge(c_loaded, N_C * 16)
            pe.wait_ge(sin_ok, 1)
            for m in range(4):
                ins = pe.matmul(ps[0][:, m * B:(m + 1) * B], cW1[:, m * P:(m + 1) * P], sn[:, 0, :],
                                start=True, stop=True)
            ins.then_inc(h1_mm, 1)
            pe.wait_ge(h1_ok, 4)
            for m in range(4):
                for c in range(4):
                    ins = pe.matmul(ps[1][:, m * B:(m + 1) * B], cW2[:, c, m * P:(m + 1) * P], h1[:, c, :],
                                    start=(c == 0), stop=(c == 3))
            ins.then_inc(h2_mm, 1)
            pe.wait_ge(h2_ok, 4)
            pe.wait_ge(se_ok, 1)
            for m in range(8):
                w, x, kk, col = ((cWsc, h2, 4, m), (cWsh, h2, 4, m - 2), (cWada, se, 2, m - 4))[
                    0 if m < 2 else 1 if m < 4 else 2]
                for c in range(kk):
                    ins = pe.matmul(ps[2][:, m * B:(m + 1) * B], w[:, c, col * P:(col + 1) * P], x[:, c, :],
                                    start=(c == 0), stop=(c == kk - 1))
            pe.wait_ge(id_ok, 1)
            pe.matmul(ps[3][0:A, 0:B], ebt[:, :], one_v[:, :], start=True, stop=False)
            pe.matmul(ps[3][0:A, 0:B], demb[:, :], one_c[0:E, :], start=False, stop=True).then_inc(cond_mm, 1)
            for c in range(8):
                if c >= 4:
                    pe.wait_ge(sel_ok, c - 3)
                pe.matmul(ps[4 + c % 4][0:B, :], one_v[:, :], etab[:, c * 512:(c + 1) * 512],
                          start=True, stop=True).then_inc(sel_mm, 1)


_DIRECT = ['x', 'condB_dt', 'itok_B_0_15', 'condB_t', 'itok_B_34_63', 'fside_Bx16xSxS_0', 'mask_Bx1xSxS_bk0',
           'L0_cond_A_grid', 'L0_cond_B_grid', 'L1_cond_down_b', 'L1_cond_up_b', 'L1_cond_expert_b',
           'L1_cond_domain_emb', 'L1_cond_ln_gamma', 'L1_cond_ln_beta', 'L2_cond_W1', 'L2_cond_b1',
           'L2_cond_W2', 'L2_cond_b2', 'L2_cond_Wsc', 'L2_cond_bsc', 'L2_cond_Wsh', 'L2_cond_bsh',
           'L2_cond_W_in', 'L2_cond_b_in', 'L2_cond_W_out', 'L2_cond_b_out', 'L3_cond_W_ada', 'L3_cond_b_ada',
           'L3_cond_Wq', 'L3_cond_bq', 'L3_cond_Wk', 'L3_cond_bk', 'L3_cond_Wv', 'L3_cond_bv', 'L3_cond_Wo',
           'L3_cond_bo', 'L3_cond_W1', 'L3_cond_b1', 'L3_cond_W2', 'L3_cond_b2', 'L3_cond_g2', 'L3_cond_beta2']


_COLUMNS = ['L2_cond_b1', 'L2_cond_b2', 'L2_cond_bsc', 'L2_cond_bsh', 'L3_cond_b_ada', 'L2_cond_b_in', 'L3_cond_bq',
            'L3_cond_bk', 'L3_cond_g2', 'L3_cond_beta2', 'L3_cond_b1']


def _shape_constants():
    grad, lap = np.zeros((S, S), np.float32), np.zeros((S, S), np.float32)
    for r in range(1, S - 1):
        grad[r, r - 1], grad[r, r + 1] = -0.5, 0.5
        lap[r, r - 1:r + 2] = 0.5, -1.0, 0.5
    grad[0, 0:3], grad[S - 1, S - 3:] = (-1.5, 2.0, -0.5), (0.5, -2.0, 1.5)
    lap[0, 0:4], lap[S - 1, S - 4:] = (1.0, -2.5, 2.0, -0.5), (-0.5, 2.0, -2.5, 1.0)
    cols = np.zeros((P, 4), np.float32)

    def freqs(half):
        step = np.float32(-np.log(10000.0) / (half - 1))
        return np.exp(np.arange(half, dtype=np.float32) * step).astype(np.float32)

    cols[:, 0] = np.tile(freqs(P // 2), 2)
    cols[:, 1] = freqs(P)
    cols[P // 2:, 2] = 0.25
    cols[P // 2:, 3] = np.pi / 2
    edge = np.array([[-3, 4, -1, 0, 0, 1, -4, 3], [-1, 0, 0, 0, 0, 0, 0, -1],
                     [1.5, -2, 0.5, 0, 0, -0.5, 2, -1.5], [1, -2.5, 2, -0.5, -0.5, 2, -2.5, 1]], np.float32)
    return {"gradT": np.ascontiguousarray(grad.T), "lapT": np.ascontiguousarray(lap.T), "enc_cols": cols,
            "row_number": np.arange(EROW + 1, dtype=np.float32).reshape(-1, 1), "edge_coef": edge.reshape(-1),
            "eye64": np.eye(A, dtype=np.float32).reshape(1, -1)}


def kernel(**inputs):
    import numpy as _np
    import concourse.bacc as _bacc
    from concourse import mybir as _mybir
    from concourse.bass_utils import run_bass_kernel_spmd as _run

    nc = _bacc.Bacc("TRN2", target_bir_lowering=False, num_devices=1)
    data = {n: _np.ascontiguousarray(inputs[n]) for n in _DIRECT}
    data["downT"] = _np.ascontiguousarray(_np.asarray(inputs["L1_cond_down_W"]).T)
    data["upT"] = _np.ascontiguousarray(_np.asarray(inputs["L1_cond_up_W"]).T)
    data["expertT"] = _np.ascontiguousarray(
        _np.asarray(inputs["L1_cond_expert_W"]).transpose(0, 2, 1)).reshape(E, A * A)
    data["gammaT"] = _np.ascontiguousarray(_np.asarray(inputs["L2_cond_gamma"]).T)
    data["betaT"] = _np.ascontiguousarray(_np.asarray(inputs["L2_cond_beta"]).T)
    for n in _COLUMNS:
        data[n] = _np.ascontiguousarray(data[n].reshape(-1, P).T)
    data.update(_shape_constants())
    arrays, aps = {}, {}
    for name, a in data.items():
        arrays[f"in_{name}_dram"] = a
        aps[name] = nc.dram_tensor(f"in_{name}_dram", a.shape, _mybir.dt.from_np(a.dtype), kind="ExternalInput").ap()
    out = nc.dram_tensor("out_0_dram", (B, S, D), _mybir.dt.float32, kind="ExternalOutput").ap()
    adapter_to_attention_kernel(nc, aps, out)
    r = _run(nc, [arrays], core_ids=[0])
    return r.results[0]["out_0_dram"]
```

```python
from contextlib import ExitStack

import numpy as np

import concourse.bass as bass
from concourse import mybir

ALU = mybir.AluOpType
ACT = mybir.ActivationFunctionType
AXX = mybir.AxisListType.X
F32 = mybir.dt.float32
BF16 = mybir.dt.bfloat16
I32 = mybir.dt.int32
U8 = mybir.dt.uint8

P = 128
B, S, D = 16, 256, 256
PAIRS = B // 2
H, DH = 16, 16
A, E = 64, 16
EROW = 32
FF = 1024
FB = FF // P
C4 = 512
NC = 10
EPS = 1e-5
NEG = -1.0e30
BIG = 3.0e38
VW = DH + 1
CH = 2
NCH = 2 * H // CH
RING = 4
LEAD = 1
HEADS = 2 * H
Q_PART = [2, 1, 0, 1, 0, 0]
K_PART = [0, 1, 2, 0, 1, 0]
Q_PLACE = [2 - part for part in Q_PART]
STACK_RUNS = [(0, 3), (3, 2), (5, 1)]
STACK = len(Q_PART) * DH
MAGIC = 12582912.0
PI2_A = 6.28125
PI2_B = float(np.float32(np.round((2 * np.pi - PI2_A) * 2.0**21) / 2.0**21))
PI2_C = float(2 * np.pi - PI2_A - PI2_B)
(C_SCALE, C_SHIFT, C_ONESC, C_SHIFT3, C_DT, C_EB) = (0, 2, 4, 6, 8, 9)
LINKS = {"front": 64, "heads": 4, "back": 4, "pool": 8, "pool_back": 2}

LAG_T, LAG_V = 2, 3
SLOTS = HEADS
AT = {"ctx": (4, 5), "wo": (6, 8), "x5": (6, 8), "hn": (7, 11), "hn_turn": (10, 11), "hold": 12,
      "w1": (12, 13, 14, 15, 16, 17, 21, 22), "w2": (23, 24, 24, 25, 29, 33, 33, 34), "out": (27, 35),
      "prods": (1, 1), "diffs": (1, 2), "edges": (1, 4), "l0": (2, 4), "x1": (4, 5), "x1_turn": (5, 6),
      "down": (7, 7), "expert": (8, 8), "up": (8, 9), "xs": (9, 10), "x2": (11, 11), "stat0": (11, 11),
      "avg0": (12, 12), "nmr0": (16, 18), "x2_turn": (17, 18), "aff0": (19, 19), "w_in": (20, 21),
      "z": (20, 21), "avg1": (21, 22), "nmr1": (22, 23), "zn": (22, 23), "aff1": (24, 24),
      "w_out": (24, 24), "x3": (24, 25), "xn3": (26, 28), "x3_turn": (26, 30), "q": (28, 31),
      "k": (28, 31), "v": (29, 31), "mask": 31}
GROUP = 8
GROUPS = HEADS // GROUP
PR = 2
SIG = 1.702


def wait_alone(eng, sem, value):
    eng.wait_ge(sem, value)
    eng.nop(nofuse=True)


def window(ap, offset, dims):
    first = list(ap.ap[0])
    return bass.AP(ap.tensor, ap.offset + offset, [first] + [list(d) for d in dims])


def adapter_to_attention_kernel(nc, i, out):
    with ExitStack() as keep:
        def sb(name, shape, dt=F32):
            return keep.enter_context(nc.sbuf_tensor(name, shape, dt))

        def sem(name):
            return keep.enter_context(nc.semaphore(name))

        ident = sb("ident", [P, P])
        mean_mat = sb("mean_mat", [P, P])
        half_neg = sb("half_neg", [P, 4])
        gradT = sb("gradT", [P, 2, S])
        lapT = sb("lapT", [P, 2, S])
        gA0, gB0, gB1, gB2, gU, gW = (sb(n, [P, 2, D]) for n in ("gA0", "gB0", "gB1", "gB2h", "gU", "gW"))
        edge1 = sb("edge1", [P, 2, 8])
        edge3 = sb("edge3", [P, 2, 8])
        downT = sb("downT", [P, 2, A])
        down_b = sb("down_b", [A, 1])
        upT = sb("upT", [A, D])
        gammaT = sb("gammaT", [P, 2, S])
        betaT = sb("betaT", [P, 2, S])
        w_in = sb("w_in", [P, 2, D])
        w_out = sb("w_out", [P, 2, D])
        wq, wk, wv, wo = (sb(n, [P, 2, D]) for n in ("wq", "wk", "wv", "wo"))
        w1 = sb("w1", [P, 2, FF])
        w2 = sb("w2", [P, FB, D])
        b_in, bq, bk, g2, beta2 = (sb(n, [P, 2]) for n in ("b_in", "bq", "bk", "g2", "beta2"))
        b1 = sb("b1", [P, FB])
        b1s = sb("b1s", [P, FB])
        up_b, ln_g, ln_b, b_out, bv, bo, b2 = (
            sb(n, [P, D]) for n in ("up_b", "ln_g", "ln_b", "b_out", "bv", "bo", "b2"))
        cond = sb("cond", [P, B, NC])
        sel_dram = nc.dram_tensor("sel_dram", [B, A, A], F32, kind="Internal").ap()
        part_dram = nc.dram_tensor("part_dram", [2, 2, 3, D, S], BF16, kind="Internal").ap()

        w_loaded = sem("w_loaded")
        scaled = sem("scaled")
        ones_set = sem("ones_set")

        WEIGHT_LOADS = [
            (gradT, "gradT"), (lapT, "lapT"), (downT, "downT"), (w_in, "L2_cond_W_in"),
            (w_out, "L2_cond_W_out"), (wq, "L3_cond_Wq"), (wk, "L3_cond_Wk"), (wv, "L3_cond_Wv"),
            (wo, "L3_cond_Wo"), (w1, "L3_cond_W1"), (w2, "L3_cond_W2"), (gammaT, "gammaT"),
            (betaT, "betaT"),
        ]
        COLUMN_LOADS = [(b_in, "L2_cond_b_in"), (bk, "L3_cond_bk"), (g2, "L3_cond_g2"),
                        (beta2, "L3_cond_beta2"), (b1, "L3_cond_b1")]
        ROW_LOADS = [(up_b, "L1_cond_up_b"), (ln_g, "L1_cond_ln_gamma"), (ln_b, "L1_cond_ln_beta"),
                     (b_out, "L2_cond_b_out"), (bv, "L3_cond_bv"), (bo, "L3_cond_bo"),
                     (b2, "L3_cond_b2")]
        N_LOADS = len(WEIGHT_LOADS) + len(COLUMN_LOADS) + len(ROW_LOADS) + 3

        setup(nc, i, locals())

        F = sb("F", [P, 4, D])
        bufs = sb("front", [P, 9, 4, D])
        p_a0, p_b0, p_b1, p_b2, p_u, p_w, X1, X3, x1 = (bufs[:, n] for n in range(9))

        def as_feature(t):
            return t[:, :, :].rearrange("p (c b) s -> p c (b s)", c=2)

        x1T = as_feature(p_a0)
        hidT = p_b0[0:A, 0:2, :].rearrange("p b s -> p (b s)")
        expT = p_b0[0:A, 2:4, :].rearrange("p b s -> p (b s)")
        res1 = p_b1
        xs = p_b2
        x2 = p_u
        x2T = as_feature(p_a0)
        yT = as_feature(p_w)
        zT = as_feature(X1)
        x2b = X3
        x3 = x1
        xn3 = p_b1
        qkf = [as_feature(p_a0), as_feature(p_b0)]
        rest = [as_feature(p_b2), as_feature(p_u)]
        part_room = bufs[:, 5:8].rearrange("p n t s -> p (n t s)").bitcast(BF16)
        parts = [part_room[:, w * 12 * D:(w + 1) * 12 * D].rearrange("p (j n) -> p j n", j=3) for w in range(2)]
        V_next = x1
        ew = sb("ew", [A, 2, A])
        cp = sb("cp", [P, 2, NC])
        qs = sb("q_stack", [P, H * 2 * S], BF16)
        ks = sb("k_stack", [P, H * 2 * S], BF16)
        stacks = [t[0:STACK, :].rearrange("p (h n) -> p h n", h=H) for t in (qs, ks)]
        ffT = sb("ffT", [P, FB, 2 * S])
        x4T_hold = sb("x4T_hold", [P, 2, 2 * S])
        x4T = sb("x4T", [P, 2, 2 * S])
        V = sb("V", [P, 4, H, VW])
        bias = sb("bias", [P, RING, CH * 2, S])
        mask_raw = sb("mask_raw", [P, 4, S], U8)
        mask_add = sb("mask_add", [P, 4, S], BF16)
        Sn = sb("Sn", [P, 2, 2, S])
        nmax = sb("nmax", [P, HEADS, 2])
        Pr = sb("Pr", [P, PR, 2, S])
        PT = sb("PT", [P, 2, 2, S])
        rsum = sb("rsum", [P, GROUPS, 2, GROUP])
        tanh = sb("tanh", [P, 2 * S])
        ctxn = sb("ctxn", [P, 4, D])
        ctxT = sb("ctxT", [P, 2, 2 * S])
        x5 = sb("x5", [P, 4, D])
        x5b = x5
        hn = ffT[:, 0:2, :].rearrange("p a (b n) -> p (a b) n", b=2)
        stats = sb("stats", [P, 4, 6])
        mv = sb("mv", [P, 4, 2])
        ms = sb("ms", [P, 2, 2])
        gs = sb("gs", [P, 2, 2])
        var = sb("var", [P, 2, 2])
        rstd = sb("rstd", [P, 2, 2])
        nmr = sb("nmr", [P, 2])
        back_stats, back_mv, back_var, back_rstd = (
            sb(n, [P, 4, m]) for n, m in (("back_stats", 6), ("back_mv", 2), ("back_var", 1), ("back_rstd", 1)))
        edge_f = sb("edge_f", [P, 4, 8])
        edge_p = sb("edge_p", [P, 2, 4, 8])

        G, SP_, TP = (keep.enter_context(nc.psum_tensor(n, [P, 2, 512], F32))
                      for n in ("G", "scores_ps", "PT_ps"))
        CP, FP = (keep.enter_context(nc.psum_tensor(n, [P, 512], F32)) for n in ("ctx_ps", "ff_ps"))
        CG = CP[:, 0:2 * GROUP * VW].rearrange("p (q h w) -> p q h w", q=2, h=GROUP)
        Gt = G[:, :, :].rearrange("p c (t n) -> p (c t) n", t=2)
        GF = [G[:, b, :].rearrange("p (c s) -> p c s", c=2) for b in range(2)]
        Ft = FP[:, :].rearrange("p (t n) -> p t n", t=2)

        f_loaded, cond_loaded, ew_loaded, mask_loaded = (
            sem(n) for n in ("f_loaded", "cond_loaded", "ew_loaded", "mask_loaded"))
        bias_loaded = [sem(f"bias_loaded{n}") for n in range(RING)]
        prods = sem("prods")
        l0_in, l0_mm, x1_pre, x1_ok, x1_tr, x1T_ok = (
            sem(n) for n in ("l0_in", "l0_mm", "x1_pre", "x1_ok", "x1_tr", "x1T_ok"))
        down_mm, hid_ok, exp_mm, expT_ok, up_mm, res1_ok = (
            sem(n) for n in ("down_mm", "hid_ok", "exp_mm", "expT_ok", "up_mm", "res1_ok"))
        x2_ok, x2_tr, win_mm, x2b_ok, wout_mm, xn3_ok, x3_tr, x4T_ok, V_ok = (
            sem(n) for n in ("x2_ok", "x2_tr", "win_mm", "x2b_ok", "wout_mm", "xn3_ok", "x3_tr", "x4T_ok", "V_ok"))
        qkv_mm = [sem(f"{n}_mm") for n in "qkv"]
        qk_ok = [sem(f"{n}_ok") for n in "qk"]
        split_ok = [sem(f"{n}_split") for n in "qk"]
        mstat_ok, mstat_mm, mstat_read, norm_ok, xnT_ok, affine_ok, y_ok = (
            sem(n) for n in ("mstat_ok", "mstat_mm", "mstat_read", "norm_ok", "xnT_ok", "affine_ok", "y_ok"))
        var_ok, rstd_ok = sem("var_ok"), sem("rstd_ok")
        back_var_ok, back_rstd_ok = sem("back_var_ok"), sem("back_rstd_ok")
        V_moved, held = sem("V_moved"), sem("held")
        part_written = [sem(f"part_written{b}") for b in range(2)]
        stack_loaded = [sem(f"stack_loaded{b}") for b in range(2)]
        mask_ok, masked = sem("mask_ok"), sem("masked")
        score_mm, biased, prob_ok, pt_tr, pt_ok, pv_mm, ctx_ok = (
            sem(n) for n in ("score_mm", "biased", "prob_ok", "pt_tr", "pt_ok", "pv_mm", "ctx_ok"))
        ctx_tr, ctxT_ok, wo_mm, x5_ok, hn_ok, hn_tr, hT_ok = (
            sem(n) for n in ("ctx_tr", "ctxT_ok", "wo_mm", "x5_ok", "hn_ok", "hn_tr", "hT_ok"))
        x5b_ok, w1_mm, tanh_ok, ff_ok, w2_mm, out_ok, stored = (
            sem(n) for n in ("x5b_ok", "w1_mm", "tanh_ok", "ff_ok", "w2_mm", "out_ok", "stored"))
        done = {n: sem(f"{n}_links") for n in LINKS}

        x_in = i["x"].rearrange("(i b) (c p) y -> i p (b c) y", b=2, p=P)
        x_out = out.rearrange("(i b) (c p) y -> i p (b c) y", b=2, p=P)
        mask_in = i["mask_Bx1xSxS_bk0"].rearrange("(i b) o (c p) k -> i p (b o c) k", b=2, p=P)
        side_in = i["fside_Bx16xSxS_0"].rearrange("(i b) h (c p) k -> i p (b h c) k", b=2, p=P)
        sel_in = sel_dram.rearrange("(i b) a o -> i a b o", b=2)
        cond_in = cond[:, :, :].rearrange("p (i b) n -> p i (b n)", b=2)
        part_out = part_dram.rearrange("w b j (c p) n -> w b p j c n", p=P)
        part_in = part_dram.rearrange("w b j (d h) n -> w b (j d) h n", h=H)

        def bc(ap, n):
            return window(ap, 0, [[0, n], list(ap.ap[1])])

        block = keep.enter_context(nc.Block())

        def run(eng, begin, head, front, back):
            def whole_turn(j, with_back, with_front, with_late):
                begin(j)
                for n in range(SLOTS):
                    head(j, n, with_back)
                    if with_late:
                        back(j - 2, n + SLOTS)
                    if with_back:
                        back(j - 1, n)
                    if with_front:
                        front(j + 1, n)

            front(0, None)
            whole_turn(0, False, True, False)
            whole_turn(1, True, True, False)
            with eng.Fori(2, PAIRS - 1) as j:
                whole_turn(j, True, True, True)
            whole_turn(PAIRS - 1, True, False, True)
            for n in range(HEADS, HEADS + LAG_V + 1):
                head(PAIRS - 1, n, True)
            for n in range(SLOTS):
                back(PAIRS - 2, n + SLOTS)
            back(PAIRS - 1, None)

        def seqs(step, n):
            return [b for b in range(2) if n is None or AT[step][b] == n]

        def later(j):
            return not isinstance(j, int) or j > 0

        def lagged(j, n, lag, with_back):
            if n >= lag:
                return (j, n - lag) if n - lag < HEADS else None
            return (j - 1, n - lag + HEADS) if with_back else None

        class Links:

            def __init__(self, eng, name, j, n=0):
                self.eng, self.name, self.j, self.n = eng, name, j, n

            def __call__(self, ins, alone=False):
                self.n += 1
                ins.then_inc(done[self.name], 1)
                value = self.j * LINKS[self.name] + self.n
                if alone:
                    wait_alone(self.eng, done[self.name], value)
                else:
                    self.eng.wait_ge(done[self.name], value)

            def end(self):
                assert self.n == LINKS[self.name], (self.name, self.n)

        @block.sync
        def _(sp):
            def load_front(j):
                sp.dma_start(F[:, :, :], x_in[j]).then_inc(f_loaded, 16)

            def load_small(j):
                sp.dma_start(cp[:, :, :].rearrange("p b n -> p (b n)"), cond_in[:, j, :]).then_inc(cond_loaded, 16)
                sp.dma_start(ew[:, :, :], sel_in[j]).then_inc(ew_loaded, 16)
                sp.dma_start(mask_raw[:, :, :], mask_in[j]).then_inc(mask_loaded, 16)

            def load_stacks(j, b):
                wait_alone(sp, part_written[b], (j + 1) * 32)
                for w, order in enumerate((Q_PLACE, K_PART)):
                    for s, count in STACK_RUNS:
                        src = part_in[w, b, order[s] * DH:(order[s] + count) * DH]
                        sp.dma_start(stacks[w][s * DH:(s + count) * DH, :, b * S:(b + 1) * S], src
                                     ).then_inc(stack_loaded[b], 16)

            def turn(j, first, last):
                for c in range(NCH):
                    if c == (2 if first else 0) and not last:
                        wait_alone(sp, x1_pre, LEAD + 2 * j + 2)
                        load_front(j + 1)
                    if c == RING and not last:
                        wait_alone(sp, x4T_ok, LEAD + 2 * j + 2)
                        sp.wait_ge(mask_ok, LEAD + j + 1)
                        load_small(j + 1)
                    if not first or c >= RING:
                        sp.wait_ge(biased, LEAD + j * (2 * HEADS) + 2 * CH * (c - RING + 1))
                    if c == RING - 1:
                        if not first:
                            wait_alone(sp, score_mm, j * HEADS - H)
                        load_stacks(j, 0)
                    sp.dma_start(bias[:, c % RING, :, :],
                                 side_in[j, :, 2 * CH * c:2 * CH * (c + 1), :]).then_inc(bias_loaded[c % RING], 16)
                    if c == RING - 1:
                        if not first:
                            wait_alone(sp, score_mm, j * HEADS)
                        load_stacks(j, 1)

            load_front(0)
            load_small(0)
            turn(0, True, False)
            with sp.Fori(1, PAIRS - 1) as j:
                turn(j, False, False)
            turn(PAIRS - 1, False, True)

        @block.gpsimd
        def _(pool):
            links = {}

            def add_mask(j, c):
                b = c * CH // H
                pool.wait_ge(bias_loaded[c % RING], (j * (NCH // RING) + c // RING + 1) * 16)
                t = bias[:, c % RING, :, :].rearrange("p (h q) k -> p h (q k)", h=CH)
                m = mask_add[:, 2 * b:2 * b + 2, :].rearrange("p q k -> p (q k)")
                nc.gpsimd.tensor_tensor(t, t, bc(m, CH), ALU.add).then_inc(masked, 1)

            def next_mask(j):
                pool.wait_ge(mask_loaded, (j + 1) * 16)
                pool.wait_ge(masked, LEAD + j * NCH)
                pool.nop(nofuse=True)
                nc.gpsimd.tensor_scalar(mask_add[:, :, :], mask_raw[:, :, :], NEG, None, ALU.mult).then_inc(mask_ok, 1)
                pool.wait_ge(mask_ok, LEAD + j + 1)
                add_mask(j, 0)

            def inv_std(link, v, r, v_ok, r_ok, count):
                wait_alone(pool, v_ok, count)
                link(nc.gpsimd.tensor_scalar(r, v, EPS, None, ALU.add))
                nc.gpsimd.tensor_tensor(r, r, half_neg[:, 0:r.shape[1]], ALU.pow).then_inc(r_ok, 1)

            def front(j, n):
                if n is None or n == 0:
                    links["f"] = Links(pool, "pool", j)
                link = links["f"]

                def inv(b, m, k):
                    inv_std(link, var[:, b, 0:m], rstd[:, b, 0:m], var_ok, rstd_ok, 8 * j + 2 * k + b + 1)
                for b in seqs("prods", n):
                    pool.wait_ge(f_loaded, (j + 1) * 16)
                    if later(j):
                        pool.wait_ge(V_ok, 2 * j)
                    for dst, grid in ((p_a0, gA0), (p_b1, gB1)):
                        nc.gpsimd.tensor_tensor(dst[:, 2 * b:2 * b + 2, :], F[:, 2 * b:2 * b + 2, :], grid[:, :, :],
                                                ALU.mult).then_inc(prods, 1)
                for b in seqs("down", n):
                    pool.wait_ge(x1_ok, 2 * j + b + 1)
                    nc.gpsimd.tensor_tensor(res1[:, 2 * b:2 * b + 2, :], x1[:, 2 * b:2 * b + 2, :], bc(up_b[:, :], 2),
                                            ALU.add).then_inc(res1_ok, 1)
                for b in seqs("xs", n):
                    inv(b, 2, 0)
                for b in seqs("avg0", n):
                    inv(b, 1, 1)
                for b in seqs("aff0", n):
                    pool.wait_ge(x2_ok, 2 * j + b + 1)
                    nc.gpsimd.tensor_tensor(x2b[:, 2 * b:2 * b + 2, :], x2[:, 2 * b:2 * b + 2, :], bc(b_out[:, :], 2),
                                            ALU.add).then_inc(x2b_ok, 1)
                for b in seqs("avg1", n):
                    inv(b, 1, 2)
                for b in seqs("x3", n):
                    inv(b, 2, 3)
                if n is None or n == SLOTS - 1:
                    link.end()

            def back(j, n):
                for b in seqs("x5", n):
                    link = Links(pool, "pool_back", j, b)
                    inv_std(link, back_var[:, 2 * b:2 * b + 2, 0], back_rstd[:, 2 * b:2 * b + 2, 0], back_var_ok,
                            back_rstd_ok, 2 * j + b + 1)
                for b in seqs("hn_turn", n):
                    pool.wait_ge(hn_ok, 2 * j + b + 1)
                    half = slice(2 * b, 2 * b + 2)
                    nc.gpsimd.tensor_tensor(x5b[:, half, :], x5[:, half, :], bc(b2[:, :], 2), ALU.add).then_inc(x5b_ok, 1)

            def head(j, n, with_back):
                if n < HEADS and n % CH == 1 and n // CH + 2 < NCH:
                    add_mask(j, n // CH + 2)
                ahead = n < HEADS and not (isinstance(j, int) and j == PAIRS - 1)
                if ahead and n == AT["mask"]:
                    next_mask(j + 1)
                if ahead and n == SLOTS - 1:
                    add_mask(j + 1, 1)

            nc.gpsimd.memset(V[:, :, :, DH:VW], 1.0).then_inc(ones_set, 1)
            for s in (mask_ok, masked):
                pool.sem_inc(s, LEAD)
            next_mask(0)
            add_mask(0, 1)
            run(pool, lambda j: None, head, front, back)

        @block.vector
        def _(dve):
            links = {}

            def row_stats(link, src, st, m, v, v_ok):
                tiles = src.shape[1]
                for t in range(tiles):
                    ins = nc.vector.bn_stats(out=st[:, t, :], in_=src[:, t, :])
                link(ins, alone=True)
                for t in range(tiles):
                    ins = nc.vector.bn_aggr(out=m[:, t, :], in_=st[:, t, :])
                link(ins)
                nc.vector.tensor_copy(v, m[:, :, 1]).then_inc(v_ok, 1)

            def row_norm(dst, src, m, r):
                for t in range(src.shape[1]):
                    ins = nc.vector.tensor_scalar(dst[:, t, :], src[:, t, :], m[:, t, 0:1], r[:, t:t + 1],
                                                  ALU.subtract, ALU.mult)
                return ins

            def whole_stats(link, b, x):
                for c in range(2):
                    ins = nc.vector.bn_stats(out=stats[:, 2 * b + c, :], in_=x[:, c, :])
                link(ins, alone=True)
                link(nc.vector.bn_aggr(out=mv[:, 2 * b, :],
                                       in_=stats[:, 2 * b:2 * b + 2, :].rearrange("p c n -> p (c n)")))
                mean, square = ms[:, b, 0:1], ms[:, b, 1:2]
                nc.vector.tensor_copy(mean, mv[:, 2 * b, 0:1])
                link(nc.vector.tensor_tensor(square, mv[:, 2 * b, 0:1], mv[:, 2 * b, 0:1], ALU.mult))
                nc.vector.tensor_tensor(square, square, mv[:, 2 * b, 1:2], ALU.add).then_inc(mstat_ok, 1)

            def whole_var(link, b, count):
                dve.wait_ge(mstat_mm, count)
                nc.vector.tensor_copy(gs[:, b, :], G[:, b, 0:2]).then_inc(mstat_read, 1)
                dve.wait_ge(mstat_read, count)
                link(nc.vector.tensor_tensor(nmr[:, b:b + 1], gs[:, b, 0:1], gs[:, b, 0:1], ALU.mult))
                nc.vector.tensor_tensor(var[:, b, 0:1], gs[:, b, 1:2], nmr[:, b:b + 1], ALU.subtract).then_inc(var_ok, 1)

            def whole_nmr(link, j, b, k):
                dve.wait_ge(rstd_ok, 8 * j + 2 * (k + 1) + b + 1)
                link(nc.vector.tensor_tensor(nmr[:, b:b + 1], gs[:, b, 0:1], rstd[:, b, 0:1], ALU.mult))
                nc.vector.tensor_scalar(nmr[:, b:b + 1], nmr[:, b:b + 1], -1.0, None, ALU.mult).then_inc(norm_ok, 1)

            def affine(link, t, b, count):
                dve.wait_ge(xnT_ok, count)
                v = t[:, :, b * S:(b + 1) * S]
                link(nc.vector.tensor_tensor(v, v, gammaT[:, :, :], ALU.mult))
                nc.vector.tensor_tensor(v, v, betaT[:, :, :], ALU.add).then_inc(affine_ok, 1)

            inner, left, right = slice(1, D - 1), slice(0, D - 2), slice(2, D)

            def front(j, n):
                if n is None or n == 0:
                    links["f"] = Links(dve, "front", j)
                link = links["f"]
                for b in seqs("prods", n):
                    mine = slice(2 * b, 2 * b + 2)
                    dve.wait_ge(f_loaded, (j + 1) * 16)
                    if later(j):
                        for w in range(2):
                            dve.wait_ge(part_written[w], j * 32)
                    for dst, grid in ((p_b0, gB0), (p_b2, gB2), (p_u, gU), (p_w, gW)):
                        ins = nc.vector.tensor_tensor(dst[:, mine, :], F[:, mine, :], grid[:, :, :], ALU.mult)
                    link(ins)
                for b in seqs("diffs", n):
                    mine = slice(2 * b, 2 * b + 2)
                    nc.vector.tensor_tensor(X1[:, mine, inner], p_b2[:, mine, right], p_b2[:, mine, left], ALU.subtract)
                    link(nc.vector.tensor_tensor(X3[:, mine, inner], p_u[:, mine, right], p_w[:, mine, left], ALU.add))
                    dve.wait_ge(prods, 2 * (2 * j + b) + 2)
                    nc.vector.tensor_tensor(X1[:, mine, inner], X1[:, mine, inner], p_a0[:, mine, inner], ALU.subtract)
                    nc.vector.tensor_tensor(X3[:, mine, inner], X3[:, mine, inner], p_b1[:, mine, inner], ALU.subtract)
                for b in seqs("edges", n):
                    mine = slice(2 * b, 2 * b + 2)
                    link(nc.vector.tensor_copy(edge_f[:, mine, :].rearrange("p t (e j) -> p t e j", e=2),
                                               window(F[:, mine, :], 0, [[D, 2], [D - 4, 2], [1, 4]])))
                    for m, e in enumerate((edge1, edge3)):
                        ins = nc.vector.tensor_tensor(edge_p[:, m, mine, :], edge_f[:, mine, :], e[:, :, :], ALU.mult)
                    link(ins)
                    for m, x in enumerate((X1, X3)):
                        ins = nc.vector.tensor_reduce(window(x[:, mine, :], 0, [[D, 2], [D - 1, 2]]),
                                                      edge_p[:, m, mine, :].rearrange("p t (e j) -> p t e j", e=2),
                                                      AXX, ALU.add)
                    ins.then_inc(l0_in, 1)
                for b in seqs("x1", n):
                    mine = slice(2 * b, 2 * b + 2)
                    dve.wait_ge(l0_in, 2 * j + b + 1)
                    dve.wait_ge(l0_mm, 2 * j + b + 1)
                    link(nc.vector.tensor_tensor(X3[:, mine, :], X3[:, mine, :], GF[b], ALU.add))
                    dve.wait_ge(cond_loaded, (j + 1) * 16)
                    nc.vector.scalar_tensor_tensor(out=x1[:, mine, :], in0=X3[:, mine, :],
                                                   scalar=cp[:, b, C_DT:C_DT + 1], in1=F[:, mine, :],
                                                   op0=ALU.mult, op1=ALU.add).then_inc(x1_pre, 1)
                for b in seqs("xs", n):
                    mine = slice(2 * b, 2 * b + 2)
                    dve.wait_ge(up_mm, 2 * j + b + 1)
                    dve.wait_ge(res1_ok, 2 * j + b + 1)
                    link(nc.vector.tensor_tensor(xs[:, mine, :], GF[b], res1[:, mine, :], ALU.add))
                    row_stats(link, xs[:, mine, :], stats[:, mine, :], mv[:, mine, :], var[:, b, :], var_ok)
                for b in seqs("x2", n):
                    mine = slice(2 * b, 2 * b + 2)
                    dve.wait_ge(rstd_ok, 8 * j + b + 1)
                    link(row_norm(xs[:, mine, :], xs[:, mine, :], mv[:, mine, :], rstd[:, b, :]))
                    link(nc.vector.tensor_tensor(x2[:, mine, :], xs[:, mine, :], bc(ln_g[:, :], 2), ALU.mult))
                    nc.vector.tensor_tensor(x2[:, mine, :], x2[:, mine, :], bc(ln_b[:, :], 2), ALU.add).then_inc(x2_ok, 1)
                for b in seqs("stat0", n):
                    dve.wait_ge(x2_ok, 2 * j + b + 1)
                    whole_stats(link, b, x2[:, 2 * b:2 * b + 2, :])
                for k in range(2):
                    if k == 1:
                        for b in seqs("z", n):
                            dve.wait_ge(win_mm, 2 * j + b + 1)
                            z = zT[:, :, b * S:(b + 1) * S]
                            for c in range(2):
                                ins = nc.vector.tensor_scalar(z[:, c, :], GF[b][:, c, :], b_in[:, c:c + 1], None, ALU.add)
                            link(ins)
                            whole_stats(link, b, z)
                    for b in seqs(("avg0", "avg1")[k], n):
                        whole_var(link, b, 4 * j + 2 * k + b + 1)
                    for b in seqs(("nmr0", "nmr1")[k], n):
                        whole_nmr(link, j, b, k)
                    for b in seqs(("aff0", "aff1")[k], n):
                        affine(link, (x2T, zT)[k], b, 4 * j + 2 * k + b + 1)
                for b in seqs("x3", n):
                    mine = slice(2 * b, 2 * b + 2)
                    dve.wait_ge(wout_mm, 2 * j + b + 1)
                    dve.wait_ge(x2b_ok, 2 * j + b + 1)
                    link(nc.vector.tensor_tensor(x3[:, mine, :], GF[b], x2b[:, mine, :], ALU.add))
                    row_stats(link, x3[:, mine, :], stats[:, mine, :], mv[:, mine, :], var[:, b, :], var_ok)
                for b in seqs("xn3", n):
                    mine = slice(2 * b, 2 * b + 2)
                    dve.wait_ge(rstd_ok, 8 * j + 6 + b + 1)
                    row_norm(xn3[:, mine, :], x3[:, mine, :], mv[:, mine, :], rstd[:, b, :]).then_inc(xn3_ok, 1)
                for w in range(2):
                    for b in seqs("qk"[w], n):
                        dve.wait_ge(qk_ok[w], 2 * j + b + 1)
                        x, r = (t[:, :, b * S:(b + 1) * S] for t in (qkf[w], rest[w]))
                        pt = parts[w][:, :, :].rearrange("p j (c n) -> p j c n", c=2)[:, :, :, b * S:(b + 1) * S]
                        high, low = (2, 0) if w == 0 else (0, 2)
                        link(nc.vector.tensor_copy(pt[:, high], x))
                        link(nc.vector.tensor_tensor(r, x, pt[:, high], ALU.subtract))
                        link(nc.vector.tensor_copy(pt[:, 1], r))
                        nc.vector.tensor_tensor(pt[:, low], r, pt[:, 1], ALU.subtract).then_inc(split_ok[w], 1)
                for b in seqs("v", n):
                    dve.wait_ge(qkv_mm[2], 2 * j + b + 1)
                    nc.vector.tensor_tensor(V_next[:, 2 * b:2 * b + 2, :], GF[b], bc(bv[:, :], 2), ALU.add).then_inc(V_ok, 1)
                if n is None or n == SLOTS - 1:
                    link.end()

            def back(j, n):
                for b in seqs("x5", n):
                    half = slice(2 * b, 2 * b + 2)
                    link = Links(dve, "back", j, 2 * b)
                    dve.wait_ge(wo_mm, LEAD + 2 * j + b + 1)
                    dve.wait_ge(stored, LEAD + 16 * j)
                    nc.vector.tensor_tensor(x5[:, half, :], Ft, bc(bo[:, :], 2), ALU.add).then_inc(x5_ok, 1)
                    dve.wait_ge(x5_ok, 2 * j + b + 1)
                    row_stats(link, x5[:, half, :], back_stats[:, half, :], back_mv[:, half, :],
                              back_var[:, half, 0], back_var_ok)
                for b in seqs("hn", n):
                    half = slice(2 * b, 2 * b + 2)
                    dve.wait_ge(back_rstd_ok, 2 * j + b + 1)
                    row_norm(hn[:, half, :], x5[:, half, :], back_mv[:, half, :],
                             back_rstd[:, half, 0]).then_inc(hn_ok, 1)
                for f in range(FB):
                    if n is None or AT["w1"][f] == n:
                        dve.wait_ge(tanh_ok, j * FB + f + 1)
                        nc.vector.scalar_tensor_tensor(out=ffT[:, f, :], in0=tanh[:, :], scalar=1.0,
                                                       in1=ffT[:, f, :], op0=ALU.add, op1=ALU.mult).then_inc(ff_ok, 1)
                for m in range(2):
                    if n is None or AT["out"][m] == n:
                        dve.wait_ge(w2_mm, 2 * j + m + 1)
                        dve.wait_ge(x5b_ok, 2 * j + m + 1)
                        half = x5b[:, 2 * m:2 * m + 2, :]
                        nc.vector.tensor_tensor(half, Ft, half, ALU.add).then_inc(out_ok, 1)

            def bias_and_max(j, n):
                c = n // CH
                dve.wait_ge(masked, LEAD + j * NCH + c + 1)
                dve.wait_ge(score_mm, j * HEADS + n + 1)
                dve.wait_ge(prob_ok, LEAD + j * HEADS + max(n - 1, 0))
                dve.nop(nofuse=True)
                for q in range(2):
                    nc.vector.tensor_tensor_reduce(
                        out=Sn[:, n % 2, q, :], in0=SP_[:, n % 2, q * S:(q + 1) * S],
                        in1=bias[:, c % RING, 2 * (n % CH) + q, :], scale=-1.0, scalar=BIG,
                        op0=ALU.add, op1=ALU.min, accum_out=nmax[:, n, q:q + 1]).then_inc(biased, 1)

            def finish_ctx(link, j, g):
                b, first = divmod(g * GROUP, H)
                dve.wait_ge(pv_mm, LEAD + j * HEADS + GROUP * (g + 1))
                if g == 0:
                    dve.wait_ge(ctx_tr, LEAD + 2 * j)
                link(nc.vector.reciprocal(rsum[:, g, :, :], CG[:, :, :, DH]))
                for q in range(2):
                    ins = nc.vector.tensor_tensor(
                        ctxn[:, 2 * b + q, first * DH:(first + GROUP) * DH].rearrange("p (h d) -> p h d", h=GROUP),
                        CG[:, q, :, 0:DH], window(rsum[:, g, q, :], 0, [[1, GROUP], [0, DH]]), ALU.mult)
                ins.then_inc(ctx_ok, 1)

            def move_v(j, b):
                dve.wait_ge(V_ok, 2 * j + b + 1)
                dve.wait_ge(pv_mm, LEAD + j * HEADS + (0 if b or isinstance(j, int) and j == 0 else -H))
                nc.vector.tensor_copy(V[:, 2 * b:2 * b + 2, :, 0:DH],
                                      V_next[:, 2 * b:2 * b + 2, :].rearrange("p t (h d) -> p t h d", h=H)
                                      ).then_inc(V_moved, 1)

            def begin(j):
                links["h"] = Links(dve, "heads", j)

            def head(j, n, with_back):
                if n % GROUP == LAG_V and (n > LAG_V or with_back):
                    if n > LAG_V and n < HEADS:
                        finish_ctx(links["h"], j, n // GROUP - 1)
                    else:
                        pair = j if n > HEADS else j - 1
                        link = Links(dve, "heads", pair, GROUPS - 1)
                        finish_ctx(link, pair, GROUPS - 1)
                        link.end()
                if n >= HEADS:
                    return
                bias_and_max(j, n)
                if n == 1:
                    move_v(j, 0)
                if n == LAG_V:
                    move_v(j, 1)
                if n == AT["hold"]:
                    dve.wait_ge(x4T_ok, LEAD + 2 * j + 2)
                    dve.wait_ge(wo_mm, LEAD + 2 * j)
                    nc.vector.tensor_copy(x4T_hold[:, :, :], x4T[:, :, :]).then_inc(held, 1)

            for s in (x1_pre, biased, ctx_ok, out_ok):
                dve.sem_inc(s, LEAD)
            dve.wait_ge(ones_set, 1)
            run(dve, begin, head, front, back)

        @block.scalar
        def _(act):
            def evac(dst, src, done_sem, scale=1.0, b=0.0):
                ins = nc.scalar.activation(dst, src, ACT.Identity, bias=b, scale=scale)
                if done_sem is not None:
                    ins.then_inc(done_sem, 1)

            def front(j, n):
                for b in seqs("x1", n):
                    act.wait_ge(x1_pre, LEAD + 2 * j + b + 1)
                    nc.scalar.activation(x1[:, 2 * b:2 * b + 2, :], x1[:, 2 * b:2 * b + 2, :], ACT.Relu).then_inc(x1_ok, 1)
                for b in seqs("x1_turn", n):
                    act.wait_ge(x1_tr, 2 * j + b + 1)
                    evac(x1T[:, :, b * S:(b + 1) * S], GF[b], x1T_ok)
                for b in seqs("down", n):
                    act.wait_ge(down_mm, 2 * j + b + 1)
                    nc.scalar.activation(hidT[:, b * S:(b + 1) * S], GF[b][0:A, 0, :], ACT.Gelu,
                                         bias=down_b[:, 0:1]).then_inc(hid_ok, 1)
                for b in seqs("expert", n):
                    act.wait_ge(exp_mm, 2 * j + b + 1)
                    evac(expT[:, b * S:(b + 1) * S], GF[b][0:A, 1, :], expT_ok, b=cp[0:A, b, C_EB:C_EB + 1])
                for k in range(2):
                    for b in seqs(("x2_turn", "zn")[k], n):
                        if k == 0:
                            act.wait_ge(x2_tr, 2 * j + b + 1)
                        act.wait_ge(norm_ok, 4 * j + 2 * k + b + 1)
                        dst = (x2T, zT)[k][:, :, b * S:(b + 1) * S]
                        evac(dst, GF[b] if k == 0 else dst, xnT_ok, scale=rstd[:, b, 0:1], b=nmr[:, b:b + 1])
                    for b in seqs(("aff0", "aff1")[k], n):
                        act.wait_ge(affine_ok, 4 * j + 2 * k + b + 1)
                        src = (x2T, zT)[k]
                        for c in range(2):
                            ins = nc.scalar.activation(
                                yT[:, c, b * S:(b + 1) * S], src[:, c, b * S:(b + 1) * S], ACT.Silu,
                                bias=cp[:, b, C_SHIFT + c:C_SHIFT + c + 1],
                                scale=cp[:, b, C_SCALE + c:C_SCALE + c + 1])
                        ins.then_inc(y_ok, 1)
                for b in seqs("x3_turn", n):
                    act.wait_ge(x3_tr, 2 * j + b + 1)
                    if later(j):
                        act.wait_ge(held, j)
                    for c in range(2):
                        evac(x4T[:, c, b * S:(b + 1) * S], GF[b][:, c, :], x4T_ok if c else None,
                             scale=cp[:, b, C_ONESC + c:C_ONESC + c + 1], b=cp[:, b, C_SHIFT3 + c:C_SHIFT3 + c + 1])
                for w in range(2):
                    for b in seqs("qk"[w], n):
                        act.wait_ge(qkv_mm[w], 2 * j + b + 1)
                        for c in range(2):
                            evac(qkf[w][:, c, b * S:(b + 1) * S], GF[b][:, c, :], qk_ok[w] if c else None,
                                 scale=(DH ** -0.5, 1.0)[w], b=(bq, bk)[w][:, c:c + 1])
                for w in range(2):
                    for b in seqs("kv"[w], n):
                        act.wait_ge(split_ok[w], 2 * j + b + 1)
                        act.dma_start(part_out[w, b],
                                      parts[w][:, :, :].rearrange("p j (c n) -> p j c n", c=2)[:, :, :, b * S:(b + 1) * S]
                                      ).then_inc(part_written[b], 16)
            def back(j, n):
                for b in seqs("ctx", n):
                    act.wait_ge(ctx_tr, LEAD + 2 * j + b + 1)
                    evac(ctxT[:, :, b * S:(b + 1) * S], Ft, ctxT_ok)
                for b in seqs("hn_turn", n):
                    act.wait_ge(hn_tr, 2 * j + b + 1)
                    for c in range(2):
                        evac(ctxT[:, c, b * S:(b + 1) * S], Ft[:, c, :], hT_ok if c else None, scale=g2[:, c:c + 1],
                             b=beta2[:, c:c + 1])
                for f in range(FB):
                    if n is None or AT["w1"][f] == n:
                        act.wait_ge(w1_mm, j * FB + f + 1)
                        if f > 0:
                            act.wait_ge(ff_ok, j * FB + f)
                        nc.scalar.activation(tanh[:, :], FP[:, :], ACT.Tanh, bias=b1s[:, f:f + 1], scale=SIG / 2)
                        nc.scalar.activation(ffT[:, f, :], FP[:, :], ACT.Identity,
                                             bias=b1[:, f:f + 1]).then_inc(tanh_ok, 1)
                if n is None or AT["out"][1] == n:
                    act.wait_ge(out_ok, LEAD + 2 * j + 2)
                    act.dma_start(x_out[j], x5b[:, :, :]).then_inc(stored, 16)

            def head(j, n, with_back):
                if n < HEADS:
                    if with_back or n >= PR:
                        act.wait_ge(pt_tr, LEAD + j * HEADS + n - PR + 1)
                    for q in range(2):
                        act.wait_ge(biased, LEAD + j * 2 * HEADS + 2 * n + q + 1)
                        ins = nc.scalar.activation(Pr[:, n % PR, q, :], Sn[:, n % 2, q, :], ACT.Exp,
                                                   bias=nmax[:, n, q:q + 1], scale=-1.0)
                    ins.then_inc(prob_ok, 1)
                copy_pt(lagged(j, n, LAG_T, with_back))

            def copy_pt(which):
                if which is None:
                    return
                j, m = which
                act.wait_ge(pt_tr, LEAD + j * HEADS + m + 1)
                act.wait_ge(pv_mm, LEAD + j * HEADS + max(m - 1, 0))
                nc.scalar.activation(PT[:, m % 2, :, :].rearrange("p c q -> p (c q)"),
                                     TP[:, m % 2, :], ACT.Identity).then_inc(pt_ok, 1)

            for s in (x4T_ok, prob_ok, pt_ok, stored):
                act.sem_inc(s, LEAD)
            act.wait_ge(scaled, 3)
            run(act, lambda j: None, head, front, back)
            act.wait_ge(stored, LEAD + 16 * PAIRS)

        @block.tensor
        def _(pe):
            def turned(dst, src, b):
                for t in range(2):
                    for c in range(2):
                        ins = pe.transpose(dst[:, c, t * P:(t + 1) * P], src[:, 2 * b + t, c * P:(c + 1) * P],
                                           ident[:, :])
                return ins

            def by_feature(w, xT, b):
                for m in range(2):
                    for c in range(2):
                        ins = pe.matmul(GF[b][:, m, :], w[:, c, m * P:(m + 1) * P], xT[:, c, b * S:(b + 1) * S],
                                        start=(c == 0), stop=(c == 1))
                return ins

            def by_token(w, xT, b):
                for t in range(2):
                    for c in range(2):
                        ins = pe.matmul(GF[b][:, t, :], xT[:, c, b * S + t * P:b * S + (t + 1) * P], w[:, c, :],
                                        start=(c == 0), stop=(c == 1))
                return ins

            def front(j, n):
                for b in seqs("l0", n):
                    pe.wait_ge(l0_in, 2 * j + b + 1)
                    if later(j):
                        pe.wait_ge(V_ok, 2 * j)
                    for m in range(2):
                        for s, (mat, x) in enumerate(((gradT, X1), (lapT, p_b0))):
                            for c in range(2):
                                ins = pe.matmul(GF[b][:, m, :], mat[:, c, m * P:(m + 1) * P], x[:, 2 * b + c, :],
                                                start=(s == 0 and c == 0), stop=(s == 1 and c == 1))
                    ins.then_inc(l0_mm, 1)
                for b in seqs("x1_turn", n):
                    pe.wait_ge(x1_ok, 2 * j + b + 1)
                    turned(GF[b], x1, b).then_inc(x1_tr, 1)
                for b in seqs("down", n):
                    pe.wait_ge(x1T_ok, 2 * j + b + 1)
                    for c in range(2):
                        ins = pe.matmul(GF[b][0:A, 0, :], downT[:, c, :], x1T[:, c, b * S:(b + 1) * S],
                                        start=(c == 0), stop=(c == 1))
                    ins.then_inc(down_mm, 1)
                for b in seqs("expert", n):
                    pe.wait_ge(hid_ok, 2 * j + b + 1)
                    wait_alone(pe, ew_loaded, (j + 1) * 16)
                    pe.matmul(GF[b][0:A, 1, :], ew[:, b, :], hidT[:, b * S:(b + 1) * S],
                              start=True, stop=True).then_inc(exp_mm, 1)
                for b in seqs("up", n):
                    pe.wait_ge(expT_ok, 2 * j + b + 1)
                    for t in range(2):
                        ins = pe.matmul(GF[b][:, t, :], expT[:, b * S + t * P:b * S + (t + 1) * P], upT[:, :],
                                        start=True, stop=True)
                    ins.then_inc(up_mm, 1)
                for k in range(2):
                    for b in seqs(("avg0", "avg1")[k], n):
                        pe.wait_ge(mstat_ok, 4 * j + 2 * k + b + 1)
                        pe.matmul(G[:, b, 0:2], mean_mat[:, :], ms[:, b, :], start=True, stop=True).then_inc(mstat_mm, 1)
                    if k == 0:
                        for b in seqs("x2_turn", n):
                            pe.wait_ge(mstat_read, 4 * j + b + 1)
                            turned(GF[b], x2, b).then_inc(x2_tr, 1)
                        for b in seqs("w_in", n):
                            pe.wait_ge(y_ok, 4 * j + b + 1)
                            by_feature(w_in, yT, b).then_inc(win_mm, 1)
                for b in seqs("w_out", n):
                    pe.wait_ge(mstat_read, 4 * j + 2 + b + 1)
                    pe.wait_ge(y_ok, 4 * j + 2 + b + 1)
                    by_token(w_out, yT, b).then_inc(wout_mm, 1)
                for b in seqs("x3_turn", n):
                    pe.wait_ge(xn3_ok, 2 * j + b + 1)
                    turned(GF[b], xn3, b).then_inc(x3_tr, 1)
                for b in seqs("q", n):
                    pe.wait_ge(x4T_ok, LEAD + 2 * j + b + 1)
                    by_feature(wq, x4T, b).then_inc(qkv_mm[0], 1)
                for b in seqs("k", n):
                    pe.wait_ge(qk_ok[0], 2 * j + b + 1)
                    by_feature(wk, x4T, b).then_inc(qkv_mm[1], 1)
                for b in seqs("v", n):
                    pe.wait_ge(qk_ok[1], 2 * j + b + 1)
                    by_token(wv, x4T, b).then_inc(qkv_mm[2], 1)

            def back(j, n):
                for b in seqs("ctx", n):
                    pe.wait_ge(ctx_ok, LEAD + GROUPS * j + GROUPS // 2 * (b + 1))
                    if b == 0:
                        pe.wait_ge(out_ok, LEAD + 2 * j)
                    else:
                        pe.wait_ge(ctxT_ok, 2 * j + 1)
                    turned(Ft, ctxn, b).then_inc(ctx_tr, 1)
                for b in seqs("wo", n):
                    pe.wait_ge(ctxT_ok, 2 * j + 2)
                    pe.wait_ge(held, j + 1)
                    if b == 1:
                        pe.wait_ge(x5_ok, 2 * j + 1)
                    for t in range(2 * b, 2 * b + 2):
                        for c in range(2):
                            pe.matmul(Ft[:, t % 2, :], ctxT[:, c, t * P:(t + 1) * P], wo[:, c, :],
                                      start=(c == 0), stop=False)
                        for c in range(2):
                            ins = pe.matmul(Ft[:, t % 2, c * P:(c + 1) * P], x4T_hold[:, c, t * P:(t + 1) * P],
                                            ident[:, :], start=False, stop=(c == 1))
                    ins.then_inc(wo_mm, 1)
                for b in seqs("hn_turn", n):
                    pe.wait_ge(hn_ok, 2 * j + b + 1)
                    if b == 0:
                        pe.wait_ge(x5_ok, 2 * j + 2)
                    else:
                        pe.wait_ge(hT_ok, 2 * j + 1)
                    turned(Ft, hn, b).then_inc(hn_tr, 1)
                for f in range(FB):
                    if n is None or AT["w1"][f] == n:
                        pe.wait_ge(hT_ok, 2 * j + 2)
                        if f > 0:
                            pe.wait_ge(tanh_ok, j * FB + f)
                        for c in range(2):
                            ins = pe.matmul(FP[:, :], w1[:, c, f * P:(f + 1) * P], ctxT[:, c, :],
                                            start=(c == 0), stop=(c == 1))
                        ins.then_inc(w1_mm, 1)
                for piece in range(8):
                    if n is None or AT["w2"][piece] == n:
                        t, part = divmod(piece, 2)
                        if piece == 0:
                            pe.wait_ge(ff_ok, (j + 1) * FB)
                        if piece == 4:
                            pe.wait_ge(out_ok, LEAD + 2 * j + 1)
                        for f in range(part * FB // 2, (part + 1) * FB // 2):
                            ins = pe.matmul(Ft[:, t % 2, :], ffT[:, f, t * P:(t + 1) * P], w2[:, f, :],
                                            start=(f == 0), stop=(f == FB - 1))
                        if piece % 4 == 3:
                            ins.then_inc(w2_mm, 1)

            def scores(j, h):
                b, hh = divmod(h, H)
                pe.wait_ge(biased, LEAD + j * 2 * HEADS + 2 * max(h - 1, 0))
                for q in range(2):
                    ins = pe.matmul(SP_[:, h % 2, q * S:(q + 1) * S],
                                    stacks[0][:, hh, b * S + q * P:b * S + (q + 1) * P],
                                    stacks[1][:, hh, b * S:(b + 1) * S], start=True, stop=True)
                ins.then_inc(score_mm, 1)

            def turn_p(which):
                if which is None:
                    return
                j, m = which
                pe.wait_ge(prob_ok, LEAD + j * HEADS + m + 1)
                pe.wait_ge(pt_ok, LEAD + j * HEADS + max(m - 1, 0))
                for q in range(2):
                    for c in range(2):
                        ins = pe.transpose(TP[:, m % 2, c * S + q * P:c * S + (q + 1) * P],
                                           Pr[:, m % PR, q, c * P:(c + 1) * P], ident[:, :])
                ins.then_inc(pt_tr, 1)

            def times_v(which):
                if which is None:
                    return
                j, m = which
                b, h = divmod(m, H)
                g, hg = divmod(m, GROUP)
                if hg == 0:
                    pe.wait_ge(ctx_ok, LEAD + j * GROUPS + g)
                if h == 0:
                    pe.wait_ge(V_moved, 2 * j + b + 1)
                pe.wait_ge(pt_ok, LEAD + j * HEADS + m + 1)
                for q in range(2):
                    for c in range(2):
                        ins = pe.matmul(CG[:, q, hg, :],
                                        PT[:, m % 2, c, q * P:(q + 1) * P], V[:, 2 * b + c, h, :],
                                        start=(c == 0), stop=(c == 1))
                ins.then_inc(pv_mm, 1)

            def head(j, n, with_back):
                if n in (0, H):
                    pe.wait_ge(stack_loaded[n // H], (j + 1) * 16 * 2 * len(STACK_RUNS))
                if n < HEADS:
                    scores(j, n)
                turn_p(lagged(j, n, LAG_T, with_back))
                times_v(lagged(j, n, LAG_V, with_back))

            for s in (pv_mm, pt_tr, wo_mm, ctx_tr):
                pe.sem_inc(s, LEAD)
            pe.wait_ge(w_loaded, N_LOADS * 16)
            pe.wait_ge(scaled, 3)
            run(pe, lambda j: None, head, front, back)


def setup(nc, i, k):
    with ExitStack() as ctx:
        def sb(name, shape, dt=F32):
            return ctx.enter_context(nc.sbuf_tensor(name, shape, dt))

        def sem(name):
            return ctx.enter_context(nc.semaphore(name))

        ident, mean_mat, half_neg, cond, sel_dram = (k[n] for n in ("ident", "mean_mat", "half_neg", "cond", "sel_dram"))
        w_loaded = k["w_loaded"]

        cW1 = sb("cW1", [P, C4])
        cW2 = sb("cW2", [P, 4, C4])
        cWsc, cWsh = sb("cWsc", [P, 4, D]), sb("cWsh", [P, 4, D])
        cWada = sb("cWada", [P, 2, 2 * D])
        cb1, cb2 = sb("cb1", [P, 4]), sb("cb2", [P, 4])
        cb = sb("cb", [P, 8])
        gA1 = sb("gA1", [P, 2, D])
        fc = sb("fc", [P, 4])
        rown = sb("rown", [EROW + 1, 1])
        ecoef = sb("ecoef", [P, 4, 8])
        tb = sb("tb", [P, B])
        t3i = sb("t3i", [P, B], I32)
        t3 = sb("t3", [P, B])
        dt_row = sb("dt_row", [P, B])
        idi = sb("idi", [EROW + 1, B], I32)
        idf, idc, one_c, one_v, ok = (sb(n, [EROW + 1, B]) for n in ("idf", "idc", "one_c", "one_v", "ok"))
        etab = sb("etab", [EROW + 1, A * A])
        ebt = sb("ebt", [EROW + 1, A])
        demb = sb("demb", [E, A])
        sel = sb("sel", [B, A * A])
        ang, turns, red, sn = (sb(n, [P, 3, B]) for n in ("ang", "turns", "red", "sn"))
        se = sb("se", [P, 2, B])
        h1, h2 = sb("h1", [P, 4, B]), sb("h2", [P, 4, B])
        edg = sb("edg", [P, 4, 2, 8])
        edt = sb("edt", [P, 2, 2, 8])
        ps = [ctx.enter_context(nc.psum_tensor(f"setup_ps{n}", [P, 512], F32)) for n in range(8)]

        tab_zero, c_loaded, small, id_ok, enc_ok, sin_ok, se_ok = (
            sem(n) for n in ("tab_zero", "c_loaded", "small", "id_ok", "enc_ok", "sin_ok", "se_ok"))
        h1_mm, h1_ok, h2_mm, h2_ok, cond_mm, sel_mm, sel_ok, sel_stored, chain, idn, acts = (
            sem(n) for n in ("h1_mm", "h1_ok", "h2_mm", "h2_ok", "cond_mm", "sel_mm", "sel_ok", "sel_stored", "chain", "idn", "acts"))
        cond_zero, a_loaded = sem("cond_zero"), sem("a_loaded")

        block = ctx.enter_context(nc.Block())

        def cols(name):
            return i[name]

        def mat(name):
            return i[name].rearrange("(c p) n -> p c n", p=P)

        A_LOADS = [(rown[:, :], i["row_number"]), (idi[:, :], i["itok_B_0_15"].partition_broadcast(EROW + 1)),
                   (demb[:, :], i["L1_cond_domain_emb"])]
        N_A = len(A_LOADS) + 3
        C_LOADS = [
            (fc[:, :], i["enc_cols"]),
            (tb[:, :], i["condB_t"].partition_broadcast(P)),
            (t3i[:, :], i["itok_B_34_63"].partition_broadcast(P)),
            (cW1[:, :], i["L2_cond_W1"]), (cW2[:, :, :], mat("L2_cond_W2")),
            (cWsc[:, :, :], mat("L2_cond_Wsc")), (cWsh[:, :, :], mat("L2_cond_Wsh")),
            (cWada[:, :, :], mat("L3_cond_W_ada")),
            (cb1[:, :], cols("L2_cond_b1")), (cb2[:, :], cols("L2_cond_b2")),
            (cb[:, 0:2], cols("L2_cond_bsc")), (cb[:, 2:4], cols("L2_cond_bsh")),
            (cb[:, 4:8], cols("L3_cond_b_ada")),
            (ecoef[:, :, :].rearrange("p a b -> p (a b)"), i["edge_coef"].partition_broadcast(P)),
            (dt_row[:, :], i["condB_dt"].partition_broadcast(P)),
            (gA1[:, :, :], i["L0_cond_A_grid"][1].rearrange("(c p) y -> p c y", p=P)),
        ] + [(k[n][:, :, :], i[g][j].rearrange("(c p) y -> p c y", p=P)) for n, g, j in (
            ("gA0", "L0_cond_A_grid", 0), ("gB0", "L0_cond_B_grid", 0), ("gB1", "L0_cond_B_grid", 1),
            ("gB2", "L0_cond_B_grid", 2))]
        N_C = len(C_LOADS)

        @block.sync
        def _(sp):
            for dst, src in A_LOADS:
                sp.dma_start(dst, src).then_inc(a_loaded, 16)
            sp.wait_ge(tab_zero, 2)
            sp.dma_start(etab[0:E, :], i["expertT"]).then_inc(a_loaded, 16)
            sp.dma_start(etab[EROW:EROW + 1, :], i["eye64"]).then_inc(a_loaded, 16)
            sp.dma_start(ebt[0:E, :], i["L1_cond_expert_b"]).then_inc(a_loaded, 16)
            for dst, src in C_LOADS:
                sp.dma_start(dst, src).then_inc(c_loaded, 16)
            sp.wait_ge(sel_ok, 8)
            sp.dma_start(sel_dram.rearrange("b a o -> b (a o)"), sel[:, :]).then_inc(sel_stored, 16)
            sp.wait_ge(sel_stored, 16)

        @block.gpsimd
        def _(pool):
            nc.gpsimd.memset(etab[:, :], 0.0).then_inc(tab_zero, 1)
            nc.gpsimd.memset(ebt[:, :], 0.0).then_inc(tab_zero, 1)
            nc.gpsimd.memset(cond[:, :, :], 0.0).then_inc(cond_zero, 1)
            nc.gpsimd.memset(half_neg[:, :], -0.5).then_inc(tab_zero, 1)
            nc.gpsimd.memset(mean_mat[:, :], 1.0 / P)
            nc.gpsimd.memset(ident[:, :], 0.0).then_inc(idn, 1)
            pool.wait_ge(idn, 1)
            nc.gpsimd.affine_select(out=ident[:, :], in_=ident[:, :], compare_op=ALU.not_equal, fill=1.0,
                                    base=0, pattern=[[-1, P]], channel_multiplier=1).then_inc(idn, 1)

        @block.scalar
        def _(act):
            for dst, name in k["WEIGHT_LOADS"]:
                act.dma_start(dst[:, :, :], mat(name)).then_inc(w_loaded, 16)
            for dst, name in k["COLUMN_LOADS"] + [(k["bq"], "L3_cond_bq")]:
                act.dma_start(dst[:, :], cols(name)).then_inc(w_loaded, 16)
            act.dma_start(k["upT"][:, :], i["upT"]).then_inc(w_loaded, 16)
            for dst, name in k["ROW_LOADS"]:
                act.dma_start(dst[:, :], i[name].partition_broadcast(P)).then_inc(w_loaded, 16)
            act.dma_start(k["down_b"][:, :], i["L1_cond_down_b"].rearrange("(a o) -> a o", o=1)).then_inc(w_loaded, 16)
            act.wait_ge(enc_ok, 1)
            nc.scalar.activation(sn[:, :, :], red[:, :, :], ACT.Sin).then_inc(sin_ok, 1)
            act.wait_ge(sin_ok, 1)
            nc.scalar.activation(se[:, :, :], sn[:, 1:3, :], ACT.Silu).then_inc(se_ok, 1)
            act.wait_ge(h1_mm, 1)
            for m in range(4):
                nc.scalar.activation(h1[:, m, :], ps[0][:, m * B:(m + 1) * B], ACT.Silu,
                                     bias=cb1[:, m:m + 1]).then_inc(h1_ok, 1)
            act.wait_ge(w_loaded, k["N_LOADS"] * 16)
            nc.scalar.mul(k["bq"][:, :], k["bq"][:, :], DH ** -0.5).then_inc(k["scaled"], 1)
            nc.scalar.mul(k["b1s"][:, :], k["b1"][:, :], SIG / 2).then_inc(k["scaled"], 1)
            nc.scalar.mul(k["w2"][:, :, :], k["w2"][:, :, :], 0.5).then_inc(k["scaled"], 1)
            act.wait_ge(k["scaled"], 3)

        @block.vector
        def _(dve):
            n = [0]

            def link(ins):
                n[0] += 1
                ins.then_inc(chain, 1)
                dve.wait_ge(chain, n[0])

            dve.wait_ge(a_loaded, N_A * 16)
            link(nc.vector.tensor_copy(idf[:, :], idi[:, :]))
            link(nc.vector.tensor_scalar(idc[:, :], idf[:, :], 0.0, float(E - 1), ALU.max, ALU.min))
            nc.vector.tensor_scalar(one_c[:, :], idc[:, :], rown[:, 0:1], None, ALU.is_equal)
            link(nc.vector.tensor_tensor(ok[:, :], idf[:, :], idc[:, :], ALU.is_equal))
            link(nc.vector.tensor_scalar(one_v[:, :], idf[:, :], rown[:, 0:1], None, ALU.is_equal))
            nc.vector.tensor_scalar(one_v[EROW:EROW + 1, :], ok[EROW:EROW + 1, :], -1.0, 1.0, ALU.mult,
                                    ALU.add).then_inc(id_ok, 1)
            for c in range(8):
                dve.wait_ge(sel_mm, c + 1)
                nc.vector.tensor_copy(sel[:, c * 512:(c + 1) * 512], ps[4 + c % 4][0:B, :]).then_inc(sel_ok, 1)
            dve.wait_ge(c_loaded, N_C * 16)
            link(nc.vector.tensor_copy(t3[:, :], t3i[:, :]))
            nc.vector.tensor_scalar(ang[:, 0, :], tb[:, :], 5000.0, fc[:, 0:1], ALU.mult, ALU.mult)
            link(nc.vector.tensor_scalar(t3[:, :], t3[:, :], 0.01, 4000.0, ALU.mult, ALU.mult))
            for j in (1, 2):
                ins = nc.vector.tensor_scalar(ang[:, j, :], t3[:, :], fc[:, 1:2], None, ALU.mult)
            link(ins)
            inv = float(1 / (2 * np.pi))
            nc.vector.tensor_scalar(turns[:, 0, :], ang[:, 0, :], inv, fc[:, 2:3], ALU.mult, ALU.add)
            nc.vector.tensor_scalar(turns[:, 1, :], ang[:, 1, :], inv, None, ALU.mult)
            link(nc.vector.tensor_scalar(turns[:, 2, :], ang[:, 2, :], inv, 0.25, ALU.mult, ALU.add))
            link(nc.vector.tensor_scalar(turns[:, :, :], turns[:, :, :], MAGIC, None, ALU.add))
            link(nc.vector.tensor_scalar(turns[:, :, :], turns[:, :, :], MAGIC, None, ALU.subtract))
            src = ang
            for part in (PI2_A, PI2_B, PI2_C):
                link(nc.vector.scalar_tensor_tensor(out=red[:, :, :], in0=turns[:, :, :], scalar=-part,
                                                    in1=src[:, :, :], op0=ALU.mult, op1=ALU.add))
                src = red
            nc.vector.tensor_scalar(red[:, 0, :], red[:, 0, :], fc[:, 3:4], None, ALU.add)
            link(nc.vector.tensor_scalar(red[:, 2, :], red[:, 2, :], float(np.pi / 2), None, ALU.add))
            nc.vector.tensor_scalar(red[:, :, :], red[:, :, :], 3.1415925, -3.1415925, ALU.min,
                                    ALU.max).then_inc(enc_ok, 1)
            g = {x: k[x][:, :, :] for x in ("gA0", "gB0", "gB1", "gB2", "gU", "gW")}
            link(nc.vector.tensor_scalar(g["gB2"], g["gB2"], 0.5, None, ALU.mult))
            nc.vector.tensor_tensor(g["gU"], g["gB1"], gA1[:, :, :], ALU.subtract)
            link(nc.vector.tensor_tensor(g["gW"], g["gB1"], gA1[:, :, :], ALU.add))
            nc.vector.tensor_scalar(g["gU"], g["gU"], 0.5, None, ALU.mult)
            nc.vector.tensor_scalar(g["gW"], g["gW"], 0.5, None, ALU.mult)
            for m, grid in enumerate((g["gB2"], g["gA0"], gA1[:, :, :], g["gB1"])):
                ins = nc.vector.tensor_copy(edg[:, m, :, :].rearrange("p c (e j) -> p c e j", e=2),
                                            window(grid, 0, [[D, 2], [D - 4, 2], [1, 4]]))
            link(ins)
            for m in range(4):
                ins = nc.vector.tensor_tensor(edg[:, m], edg[:, m],
                                              window(ecoef[:, m, :], 0, [[0, 2], [1, 8]]), ALU.mult)
            link(ins)
            nc.vector.tensor_tensor(k["edge1"][:, :, :], edg[:, 0], edg[:, 1], ALU.add)
            nc.vector.tensor_tensor(k["edge3"][:, :, :], edg[:, 2], edg[:, 3], ALU.add)
            dve.wait_ge(cond_zero, 1)
            dve.wait_ge(h2_mm, 1)
            for m in range(4):
                nc.vector.tensor_scalar(h2[:, m, :], ps[1][:, m * B:(m + 1) * B], cb2[:, m:m + 1], None,
                                        ALU.add).then_inc(h2_ok, 1)
            dve.wait_ge(cond_mm, 1)
            for m in range(8):
                one = 1.0 if C_ONESC <= m < C_SHIFT3 else 0.0
                nc.vector.tensor_scalar(cond[:, :, m], ps[2][:, m * B:(m + 1) * B], cb[:, m:m + 1], one,
                                        ALU.add, ALU.add)
            nc.vector.tensor_copy(cond[:, :, C_DT], dt_row[:, :])
            nc.vector.tensor_copy(cond[0:A, :, C_EB], ps[3][0:A, 0:B])

        @block.tensor
        def _(pe):
            pe.wait_ge(a_loaded, N_A * 16)
            pe.wait_ge(id_ok, 1)
            for c in range(8):
                if c >= 4:
                    pe.wait_ge(sel_ok, c - 3)
                pe.matmul(ps[4 + c % 4][0:B, :], one_v[:, :], etab[:, c * 512:(c + 1) * 512],
                          start=True, stop=True).then_inc(sel_mm, 1)
            pe.wait_ge(c_loaded, N_C * 16)
            pe.wait_ge(sin_ok, 1)
            for m in range(4):
                ins = pe.matmul(ps[0][:, m * B:(m + 1) * B], cW1[:, m * P:(m + 1) * P], sn[:, 0, :],
                                start=True, stop=True)
            ins.then_inc(h1_mm, 1)
            pe.wait_ge(h1_ok, 4)
            for m in range(4):
                for c in range(4):
                    ins = pe.matmul(ps[1][:, m * B:(m + 1) * B], cW2[:, c, m * P:(m + 1) * P], h1[:, c, :],
                                    start=(c == 0), stop=(c == 3))
            ins.then_inc(h2_mm, 1)
            pe.wait_ge(h2_ok, 4)
            pe.wait_ge(se_ok, 1)
            for m in range(8):
                w, x, kk, col = ((cWsc, h2, 4, m), (cWsh, h2, 4, m - 2), (cWada, se, 2, m - 4))[
                    0 if m < 2 else 1 if m < 4 else 2]
                for c in range(kk):
                    ins = pe.matmul(ps[2][:, m * B:(m + 1) * B], w[:, c, col * P:(col + 1) * P], x[:, c, :],
                                    start=(c == 0), stop=(c == kk - 1))
            pe.matmul(ps[3][0:A, 0:B], ebt[:, :], one_v[:, :], start=True, stop=False)
            pe.matmul(ps[3][0:A, 0:B], demb[:, :], one_c[0:E, :], start=False, stop=True).then_inc(cond_mm, 1)


_DIRECT = ['x', 'condB_dt', 'itok_B_0_15', 'condB_t', 'itok_B_34_63', 'fside_Bx16xSxS_0', 'mask_Bx1xSxS_bk0',
           'L0_cond_A_grid', 'L0_cond_B_grid', 'L1_cond_down_b', 'L1_cond_up_b', 'L1_cond_expert_b',
           'L1_cond_domain_emb', 'L1_cond_ln_gamma', 'L1_cond_ln_beta', 'L2_cond_W1', 'L2_cond_b1',
           'L2_cond_W2', 'L2_cond_b2', 'L2_cond_Wsc', 'L2_cond_bsc', 'L2_cond_Wsh', 'L2_cond_bsh',
           'L2_cond_W_in', 'L2_cond_b_in', 'L2_cond_W_out', 'L2_cond_b_out', 'L3_cond_W_ada', 'L3_cond_b_ada',
           'L3_cond_Wq', 'L3_cond_bq', 'L3_cond_Wk', 'L3_cond_bk', 'L3_cond_Wv', 'L3_cond_bv', 'L3_cond_Wo',
           'L3_cond_bo', 'L3_cond_W1', 'L3_cond_b1', 'L3_cond_W2', 'L3_cond_b2', 'L3_cond_g2', 'L3_cond_beta2']


_COLUMNS = ['L2_cond_b1', 'L2_cond_b2', 'L2_cond_bsc', 'L2_cond_bsh', 'L3_cond_b_ada', 'L2_cond_b_in', 'L3_cond_bq',
            'L3_cond_bk', 'L3_cond_g2', 'L3_cond_beta2', 'L3_cond_b1']


def _shape_constants():
    grad, lap = np.zeros((S, S), np.float32), np.zeros((S, S), np.float32)
    for r in range(1, S - 1):
        grad[r, r - 1], grad[r, r + 1] = -0.5, 0.5
        lap[r, r - 1:r + 2] = 0.5, -1.0, 0.5
    grad[0, 0:3], grad[S - 1, S - 3:] = (-1.5, 2.0, -0.5), (0.5, -2.0, 1.5)
    lap[0, 0:4], lap[S - 1, S - 4:] = (1.0, -2.5, 2.0, -0.5), (-0.5, 2.0, -2.5, 1.0)
    cols = np.zeros((P, 4), np.float32)

    def freqs(half):
        step = np.float32(-np.log(10000.0) / (half - 1))
        return np.exp(np.arange(half, dtype=np.float32) * step).astype(np.float32)

    cols[:, 0] = np.tile(freqs(P // 2), 2)
    cols[:, 1] = freqs(P)
    cols[P // 2:, 2] = 0.25
    cols[P // 2:, 3] = np.pi / 2
    edge = np.array([[-3, 4, -1, 0, 0, 1, -4, 3], [-1, 0, 0, 0, 0, 0, 0, -1],
                     [1.5, -2, 0.5, 0, 0, -0.5, 2, -1.5], [1, -2.5, 2, -0.5, -0.5, 2, -2.5, 1]], np.float32)
    return {"gradT": np.ascontiguousarray(grad.T), "lapT": np.ascontiguousarray(lap.T), "enc_cols": cols,
            "row_number": np.arange(EROW + 1, dtype=np.float32).reshape(-1, 1), "edge_coef": edge.reshape(-1),
            "eye64": np.eye(A, dtype=np.float32).reshape(1, -1)}


def kernel(**inputs):
    import numpy as _np
    import concourse.bacc as _bacc
    from concourse import mybir as _mybir
    from concourse.bass_utils import run_bass_kernel_spmd as _run

    nc = _bacc.Bacc("TRN2", target_bir_lowering=False, num_devices=1)
    data = {n: _np.ascontiguousarray(inputs[n]) for n in _DIRECT}
    data["downT"] = _np.ascontiguousarray(_np.asarray(inputs["L1_cond_down_W"]).T)
    data["upT"] = _np.ascontiguousarray(_np.asarray(inputs["L1_cond_up_W"]).T)
    data["expertT"] = _np.ascontiguousarray(
        _np.asarray(inputs["L1_cond_expert_W"]).transpose(0, 2, 1)).reshape(E, A * A)
    data["gammaT"] = _np.ascontiguousarray(_np.asarray(inputs["L2_cond_gamma"]).T)
    data["betaT"] = _np.ascontiguousarray(_np.asarray(inputs["L2_cond_beta"]).T)
    for n in ("L3_cond_Wq", "L3_cond_Wk", "L3_cond_bq", "L3_cond_bk"):
        data[n] = _np.ascontiguousarray(data[n].reshape(-1, H, DH).swapaxes(1, 2)).reshape(data[n].shape)
    for n in _COLUMNS:
        data[n] = _np.ascontiguousarray(data[n].reshape(-1, P).T)
    data.update(_shape_constants())
    arrays, aps = {}, {}
    for name, a in data.items():
        arrays[f"in_{name}_dram"] = a
        aps[name] = nc.dram_tensor(f"in_{name}_dram", a.shape, _mybir.dt.from_np(a.dtype), kind="ExternalInput").ap()
    out = nc.dram_tensor("out_0_dram", (B, S, D), _mybir.dt.float32, kind="ExternalOutput").ap()
    adapter_to_attention_kernel(nc, aps, out)
    r = _run(nc, [arrays], core_ids=[0])
    return r.results[0]["out_0_dram"]
```
